# Optimizing a Trainium2 kernel written in Bass

```python
import numpy as np
import jax
import jax.numpy as jnp

def _softmax(x, axis=-1):
    return jax.nn.softmax(x, axis=axis)

def _gelu(x):
    return jax.nn.gelu(x, approximate=True)

def _silu(x):
    return jax.nn.silu(x)

def _sigmoid(x):
    return jax.nn.sigmoid(x)

def _layernorm(x, axis=-1, eps=1e-05):
    m = jnp.mean(x, axis=axis, keepdims=True)
    v = jnp.var(x, axis=axis, keepdims=True)
    return (x - m) / jnp.sqrt(v + eps)

def _scatter_add(tgt, idx, src, axis=0):
    return tgt.at[idx].add(src)

def _segment_sum(src, seg, n):
    return jax.ops.segment_sum(src, seg, n)
kernel_name = 'mk_gnn_preln_d4_gnn_r8_0fe71b'

def setup_inputs(seed: int=0):
    np.random.seed(seed)
    _w = jnp.asarray

    def _rec_inputs():
        import jax
        import jax.numpy as jnp
        _gk = jax.random.key(seed)
        x = -1.686e-05 + 1 * jax.random.normal(jax.random.fold_in(_gk, 1), (12500, 160), jnp.float32)
        src = jax.random.randint(jax.random.fold_in(_gk, 2), (200000,), 0, 12500, jnp.int32)
        dst = jnp.minimum((12500 * jax.random.uniform(jax.random.fold_in(_gk, 3), (200000,)) ** 2.0).astype(jnp.int32), 99999)
        _o = jnp.argsort(dst, stable=True)
        src = src[_o]
        dst = dst[_o]
        edge_attr_10 = jax.random.uniform(jax.random.fold_in(_gk, 12), (200000, 10), jnp.float32, 0.0, 1)
        edge_attr_16 = jax.random.uniform(jax.random.fold_in(_gk, 13), (200000, 16), jnp.float32, 0.0, 1)
        edge_attr_3 = 0.00262751 + 0.999568 * jax.random.normal(jax.random.fold_in(_gk, 14), (200000, 3), jnp.float32)
        edge_attr_4 = -0.000107899 + 1.00008 * jax.random.normal(jax.random.fold_in(_gk, 15), (200000, 4), jnp.float32)
        edge_attr_64 = jax.random.uniform(jax.random.fold_in(_gk, 16), (200000, 64), jnp.float32, 0.0, 1)
        node_vec1 = jax.random.uniform(jax.random.fold_in(_gk, 18), (12500, 1), jnp.float32, 0.0, 1)
        return (x, src, dst, edge_attr_10, edge_attr_16, edge_attr_3, edge_attr_4, edge_attr_64, node_vec1)
    x, src, dst, edge_attr_10, edge_attr_16, edge_attr_3, edge_attr_4, edge_attr_64, node_vec1 = _rec_inputs()

    def _L0_gnn_setup():
        import jax, jax.numpy as jnp
        import numpy as np
        N_NODES = 6250
        N_EDGES = 100000
        MUL0, MUL1 = (64, 32)
        N_BASIS, N_RADIAL = (10, 100)
        W_NUMEL = 192
        NUM_NEIGHBORS = 16.0
        INV_SQRT3 = np.float32(1.0 / np.sqrt(3.0))
        RELU_GAIN = np.float32(np.sqrt(2.0))
        FAN_L2 = np.float32(np.sqrt(MUL0 + MUL1))

        def _fctp_scalar_attr(x0, x1, a, W0, W1):
            o0 = x0 @ W0 * a * (1.0 / np.sqrt(W0.shape[0]))
            o1 = jnp.einsum('nud,uw->nwd', x1, W1) * a[..., None] * (1.0 / np.sqrt(W1.shape[0]))
            return (o0, o1)
        key = jax.random.key(seed)
        ks = jax.random.split(key, 16)
        return {'node_input': jax.random.normal(ks[0], (N_NODES, MUL0 + 3 * MUL1), jnp.float32), 'node_attr': jnp.ones((N_NODES, 1), jnp.float32), 'edge_attr': jax.random.normal(ks[1], (N_EDGES, 4), jnp.float32), 'edge_length_embedded': jax.random.uniform(ks[2], (N_EDGES, N_BASIS), dtype=jnp.float32), 'W_si0': jax.random.normal(ks[3], (MUL0, MUL0), jnp.float32), 'W_si1': jax.random.normal(ks[4], (MUL1, MUL1), jnp.float32), 'W_l1_0': jax.random.normal(ks[5], (MUL0, MUL0), jnp.float32), 'W_l1_1': jax.random.normal(ks[6], (MUL1, MUL1), jnp.float32), 'W_l2_00': jax.random.normal(ks[7], (MUL0, MUL0), jnp.float32), 'W_l2_10': jax.random.normal(ks[8], (MUL1, MUL0), jnp.float32), 'W_l2_01': jax.random.normal(ks[9], (MUL0, MUL1), jnp.float32), 'W_l2_11': jax.random.normal(ks[10], (MUL1, MUL1), jnp.float32), 'W_fc1': jax.random.normal(ks[11], (N_BASIS, N_RADIAL), jnp.float32), 'W_fc2': jax.random.normal(ks[12], (N_RADIAL, W_NUMEL), jnp.float32), 'edge_src': jax.random.randint(ks[13], (N_EDGES,), 0, N_NODES), 'edge_dst': jax.random.randint(ks[14], (N_EDGES,), 0, N_NODES)}
    _L0_gnn_all = _L0_gnn_setup()
    _L0_gnn_in = {k: v for k, v in _L0_gnn_all.items() if k in ('W_si0', 'W_si1', 'W_l1_0', 'W_l1_1', 'W_l2_00', 'W_l2_10', 'W_l2_01', 'W_l2_11', 'W_fc1', 'W_fc2')}
    del _L0_gnn_all

    def _L1_gnn_setup():
        import jax, jax.numpy as jnp
        import numpy as np
        N, E = (2500, 40000)
        CS, CV = (64, 32)
        AS_, AV, H = (16, 8, 4)
        NB = 16
        SQRT3 = 1.7320508075688772
        SQRT2 = 1.4142135623730951
        EPS = 1e-05

        def _cg_tp(s, v, y0, y1, w_ss, w_sv, w_vs, w_vv0, w_vv1):
            out_s = jnp.concatenate([w_ss * s * y0[:, None], w_vv0 * (jnp.einsum('eci,ei->ec', v, y1) / SQRT3)], axis=-1)
            out_v = jnp.concatenate([(w_sv * s)[:, :, None] * y1[:, None, :], (w_vs * jnp.ones_like(v[..., 0]))[..., None] * v * y0[:, None, None], (w_vv1 * jnp.ones_like(v[..., 0]))[..., None] * (jnp.cross(v, y1[:, None, :]) / SQRT2)], axis=1)
            return (out_s, out_v)

        def _equiv_layernorm(s, v, gamma_s, beta_s, gamma_v):
            mu = jnp.mean(s, axis=-1, keepdims=True)
            var = jnp.var(s, axis=-1, keepdims=True)
            s_n = (s - mu) * jax.lax.rsqrt(var + EPS) * gamma_s + beta_s
            rms = jnp.sqrt(jnp.mean(jnp.sum(v * v, axis=-1), axis=-1, keepdims=True) + EPS)
            v_n = v / rms[..., None] * gamma_v[None, :, None]
            return (s_n, v_n)
        key = jax.random.key(seed)
        ks = jax.random.split(key, 26)

        def rn(k, shape, fan):
            return jax.random.normal(k, shape, jnp.float32) / np.sqrt(fan)
        D1S, D1V = (CS + CV, CS + 2 * CV)
        WN = 2 * CS + 3 * CV
        inp = {'node': jax.random.normal(ks[0], (N, CS + 3 * CV), jnp.float32), 'edge_index': jax.random.randint(ks[1], (2, E), 0, N, jnp.int64 if jax.config.jax_enable_x64 else jnp.int32), 'rbf': jax.random.uniform(ks[2], (E, NB), jnp.float32), 'rsh': jax.random.normal(ks[3], (E, 4), jnp.float32), 'gamma_s': jnp.ones((CS,), jnp.float32), 'beta_s': jnp.zeros((CS,), jnp.float32), 'gamma_v': jnp.ones((CV,), jnp.float32), 'Ws_src': rn(ks[4], (CS, CS), CS), 'Wv_src': rn(ks[5], (CV, CV), CV), 'Ws_dst': rn(ks[6], (CS, CS), CS), 'Wv_dst': rn(ks[7], (CV, CV), CV), 'W_rbf': rn(ks[8], (NB, WN), NB), 'W_alpha': rn(ks[9], (D1S, H * AS_), D1S), 'alpha_dot': rn(ks[10], (1, H, AS_), AS_), 'Ws_val': rn(ks[11], (D1S, CS), D1S), 'Wv_val': rn(ks[12], (D1V, CV), D1V), 'Wg': rn(ks[13], (CS, CV), CS), 'w2_ss': rn(ks[14], (CS,), 1), 'w2_sv': rn(ks[15], (CS,), 1), 'w2_vs': rn(ks[16], (CV,), 1), 'w2_vv0': rn(ks[17], (CV,), 1), 'w2_vv1': rn(ks[18], (CV,), 1), 'Ws_vlin': rn(ks[19], (D1S, H * AS_), D1S), 'Wv_vlin': rn(ks[20], (D1V, H * AV), D1V), 'Wps': rn(ks[21], (H * AS_, CS), H * AS_), 'Wpv': rn(ks[22], (H * AV, CV), H * AV)}
        return inp
    _L1_gnn_all = _L1_gnn_setup()
    _L1_gnn_in = {k: v for k, v in _L1_gnn_all.items() if k in ('gamma_s', 'beta_s', 'gamma_v', 'Ws_src', 'Wv_src', 'Ws_dst', 'Wv_dst', 'W_rbf', 'W_alpha', 'alpha_dot', 'Ws_val', 'Wv_val', 'Wg', 'w2_ss', 'w2_sv', 'w2_vs', 'w2_vv0', 'w2_vv1', 'Ws_vlin', 'Wv_vlin', 'Wps', 'Wpv')}
    del _L1_gnn_all

    def _L2_gnn_setup():
        import jax, jax.numpy as jnp
        import numpy as np
        N_NODES = 12500
        N_EDGES = 100000
        MUL_S = 64
        MUL_V = 32
        DIM = MUL_S + 3 * MUL_V
        EDGE_SCALAR_DIM = 16
        ISQ3 = 1.0 / np.sqrt(3.0)
        ISQ2 = 1.0 / np.sqrt(2.0)

        def _forward(x, edge_index, edge_feat, edge_scalars, W_ss, W_sv, W_vs, W_vv, W_rad, b_rad, L_s, L_v):
            src, dst = (edge_index[0], edge_index[1])
            n = x.shape[0]
            xs = x[:, :MUL_S]
            xv = x[:, MUL_S:].reshape(n, MUL_V, 3)
            xs_e = xs[src]
            xv_e = xv[src]
            es = edge_feat[:, 0]
            ev = edge_feat[:, 1:4]
            out_s = (jnp.einsum('eu,uo->eo', xs_e * es[:, None], W_ss) / np.sqrt(MUL_S) + jnp.einsum('eud,ed,uo->eo', xv_e, ev, W_vv) * ISQ3 / np.sqrt(MUL_V)) * ISQ2
            out_v = (jnp.einsum('eu,ed,uv->evd', xs_e, ev, W_sv) * ISQ3 / np.sqrt(MUL_S) + jnp.einsum('eud,e,uv->evd', xv_e, es, W_vs) * ISQ3 / np.sqrt(MUL_V)) * ISQ2
            messages = jnp.concatenate([out_s, out_v.reshape(-1, 3 * MUL_V)], axis=1)
            scale = jax.nn.sigmoid(edge_scalars @ W_rad.T + b_rad)
            messages = messages * scale
            agg = jax.ops.segment_sum(messages, dst, num_segments=n)
            h = x + agg
            hs = h[:, :MUL_S]
            hv = h[:, MUL_S:].reshape(n, MUL_V, 3)
            ys = hs @ L_s / np.sqrt(MUL_S)
            yv = jnp.einsum('nud,uv->nvd', hv, L_v) / np.sqrt(MUL_V)
            return jnp.concatenate([ys, yv.reshape(n, 3 * MUL_V)], axis=1)
        key = jax.random.key(seed)
        ks = jax.random.split(key, 12)
        x = jax.random.normal(ks[0], (N_NODES, DIM), dtype=jnp.float32)
        edge_index = jax.random.randint(ks[1], (2, N_EDGES), 0, N_NODES, dtype=jnp.int64)
        edge_feat = jax.random.normal(ks[2], (N_EDGES, 4), dtype=jnp.float32)
        edge_scalars = jax.random.normal(ks[3], (N_EDGES, EDGE_SCALAR_DIM), dtype=jnp.float32)
        W_ss = jax.random.normal(ks[4], (MUL_S, MUL_S), dtype=jnp.float32)
        W_sv = jax.random.normal(ks[5], (MUL_S, MUL_V), dtype=jnp.float32)
        W_vs = jax.random.normal(ks[6], (MUL_V, MUL_V), dtype=jnp.float32)
        W_vv = jax.random.normal(ks[7], (MUL_V, MUL_S), dtype=jnp.float32)
        W_rad = jax.random.normal(ks[8], (DIM, EDGE_SCALAR_DIM), dtype=jnp.float32) / np.sqrt(EDGE_SCALAR_DIM)
        b_rad = jax.random.normal(ks[9], (DIM,), dtype=jnp.float32) * 0.1
        L_s = jax.random.normal(ks[10], (MUL_S, MUL_S), dtype=jnp.float32)
        L_v = jax.random.normal(ks[11], (MUL_V, MUL_V), dtype=jnp.float32)
        return {'x': x, 'edge_index': edge_index, 'edge_feat': edge_feat, 'edge_scalars': edge_scalars, 'W_ss': W_ss, 'W_sv': W_sv, 'W_vs': W_vs, 'W_vv': W_vv, 'W_rad': W_rad, 'b_rad': b_rad, 'L_s': L_s, 'L_v': L_v}
    _L2_gnn_all = _L2_gnn_setup()
    _L2_gnn_in = {k: v for k, v in _L2_gnn_all.items() if k in ('W_ss', 'W_sv', 'W_vs', 'W_vv', 'W_rad', 'b_rad', 'L_s', 'L_v')}
    del _L2_gnn_all

    def _L3_gnn_setup():
        import jax, jax.numpy as jnp
        import numpy as np
        N, E = (1250, 20000)
        C0, C1 = (64, 32)
        H, A = (8, 8)
        H0, H1 = (8, 4)
        M0, M1 = (128, 64)
        NG, RH = (64, 64)
        WN = C0 + C0 + C1 + C1 + C1
        DS, DV = (C0 + C1, C0 + 2 * C1)
        EPS = 1e-05
        SQ3 = np.float32(np.sqrt(3.0))
        SQ2 = np.float32(np.sqrt(2.0))

        def _split(x):
            return (x[:, :C0], x[:, C0:].reshape(x.shape[0], C1, 3))

        def _merge(s, v):
            return jnp.concatenate([s, v.reshape(v.shape[0], -1)], axis=1)

        def _eq_ln(x, w0, b0, w1):
            s, v = _split(x)
            s = s - s.mean(axis=1, keepdims=True)
            s = s * jax.lax.rsqrt(jnp.square(s).mean(axis=1, keepdims=True) + EPS) * w0 + b0
            v = v * jax.lax.rsqrt(jnp.square(v).mean(axis=(1, 2), keepdims=True) + EPS) * w1[None, :, None]
            return (s, v)

        def _eq_lin(s, v, ws, bs, wv):
            return (s @ ws + bs, jnp.einsum('nud,uk->nkd', v, wv))

        def _ln(x, g, b):
            xc = x - x.mean(-1, keepdims=True)
            return xc * jax.lax.rsqrt(jnp.square(xc).mean(-1, keepdims=True) + EPS) * g + b

        def _smooth_leaky(x, alpha=0.2):
            return 0.5 * (1 + alpha) * x + 0.5 * (1 - alpha) * x * (2.0 * jax.nn.sigmoid(x) - 1.0)

        def _forward(node_input, node_attr, edge_vec, edge_scalars, edge_src, edge_dst, ln1_w0, ln1_b0, ln1_w1, ln2_w0, ln2_b0, ln2_w1, msrc_ws, msrc_wv, mdst_ws, mdst_bs, mdst_wv, rw1, rb1, rg1, rbe1, rw2, rb2, rg2, rbe2, rw3, roff, lin_ws, lin_bs, lin_wv, alpha_dot, proj_ws, proj_bs, proj_wv, f1_ws, f1_bs, f1_wv, f2_ws, f2_bs, f2_wv):
            n = node_input.shape[0]
            s, v = _eq_ln(node_input, ln1_w0, ln1_b0, ln1_w1)
            src_s = s @ msrc_ws
            src_v = jnp.einsum('nud,uk->nkd', v, msrc_wv)
            dst_s = s @ mdst_ws + mdst_bs
            dst_v = jnp.einsum('nud,uk->nkd', v, mdst_wv)
            ms = src_s[edge_src] + dst_s[edge_dst]
            mv = src_v[edge_src] + dst_v[edge_dst]
            h = jax.nn.silu(_ln(edge_scalars @ rw1 + rb1, rg1, rbe1))
            h = jax.nn.silu(_ln(h @ rw2 + rb2, rg2, rbe2))
            w = h @ rw3 + roff
            rhat = edge_vec * jax.lax.rsqrt(jnp.sum(jnp.square(edge_vec), -1, keepdims=True) + 1e-12)
            Y1 = SQ3 * rhat
            w1, w2, w3, w4, w5 = jnp.split(w, [C0, 2 * C0, 2 * C0 + C1, 2 * C0 + 2 * C1], axis=1)
            o0a = w1 * ms
            o0b = w4 * (jnp.einsum('eud,ed->eu', mv, Y1) / SQ3)
            o1a = (w2 * ms)[:, :, None] * Y1[:, None, :]
            o1b = w3[:, :, None] * mv
            o1c = w5[:, :, None] * (jnp.cross(mv, Y1[:, None, :]) / SQ2)
            ds = jnp.concatenate([o0a, o0b], axis=1)
            dv = jnp.concatenate([o1a, o1b, o1c], axis=1)
            ls, lv = _eq_lin(ds, dv, lin_ws, lin_bs, lin_wv)
            e = ls.shape[0]
            alpha = ls[:, :H * A].reshape(e, H, A)
            vs = ls[:, H * A:].reshape(e, H, H0)
            vv = lv.reshape(e, H, H1, 3)
            a = jnp.einsum('ehk,hk->eh', _smooth_leaky(alpha), alpha_dot)
            amax = jax.lax.stop_gradient(jax.ops.segment_max(a, edge_dst, num_segments=n))
            a = jnp.exp(a - amax[edge_dst])
            a = a / (jax.ops.segment_sum(a, edge_dst, num_segments=n)[edge_dst] + 1e-12)
            ns = jax.ops.segment_sum(vs * a[..., None], edge_dst, num_segments=n).reshape(n, H * H0)
            nv = jax.ops.segment_sum(vv * a[..., None, None], edge_dst, num_segments=n).reshape(n, H * H1, 3)
            ps, pv = _eq_lin(ns, nv, proj_ws, proj_bs, proj_wv)
            x = node_input + _merge(ps, pv)
            s2, v2 = _eq_ln(x, ln2_w0, ln2_b0, ln2_w1)
            a0 = node_attr[:, :1]
            fs, fv = _eq_lin(s2, v2, f1_ws, f1_bs, f1_wv)
            fs = fs * a0
            fv = fv * a0[:, :, None]
            sc = jax.nn.silu(fs[:, :M0])
            fv = fv * jax.nn.sigmoid(fs[:, M0:])[:, :, None]
            os_, ov = _eq_lin(sc, fv, f2_ws, f2_bs, f2_wv)
            os_ = os_ * a0
            ov = ov * a0[:, :, None]
            return x + _merge(os_, ov)
        key = jax.random.key(seed)
        ks = iter(jax.random.split(key, 24))

        def nrm(shape, fan):
            return jax.random.normal(next(ks), shape, jnp.float32) / np.float32(np.sqrt(fan))
        inp = {}
        inp['node_input'] = jax.random.normal(next(ks), (N, C0 + 3 * C1), jnp.float32)
        inp['node_attr'] = jnp.ones((N, 1), jnp.float32)
        inp['edge_vec'] = jax.random.normal(next(ks), (E, 3), jnp.float32)
        inp['edge_scalars'] = jax.random.uniform(next(ks), (E, NG), dtype=jnp.float32)
        inp['edge_src'] = jax.random.randint(next(ks), (E,), 0, N)
        inp['edge_dst'] = jax.random.randint(next(ks), (E,), 0, N)
        inp['ln1_w0'] = jnp.ones((C0,), jnp.float32)
        inp['ln1_b0'] = jnp.zeros((C0,), jnp.float32)
        inp['ln1_w1'] = jnp.ones((C1,), jnp.float32)
        inp['ln2_w0'] = jnp.ones((C0,), jnp.float32)
        inp['ln2_b0'] = jnp.zeros((C0,), jnp.float32)
        inp['ln2_w1'] = jnp.ones((C1,), jnp.float32)
        inp['msrc_ws'] = nrm((C0, C0), C0)
        inp['msrc_wv'] = nrm((C1, C1), C1)
        inp['mdst_ws'] = nrm((C0, C0), C0)
        inp['mdst_bs'] = jnp.zeros((C0,), jnp.float32)
        inp['mdst_wv'] = nrm((C1, C1), C1)
        inp['rw1'] = nrm((NG, RH), NG)
        inp['rb1'] = jnp.zeros((RH,), jnp.float32)
        inp['rg1'] = jnp.ones((RH,), jnp.float32)
        inp['rbe1'] = jnp.zeros((RH,), jnp.float32)
        inp['rw2'] = nrm((RH, RH), RH)
        inp['rb2'] = jnp.zeros((RH,), jnp.float32)
        inp['rg2'] = jnp.ones((RH,), jnp.float32)
        inp['rbe2'] = jnp.zeros((RH,), jnp.float32)
        inp['rw3'] = nrm((RH, WN), RH)
        inp['roff'] = 0.1 * jax.random.normal(next(ks), (WN,), jnp.float32)
        inp['lin_ws'] = nrm((DS, H * A + H * H0), DS)
        inp['lin_bs'] = jnp.zeros((H * A + H * H0,), jnp.float32)
        inp['lin_wv'] = nrm((DV, H * H1), DV)
        inp['alpha_dot'] = nrm((H, A), A)
        inp['proj_ws'] = nrm((H * H0, C0), H * H0)
        inp['proj_bs'] = jnp.zeros((C0,), jnp.float32)
        inp['proj_wv'] = nrm((H * H1, C1), H * H1)
        inp['f1_ws'] = nrm((C0, M0 + M1), C0)
        inp['f1_bs'] = jnp.zeros((M0 + M1,), jnp.float32)
        inp['f1_wv'] = nrm((C1, M1), C1)
        inp['f2_ws'] = nrm((M0, C0), M0)
        inp['f2_bs'] = jnp.zeros((C0,), jnp.float32)
        inp['f2_wv'] = nrm((M1, C1), M1)
        return inp
    _L3_gnn_all = _L3_gnn_setup()
    _L3_gnn_in = {k: v for k, v in _L3_gnn_all.items() if k in ('ln1_w0', 'ln1_b0', 'ln1_w1', 'ln2_w0', 'ln2_b0', 'ln2_w1', 'msrc_ws', 'msrc_wv', 'mdst_ws', 'mdst_bs', 'mdst_wv', 'rw1', 'rb1', 'rg1', 'rbe1', 'rw2', 'rb2', 'rg2', 'rbe2', 'rw3', 'roff', 'lin_ws', 'lin_bs', 'lin_wv', 'alpha_dot', 'proj_ws', 'proj_bs', 'proj_wv', 'f1_ws', 'f1_bs', 'f1_wv', 'f2_ws', 'f2_bs', 'f2_wv')}
    del _L3_gnn_all
    return {'x': x, 'src': src, 'dst': dst, 'edge_attr_10': edge_attr_10, 'edge_attr_16': edge_attr_16, 'edge_attr_3': edge_attr_3, 'edge_attr_4': edge_attr_4, 'edge_attr_64': edge_attr_64, 'node_vec1': node_vec1, 'L0_gnn_W_si0': _L0_gnn_in['W_si0'], 'L0_gnn_W_si1': _L0_gnn_in['W_si1'], 'L0_gnn_W_l1_0': _L0_gnn_in['W_l1_0'], 'L0_gnn_W_l1_1': _L0_gnn_in['W_l1_1'], 'L0_gnn_W_l2_00': _L0_gnn_in['W_l2_00'], 'L0_gnn_W_l2_10': _L0_gnn_in['W_l2_10'], 'L0_gnn_W_l2_01': _L0_gnn_in['W_l2_01'], 'L0_gnn_W_l2_11': _L0_gnn_in['W_l2_11'], 'L0_gnn_W_fc1': _L0_gnn_in['W_fc1'], 'L0_gnn_W_fc2': _L0_gnn_in['W_fc2'], 'L1_gnn_gamma_s': _L1_gnn_in['gamma_s'], 'L1_gnn_beta_s': _L1_gnn_in['beta_s'], 'L1_gnn_gamma_v': _L1_gnn_in['gamma_v'], 'L1_gnn_Ws_src': _L1_gnn_in['Ws_src'], 'L1_gnn_Wv_src': _L1_gnn_in['Wv_src'], 'L1_gnn_Ws_dst': _L1_gnn_in['Ws_dst'], 'L1_gnn_Wv_dst': _L1_gnn_in['Wv_dst'], 'L1_gnn_W_rbf': _L1_gnn_in['W_rbf'], 'L1_gnn_W_alpha': _L1_gnn_in['W_alpha'], 'L1_gnn_alpha_dot': _L1_gnn_in['alpha_dot'], 'L1_gnn_Ws_val': _L1_gnn_in['Ws_val'], 'L1_gnn_Wv_val': _L1_gnn_in['Wv_val'], 'L1_gnn_Wg': _L1_gnn_in['Wg'], 'L1_gnn_w2_ss': _L1_gnn_in['w2_ss'], 'L1_gnn_w2_sv': _L1_gnn_in['w2_sv'], 'L1_gnn_w2_vs': _L1_gnn_in['w2_vs'], 'L1_gnn_w2_vv0': _L1_gnn_in['w2_vv0'], 'L1_gnn_w2_vv1': _L1_gnn_in['w2_vv1'], 'L1_gnn_Ws_vlin': _L1_gnn_in['Ws_vlin'], 'L1_gnn_Wv_vlin': _L1_gnn_in['Wv_vlin'], 'L1_gnn_Wps': _L1_gnn_in['Wps'], 'L1_gnn_Wpv': _L1_gnn_in['Wpv'], 'L2_gnn_W_ss': _L2_gnn_in['W_ss'], 'L2_gnn_W_sv': _L2_gnn_in['W_sv'], 'L2_gnn_W_vs': _L2_gnn_in['W_vs'], 'L2_gnn_W_vv': _L2_gnn_in['W_vv'], 'L2_gnn_W_rad': _L2_gnn_in['W_rad'], 'L2_gnn_b_rad': _L2_gnn_in['b_rad'], 'L2_gnn_L_s': _L2_gnn_in['L_s'], 'L2_gnn_L_v': _L2_gnn_in['L_v'], 'L3_gnn_ln1_w0': _L3_gnn_in['ln1_w0'], 'L3_gnn_ln1_b0': _L3_gnn_in['ln1_b0'], 'L3_gnn_ln1_w1': _L3_gnn_in['ln1_w1'], 'L3_gnn_ln2_w0': _L3_gnn_in['ln2_w0'], 'L3_gnn_ln2_b0': _L3_gnn_in['ln2_b0'], 'L3_gnn_ln2_w1': _L3_gnn_in['ln2_w1'], 'L3_gnn_msrc_ws': _L3_gnn_in['msrc_ws'], 'L3_gnn_msrc_wv': _L3_gnn_in['msrc_wv'], 'L3_gnn_mdst_ws': _L3_gnn_in['mdst_ws'], 'L3_gnn_mdst_bs': _L3_gnn_in['mdst_bs'], 'L3_gnn_mdst_wv': _L3_gnn_in['mdst_wv'], 'L3_gnn_rw1': _L3_gnn_in['rw1'], 'L3_gnn_rb1': _L3_gnn_in['rb1'], 'L3_gnn_rg1': _L3_gnn_in['rg1'], 'L3_gnn_rbe1': _L3_gnn_in['rbe1'], 'L3_gnn_rw2': _L3_gnn_in['rw2'], 'L3_gnn_rb2': _L3_gnn_in['rb2'], 'L3_gnn_rg2': _L3_gnn_in['rg2'], 'L3_gnn_rbe2': _L3_gnn_in['rbe2'], 'L3_gnn_rw3': _L3_gnn_in['rw3'], 'L3_gnn_roff': _L3_gnn_in['roff'], 'L3_gnn_lin_ws': _L3_gnn_in['lin_ws'], 'L3_gnn_lin_bs': _L3_gnn_in['lin_bs'], 'L3_gnn_lin_wv': _L3_gnn_in['lin_wv'], 'L3_gnn_alpha_dot': _L3_gnn_in['alpha_dot'], 'L3_gnn_proj_ws': _L3_gnn_in['proj_ws'], 'L3_gnn_proj_bs': _L3_gnn_in['proj_bs'], 'L3_gnn_proj_wv': _L3_gnn_in['proj_wv'], 'L3_gnn_f1_ws': _L3_gnn_in['f1_ws'], 'L3_gnn_f1_bs': _L3_gnn_in['f1_bs'], 'L3_gnn_f1_wv': _L3_gnn_in['f1_wv'], 'L3_gnn_f2_ws': _L3_gnn_in['f2_ws'], 'L3_gnn_f2_bs': _L3_gnn_in['f2_bs'], 'L3_gnn_f2_wv': _L3_gnn_in['f2_wv']}

def reference(x, src, dst, edge_attr_10, edge_attr_16, edge_attr_3, edge_attr_4, edge_attr_64, node_vec1, L0_gnn_W_si0, L0_gnn_W_si1, L0_gnn_W_l1_0, L0_gnn_W_l1_1, L0_gnn_W_l2_00, L0_gnn_W_l2_10, L0_gnn_W_l2_01, L0_gnn_W_l2_11, L0_gnn_W_fc1, L0_gnn_W_fc2, L1_gnn_gamma_s, L1_gnn_beta_s, L1_gnn_gamma_v, L1_gnn_Ws_src, L1_gnn_Wv_src, L1_gnn_Ws_dst, L1_gnn_Wv_dst, L1_gnn_W_rbf, L1_gnn_W_alpha, L1_gnn_alpha_dot, L1_gnn_Ws_val, L1_gnn_Wv_val, L1_gnn_Wg, L1_gnn_w2_ss, L1_gnn_w2_sv, L1_gnn_w2_vs, L1_gnn_w2_vv0, L1_gnn_w2_vv1, L1_gnn_Ws_vlin, L1_gnn_Wv_vlin, L1_gnn_Wps, L1_gnn_Wpv, L2_gnn_W_ss, L2_gnn_W_sv, L2_gnn_W_vs, L2_gnn_W_vv, L2_gnn_W_rad, L2_gnn_b_rad, L2_gnn_L_s, L2_gnn_L_v, L3_gnn_ln1_w0, L3_gnn_ln1_b0, L3_gnn_ln1_w1, L3_gnn_ln2_w0, L3_gnn_ln2_b0, L3_gnn_ln2_w1, L3_gnn_msrc_ws, L3_gnn_msrc_wv, L3_gnn_mdst_ws, L3_gnn_mdst_bs, L3_gnn_mdst_wv, L3_gnn_rw1, L3_gnn_rb1, L3_gnn_rg1, L3_gnn_rbe1, L3_gnn_rw2, L3_gnn_rb2, L3_gnn_rg2, L3_gnn_rbe2, L3_gnn_rw3, L3_gnn_roff, L3_gnn_lin_ws, L3_gnn_lin_bs, L3_gnn_lin_wv, L3_gnn_alpha_dot, L3_gnn_proj_ws, L3_gnn_proj_bs, L3_gnn_proj_wv, L3_gnn_f1_ws, L3_gnn_f1_bs, L3_gnn_f1_wv, L3_gnn_f2_ws, L3_gnn_f2_bs, L3_gnn_f2_wv):
    import jax
    import jax.numpy as jnp

    def _L0_gnn_ref(node_input, node_attr, edge_src, edge_dst, edge_attr, edge_length_embedded, W_si0, W_si1, W_l1_0, W_l1_1, W_l2_00, W_l2_10, W_l2_01, W_l2_11, W_fc1, W_fc2):
        import jax, jax.numpy as jnp
        import numpy as np
        N_NODES = 6250
        N_EDGES = 100000
        MUL0, MUL1 = (64, 32)
        N_BASIS, N_RADIAL = (10, 100)
        W_NUMEL = 192
        NUM_NEIGHBORS = 16.0
        INV_SQRT3 = np.float32(1.0 / np.sqrt(3.0))
        RELU_GAIN = np.float32(np.sqrt(2.0))
        FAN_L2 = np.float32(np.sqrt(MUL0 + MUL1))

        def _fctp_scalar_attr(x0, x1, a, W0, W1):
            o0 = x0 @ W0 * a * (1.0 / np.sqrt(W0.shape[0]))
            o1 = jnp.einsum('nud,uw->nwd', x1, W1) * a[..., None] * (1.0 / np.sqrt(W1.shape[0]))
            return (o0, o1)
        N = node_input.shape[0]
        x0 = node_input[:, :MUL0]
        x1 = node_input[:, MUL0:].reshape(N, MUL1, 3)
        a = node_attr
        h = jax.nn.relu(edge_length_embedded @ W_fc1 * (1.0 / np.sqrt(N_BASIS))) * RELU_GAIN
        w = h @ W_fc2 * (1.0 / np.sqrt(N_RADIAL))
        w0, w1, w2, w3 = (w[:, :64], w[:, 64:128], w[:, 128:160], w[:, 160:192])
        si0, si1 = _fctp_scalar_attr(x0, x1, a, W_si0, W_si1)
        l0, l1 = _fctp_scalar_attr(x0, x1, a, W_l1_0, W_l1_1)
        y0 = l0[edge_src]
        y1 = l1[edge_src]
        e0 = edge_attr[:, :1]
        e1 = edge_attr[:, 1:4]
        m0 = w0 * y0 * e0
        m1 = (w1 * y0)[:, :, None] * e1[:, None, :]
        m2 = (w2 * e0)[:, :, None] * y1
        m3 = w3 * jnp.einsum('eud,ed->eu', y1, e1) * INV_SQRT3
        inv = np.float32(1.0 / np.sqrt(NUM_NEIGHBORS))
        s0 = jax.ops.segment_sum(m0, edge_dst, num_segments=N) * inv
        s1 = jax.ops.segment_sum(m1, edge_dst, num_segments=N) * inv
        s2 = jax.ops.segment_sum(m2, edge_dst, num_segments=N) * inv
        s3 = jax.ops.segment_sum(m3, edge_dst, num_segments=N) * inv
        o0 = (s0 @ W_l2_00 + s3 @ W_l2_10) * a / FAN_L2
        o1 = (jnp.einsum('nud,uw->nwd', s1, W_l2_01) + jnp.einsum('nud,uw->nwd', s2, W_l2_11)) * a[..., None] / FAN_L2
        out0 = si0 + 0.5 * o0
        out1 = si1 + 0.5 * o1
        return jnp.concatenate([out0, out1.reshape(N, 3 * MUL1)], axis=1)

    def _L1_gnn_ref(node, rbf, rsh, gamma_s, beta_s, gamma_v, Ws_src, Wv_src, Ws_dst, Wv_dst, W_rbf, W_alpha, alpha_dot, Ws_val, Wv_val, Wg, w2_ss, w2_sv, w2_vs, w2_vv0, w2_vv1, Ws_vlin, Wv_vlin, Wps, Wpv, edge_index):
        import jax, jax.numpy as jnp
        import numpy as np
        N, E = (2500, 40000)
        CS, CV = (64, 32)
        AS_, AV, H = (16, 8, 4)
        NB = 16
        SQRT3 = 1.7320508075688772
        SQRT2 = 1.4142135623730951
        EPS = 1e-05

        def _cg_tp(s, v, y0, y1, w_ss, w_sv, w_vs, w_vv0, w_vv1):
            out_s = jnp.concatenate([w_ss * s * y0[:, None], w_vv0 * (jnp.einsum('eci,ei->ec', v, y1) / SQRT3)], axis=-1)
            out_v = jnp.concatenate([(w_sv * s)[:, :, None] * y1[:, None, :], (w_vs * jnp.ones_like(v[..., 0]))[..., None] * v * y0[:, None, None], (w_vv1 * jnp.ones_like(v[..., 0]))[..., None] * (jnp.cross(v, y1[:, None, :]) / SQRT2)], axis=1)
            return (out_s, out_v)

        def _equiv_layernorm(s, v, gamma_s, beta_s, gamma_v):
            mu = jnp.mean(s, axis=-1, keepdims=True)
            var = jnp.var(s, axis=-1, keepdims=True)
            s_n = (s - mu) * jax.lax.rsqrt(var + EPS) * gamma_s + beta_s
            rms = jnp.sqrt(jnp.mean(jnp.sum(v * v, axis=-1), axis=-1, keepdims=True) + EPS)
            v_n = v / rms[..., None] * gamma_v[None, :, None]
            return (s_n, v_n)
        n = node.shape[0]
        e = rsh.shape[0]
        s = node[:, :CS]
        v = node[:, CS:].reshape(n, CV, 3)
        s_n, v_n = _equiv_layernorm(s, v, gamma_s, beta_s, gamma_v)
        src, dst = (edge_index[0], edge_index[1])
        msg_s = (s_n @ Ws_src)[src] + (s_n @ Ws_dst)[dst]
        msg_v = jnp.einsum('ncx,cd->ndx', v_n, Wv_src)[src] + jnp.einsum('ncx,cd->ndx', v_n, Wv_dst)[dst]
        y0, y1 = (rsh[:, 0], rsh[:, 1:4])
        w1 = rbf @ W_rbf
        m1_s, m1_v = _cg_tp(msg_s, msg_v, y0, y1, w1[:, :CS], w1[:, CS:2 * CS], w1[:, 2 * CS:2 * CS + CV], w1[:, 2 * CS + CV:2 * CS + 2 * CV], w1[:, 2 * CS + 2 * CV:])
        a = (m1_s @ W_alpha).reshape(e, H, AS_)
        a = jnp.where(a > 0, a, 0.2 * a)
        a = jnp.sum(a * alpha_dot, axis=-1, keepdims=True)
        amax = jax.ops.segment_max(a, dst, num_segments=n)
        amax = jnp.where(jnp.isfinite(amax), amax, 0.0)
        ex = jnp.exp(a - amax[dst])
        den = jax.ops.segment_sum(ex, dst, num_segments=n)
        alpha = ex / (den[dst] + 1e-16)
        val_s = m1_s @ Ws_val
        val_v = jnp.einsum('ecx,cd->edx', m1_v, Wv_val)
        val_v = val_v * jax.nn.sigmoid(val_s @ Wg)[..., None]
        val_s = jax.nn.sigmoid(val_s)
        m2_s, m2_v = _cg_tp(val_s, val_v, y0, y1, w2_ss, w2_sv, w2_vs, w2_vv0, w2_vv1)
        hs = (m2_s @ Ws_vlin).reshape(e, H, AS_)
        hv = jnp.einsum('ecx,cd->edx', m2_v, Wv_vlin).reshape(e, H, AV, 3)
        h = jnp.concatenate([hs, hv.reshape(e, H, AV * 3)], axis=-1)
        agg = jax.ops.segment_sum(alpha * h, dst, num_segments=n)
        agg_s = agg[:, :, :AS_].reshape(n, H * AS_)
        agg_v = agg[:, :, AS_:].reshape(n, H * AV, 3)
        out = node + jnp.concatenate([agg_s @ Wps, jnp.einsum('ncx,cd->ndx', agg_v, Wpv).reshape(n, CV * 3)], axis=-1)
        return out

    def _L2_gnn_ref(x, edge_index, edge_feat, edge_scalars, W_ss, W_sv, W_vs, W_vv, W_rad, b_rad, L_s, L_v):
        import jax, jax.numpy as jnp
        import numpy as np
        N_NODES = 12500
        N_EDGES = 100000
        MUL_S = 64
        MUL_V = 32
        DIM = MUL_S + 3 * MUL_V
        EDGE_SCALAR_DIM = 16
        ISQ3 = 1.0 / np.sqrt(3.0)
        ISQ2 = 1.0 / np.sqrt(2.0)

        def _forward(x, edge_index, edge_feat, edge_scalars, W_ss, W_sv, W_vs, W_vv, W_rad, b_rad, L_s, L_v):
            src, dst = (edge_index[0], edge_index[1])
            n = x.shape[0]
            xs = x[:, :MUL_S]
            xv = x[:, MUL_S:].reshape(n, MUL_V, 3)
            xs_e = xs[src]
            xv_e = xv[src]
            es = edge_feat[:, 0]
            ev = edge_feat[:, 1:4]
            out_s = (jnp.einsum('eu,uo->eo', xs_e * es[:, None], W_ss) / np.sqrt(MUL_S) + jnp.einsum('eud,ed,uo->eo', xv_e, ev, W_vv) * ISQ3 / np.sqrt(MUL_V)) * ISQ2
            out_v = (jnp.einsum('eu,ed,uv->evd', xs_e, ev, W_sv) * ISQ3 / np.sqrt(MUL_S) + jnp.einsum('eud,e,uv->evd', xv_e, es, W_vs) * ISQ3 / np.sqrt(MUL_V)) * ISQ2
            messages = jnp.concatenate([out_s, out_v.reshape(-1, 3 * MUL_V)], axis=1)
            scale = jax.nn.sigmoid(edge_scalars @ W_rad.T + b_rad)
            messages = messages * scale
            agg = jax.ops.segment_sum(messages, dst, num_segments=n)
            h = x + agg
            hs = h[:, :MUL_S]
            hv = h[:, MUL_S:].reshape(n, MUL_V, 3)
            ys = hs @ L_s / np.sqrt(MUL_S)
            yv = jnp.einsum('nud,uv->nvd', hv, L_v) / np.sqrt(MUL_V)
            return jnp.concatenate([ys, yv.reshape(n, 3 * MUL_V)], axis=1)
        return _forward(x, edge_index, edge_feat, edge_scalars, W_ss, W_sv, W_vs, W_vv, W_rad, b_rad, L_s, L_v)

    def _L3_gnn_ref(node_input, node_attr, edge_vec, edge_scalars, edge_src, edge_dst, ln1_w0, ln1_b0, ln1_w1, ln2_w0, ln2_b0, ln2_w1, msrc_ws, msrc_wv, mdst_ws, mdst_bs, mdst_wv, rw1, rb1, rg1, rbe1, rw2, rb2, rg2, rbe2, rw3, roff, lin_ws, lin_bs, lin_wv, alpha_dot, proj_ws, proj_bs, proj_wv, f1_ws, f1_bs, f1_wv, f2_ws, f2_bs, f2_wv):
        import jax, jax.numpy as jnp
        import numpy as np
        N, E = (1250, 20000)
        C0, C1 = (64, 32)
        H, A = (8, 8)
        H0, H1 = (8, 4)
        M0, M1 = (128, 64)
        NG, RH = (64, 64)
        WN = C0 + C0 + C1 + C1 + C1
        DS, DV = (C0 + C1, C0 + 2 * C1)
        EPS = 1e-05
        SQ3 = np.float32(np.sqrt(3.0))
        SQ2 = np.float32(np.sqrt(2.0))

        def _split(x):
            return (x[:, :C0], x[:, C0:].reshape(x.shape[0], C1, 3))

        def _merge(s, v):
            return jnp.concatenate([s, v.reshape(v.shape[0], -1)], axis=1)

        def _eq_ln(x, w0, b0, w1):
            s, v = _split(x)
            s = s - s.mean(axis=1, keepdims=True)
            s = s * jax.lax.rsqrt(jnp.square(s).mean(axis=1, keepdims=True) + EPS) * w0 + b0
            v = v * jax.lax.rsqrt(jnp.square(v).mean(axis=(1, 2), keepdims=True) + EPS) * w1[None, :, None]
            return (s, v)

        def _eq_lin(s, v, ws, bs, wv):
            return (s @ ws + bs, jnp.einsum('nud,uk->nkd', v, wv))

        def _ln(x, g, b):
            xc = x - x.mean(-1, keepdims=True)
            return xc * jax.lax.rsqrt(jnp.square(xc).mean(-1, keepdims=True) + EPS) * g + b

        def _smooth_leaky(x, alpha=0.2):
            return 0.5 * (1 + alpha) * x + 0.5 * (1 - alpha) * x * (2.0 * jax.nn.sigmoid(x) - 1.0)

        def _forward(node_input, node_attr, edge_vec, edge_scalars, edge_src, edge_dst, ln1_w0, ln1_b0, ln1_w1, ln2_w0, ln2_b0, ln2_w1, msrc_ws, msrc_wv, mdst_ws, mdst_bs, mdst_wv, rw1, rb1, rg1, rbe1, rw2, rb2, rg2, rbe2, rw3, roff, lin_ws, lin_bs, lin_wv, alpha_dot, proj_ws, proj_bs, proj_wv, f1_ws, f1_bs, f1_wv, f2_ws, f2_bs, f2_wv):
            n = node_input.shape[0]
            s, v = _eq_ln(node_input, ln1_w0, ln1_b0, ln1_w1)
            src_s = s @ msrc_ws
            src_v = jnp.einsum('nud,uk->nkd', v, msrc_wv)
            dst_s = s @ mdst_ws + mdst_bs
            dst_v = jnp.einsum('nud,uk->nkd', v, mdst_wv)
            ms = src_s[edge_src] + dst_s[edge_dst]
            mv = src_v[edge_src] + dst_v[edge_dst]
            h = jax.nn.silu(_ln(edge_scalars @ rw1 + rb1, rg1, rbe1))
            h = jax.nn.silu(_ln(h @ rw2 + rb2, rg2, rbe2))
            w = h @ rw3 + roff
            rhat = edge_vec * jax.lax.rsqrt(jnp.sum(jnp.square(edge_vec), -1, keepdims=True) + 1e-12)
            Y1 = SQ3 * rhat
            w1, w2, w3, w4, w5 = jnp.split(w, [C0, 2 * C0, 2 * C0 + C1, 2 * C0 + 2 * C1], axis=1)
            o0a = w1 * ms
            o0b = w4 * (jnp.einsum('eud,ed->eu', mv, Y1) / SQ3)
            o1a = (w2 * ms)[:, :, None] * Y1[:, None, :]
            o1b = w3[:, :, None] * mv
            o1c = w5[:, :, None] * (jnp.cross(mv, Y1[:, None, :]) / SQ2)
            ds = jnp.concatenate([o0a, o0b], axis=1)
            dv = jnp.concatenate([o1a, o1b, o1c], axis=1)
            ls, lv = _eq_lin(ds, dv, lin_ws, lin_bs, lin_wv)
            e = ls.shape[0]
            alpha = ls[:, :H * A].reshape(e, H, A)
            vs = ls[:, H * A:].reshape(e, H, H0)
            vv = lv.reshape(e, H, H1, 3)
            a = jnp.einsum('ehk,hk->eh', _smooth_leaky(alpha), alpha_dot)
            amax = jax.lax.stop_gradient(jax.ops.segment_max(a, edge_dst, num_segments=n))
            a = jnp.exp(a - amax[edge_dst])
            a = a / (jax.ops.segment_sum(a, edge_dst, num_segments=n)[edge_dst] + 1e-12)
            ns = jax.ops.segment_sum(vs * a[..., None], edge_dst, num_segments=n).reshape(n, H * H0)
            nv = jax.ops.segment_sum(vv * a[..., None, None], edge_dst, num_segments=n).reshape(n, H * H1, 3)
            ps, pv = _eq_lin(ns, nv, proj_ws, proj_bs, proj_wv)
            x = node_input + _merge(ps, pv)
            s2, v2 = _eq_ln(x, ln2_w0, ln2_b0, ln2_w1)
            a0 = node_attr[:, :1]
            fs, fv = _eq_lin(s2, v2, f1_ws, f1_bs, f1_wv)
            fs = fs * a0
            fv = fv * a0[:, :, None]
            sc = jax.nn.silu(fs[:, :M0])
            fv = fv * jax.nn.sigmoid(fs[:, M0:])[:, :, None]
            os_, ov = _eq_lin(sc, fv, f2_ws, f2_bs, f2_wv)
            os_ = os_ * a0
            ov = ov * a0[:, :, None]
            return x + _merge(os_, ov)
        return _forward(node_input, node_attr, edge_vec, edge_scalars, edge_src, edge_dst, ln1_w0, ln1_b0, ln1_w1, ln2_w0, ln2_b0, ln2_w1, msrc_ws, msrc_wv, mdst_ws, mdst_bs, mdst_wv, rw1, rb1, rg1, rbe1, rw2, rb2, rg2, rbe2, rw3, roff, lin_ws, lin_bs, lin_wv, alpha_dot, proj_ws, proj_bs, proj_wv, f1_ws, f1_bs, f1_wv, f2_ws, f2_bs, f2_wv)
    edge_index = jnp.stack([src, dst])
    h = jnp.maximum(_layernorm(x, axis=-1), 0.0)
    x = x + _L0_gnn_ref(h, node_vec1, src, dst, edge_attr_4, edge_attr_10, L0_gnn_W_si0, L0_gnn_W_si1, L0_gnn_W_l1_0, L0_gnn_W_l1_1, L0_gnn_W_l2_00, L0_gnn_W_l2_10, L0_gnn_W_l2_01, L0_gnn_W_l2_11, L0_gnn_W_fc1, L0_gnn_W_fc2)
    h = jnp.maximum(_layernorm(x, axis=-1), 0.0)
    x = x + _L1_gnn_ref(h, edge_attr_16, edge_attr_4, L1_gnn_gamma_s, L1_gnn_beta_s, L1_gnn_gamma_v, L1_gnn_Ws_src, L1_gnn_Wv_src, L1_gnn_Ws_dst, L1_gnn_Wv_dst, L1_gnn_W_rbf, L1_gnn_W_alpha, L1_gnn_alpha_dot, L1_gnn_Ws_val, L1_gnn_Wv_val, L1_gnn_Wg, L1_gnn_w2_ss, L1_gnn_w2_sv, L1_gnn_w2_vs, L1_gnn_w2_vv0, L1_gnn_w2_vv1, L1_gnn_Ws_vlin, L1_gnn_Wv_vlin, L1_gnn_Wps, L1_gnn_Wpv, edge_index)
    h = jnp.maximum(_layernorm(x, axis=-1), 0.0)
    x = x + _L2_gnn_ref(h, edge_index, edge_attr_4, edge_attr_16, L2_gnn_W_ss, L2_gnn_W_sv, L2_gnn_W_vs, L2_gnn_W_vv, L2_gnn_W_rad, L2_gnn_b_rad, L2_gnn_L_s, L2_gnn_L_v)
    h = jnp.maximum(_layernorm(x, axis=-1), 0.0)
    x = x + _L3_gnn_ref(h, node_vec1, edge_attr_3, edge_attr_64, src, dst, L3_gnn_ln1_w0, L3_gnn_ln1_b0, L3_gnn_ln1_w1, L3_gnn_ln2_w0, L3_gnn_ln2_b0, L3_gnn_ln2_w1, L3_gnn_msrc_ws, L3_gnn_msrc_wv, L3_gnn_mdst_ws, L3_gnn_mdst_bs, L3_gnn_mdst_wv, L3_gnn_rw1, L3_gnn_rb1, L3_gnn_rg1, L3_gnn_rbe1, L3_gnn_rw2, L3_gnn_rb2, L3_gnn_rg2, L3_gnn_rbe2, L3_gnn_rw3, L3_gnn_roff, L3_gnn_lin_ws, L3_gnn_lin_bs, L3_gnn_lin_wv, L3_gnn_alpha_dot, L3_gnn_proj_ws, L3_gnn_proj_bs, L3_gnn_proj_wv, L3_gnn_f1_ws, L3_gnn_f1_bs, L3_gnn_f1_wv, L3_gnn_f2_ws, L3_gnn_f2_bs, L3_gnn_f2_wv)
    return x

_drawn_inputs = setup_inputs


def setup_inputs(seed=0):
    import zlib

    import numpy as np

    out = dict(_drawn_inputs(seed))
    spreads = {'L1_gnn_gamma_s': (1.0, 0.6),
     'L1_gnn_beta_s': (0.0, 0.516),
     'L1_gnn_gamma_v': (1.0, 0.6),
     'L3_gnn_ln1_w0': (1.0, 0.6),
     'L3_gnn_ln1_b0': (0.0, 0.428),
     'L3_gnn_ln1_w1': (1.0, 0.6),
     'L3_gnn_ln2_w0': (1.0, 0.6),
     'L3_gnn_ln2_b0': (0.0, 0.8),
     'L3_gnn_ln2_w1': (1.0, 0.6),
     'L3_gnn_mdst_bs': (0.0, 0.648),
     'L3_gnn_rb1': (0.0, 0.1),
     'L3_gnn_rg1': (1.0, 0.2),
     'L3_gnn_rbe1': (0.0, 0.374),
     'L3_gnn_rb2': (0.0, 0.1),
     'L3_gnn_rg2': (1.0, 0.2),
     'L3_gnn_rbe2': (0.0, 0.434),
     'L3_gnn_lin_bs': (0.0, 0.377),
     'L3_gnn_proj_bs': (0.0, 0.341),
     'L3_gnn_f1_bs': (0.0, 0.8),
     'L3_gnn_f2_bs': (0.0, 0.622)}
    factors = {'L0_gnn_W_l2_10': 2.775, 'L1_gnn_w2_vv1': 3.164}
    for name, (base, spread) in spreads.items():
        noise = np.random.default_rng([zlib.crc32(name.encode()), seed]).standard_normal(out[name].shape)
        drawn = base * np.exp(spread * noise) if base else spread * noise
        out[name] = jnp.asarray(drawn.astype(out[name].dtype))
    for name, factor in factors.items():
        out[name] = (out[name] * factor).astype(out[name].dtype)
    return out
```

```python
from contextlib import ExitStack

import numpy as np

import concourse.bass as bass
from concourse import mybir

F32 = mybir.dt.float32
BF16 = mybir.dt.bfloat16
I32 = mybir.dt.int32
ALU = mybir.AluOpType
ACT = mybir.ActivationFunctionType
AX = mybir.AxisListType

P = 128
N = 12500
NT = -(-N // P)
NP = NT * P
E = 200000
G = 4
SB = G * P
S = -(-E // (2 * SB)) * 2
T = S * G
EP = T * P
C0, C1 = 64, 32
W = C0 + 3 * C1
EPS = 1e-5
BIG = 1e30
LAYERS = 4

HW = 192
HEADS = (0, 4, 0, 8)
ROW_W = (384, W + 2 * 4, W, W + 2 * 8)
ZERO_ROW = EP
ZERO_CARRY = T + 1


class Steps:

    def __init__(self, sem, names):
        self.sem, self.names, self.n = sem, names, len(names)

    def at(self, r, name):
        return r * self.n + (self.names.index(name) + 1)




def wait(eng, steps, r, name):
    eng.wait_ge(steps.sem, steps.at(r, name))


def rounds(eng, stages, total):
    lag = max(l for _, l in stages)

    def turn(i, par, k):
        for fn, l in stages:
            if not isinstance(i, int) or 0 <= i - l < total:
                fn(i - l, (par - l) % 2, k + (par - l) // 2)

    head = lag + 2
    head += head % 2
    tail = total - (total - head) % 2
    for i in range(head):
        turn(i, i % 2, i // 2)
    with eng.Fori(head // 2, tail // 2) as k:
        turn(2 * k, 0, k)
        turn(2 * k + 1, 1, k)
    for i in range(tail, total + lag):
        turn(i, i % 2, i // 2)


def early(r, n=2):
    return isinstance(r, int) and r < n


class Env:
    pass


def clear(nc, sems):
    with nc.Block() as block:
        @block.gpsimd
        def _(pool):
            for s in sems:
                pool.sem_clear(s)


def load_blocks(sp, sem, pairs):
    for out, src in pairs:
        sp.dma_start(out, src).then_inc(sem, 16)
    return 16 * len(pairs)


def setup(nc, ctx, d):
    e = Env()

    def pool_dma_sem(name):
        return ctx.enter_context(nc.semaphore(name))

    e.pool_dma_sem = pool_dma_sem
    tag = "setup_"

    def sb(name, shape, dt=F32):
        return ctx.enter_context(nc.sbuf_tensor(tag + name, shape, dt))

    e.x = sb("x_nodes", [P, NT, W])
    e.src = sb("src_cols", [P, T], I32)
    e.dst = sb("dst_cols", [P, T], I32)
    e.ea4 = sb("ea4_cols", [P, T, 4])
    e.chain = sb("chain", [P, T])
    e.last = sb("last_row", [P, NT], I32)
    e.carry = sb("carry_row", [P, NT], I32)
    e.ident = sb("ident", [P, P])
    e.ones = sb("ones", [P, P])
    e.mhalf = sb("minus_half", [P, 8])
    e.attr = sb("node_attr", [P, NT])
    e.rows, e.carries, e.tsrc = [], [], []
    for layer, w in enumerate(ROW_W):
        e.rows.append([nc.dram_tensor(f"edge_rows{layer}_{i}", [EP + 1, min(w, HW)], F32, kind="Internal").ap()
                       for i in range(-(-w // HW))])
        e.carries.append(nc.dram_tensor(f"carry_rows{layer}", [T + 2, w], F32, kind="Internal").ap())
        e.tsrc.append(nc.dram_tensor(f"table_src{layer}", [NP, 384 if layer == 2 else W], F32,
                                     kind="Internal").ap())
    e.tdst = nc.dram_tensor("table_dst", [NP, W], F32, kind="Internal").ap()
    e.pens = nc.dram_tensor("resets", [EP + P], F32, kind="Internal").ap()
    e.h3 = nc.dram_tensor("h_last", [NP, W], F32, kind="Internal").ap()

    with ExitStack() as loc:
        def tmp(name, shape, dt=F32):
            return loc.enter_context(nc.sbuf_tensor(tag + name, shape, dt))

        sems = []

        def sem(name):
            sems.append(loc.enter_context(nc.semaphore(tag + name)))
            return sems[-1]

        RW = EP // P
        iota = tmp("iota", [P, P])
        hi_i = tmp("hi_i", [P, T], I32)
        hi = tmp("hi", [P, T])
        lo = tmp("lo", [P, T])
        is_lo = tmp("is_lo", [P, 2, G, P], BF16)
        is_hi = tmp("is_hi", [P, 2, G, NT], BF16)
        ends = tmp("ends", [P, T + 1], I32)
        run = tmp("run", [P, RW + 1], I32)
        pen = tmp("pen", [P, RW])
        tri = tmp("tri", [P, P])
        cnt = tmp("cnt", [P, NT])
        tot = tmp("tot", [P, NT])
        offs = tmp("offs", [P, NT + 1])
        end = tmp("end", [P, NT])
        beg = tmp("beg", [P, NT])
        has = tmp("has", [P, NT])
        w0 = tmp("w0", [P, NT])
        w1 = tmp("w1", [P, NT])
        til = tmp("til", [P, NT])
        til_i = tmp("til_i", [P, NT], I32)
        zrow = tmp("zrow", [P, 3 * P])
        counts = loc.enter_context(nc.psum_tensor("counts", [P, 512], F32))
        sums = loc.enter_context(nc.psum_tensor("sums", [P, 512], F32))
        loaded, stored = sem("loaded"), sem("stored")
        consts, ready = sem("consts"), sem("ready")
        hot, counted, summed, vec = sem("one_hots"), sem("counted"), sem("summed"), sem("vec")
        loc.callback(clear, nc, sems)
        block = loc.enter_context(nc.Block())

        @block.sync
        def _(sp):
            load_blocks(sp, loaded, [
                (e.dst[:, :], d["dst_cols"]), (e.src[:, :], d["src_cols"]),
                (ends[:, 1:T + 1], d["dst_cols"][P - 1:P, :].to_broadcast([P, T])),
                (ends[:, 0:1], d["dst_run"][0:1].rearrange("(a b) -> a b", a=1).to_broadcast([P, 1])),
                (run[:, 0:RW], d["dst_run"][0:EP].rearrange("(p f) -> p f", p=P)),
                (run[:, RW:RW + 1], d["dst_run"][RW:RW + EP].rearrange("(p f) -> p f", p=P)[:, 0:1]),
                (e.ea4[:, :, :], d["ea4_cols"]), (e.x[:, :, :], d["x"]), (e.attr[:, :], d["attr"])])
            sp.wait_ge(ready, 1)
            sp.dma_start(e.pens[0:EP].rearrange("(p f) -> p f", p=P), pen[:, :]).then_inc(stored, 16)
            sp.wait_ge(ready, 2)
            n = 2
            for rows, carries, w in zip(e.rows, e.carries, ROW_W):
                for part in rows:
                    sp.dma_start(part[EP:EP + 1, :], zrow[0:1, 0:min(w, HW)]).then_inc(stored, 16)
                    n += 1
                for k in (0, ZERO_CARRY):
                    sp.dma_start(carries[k:k + 1, :], zrow[0:1, 0:w]).then_inc(stored, 16)
                    n += 1
            sp.wait_ge(ready, 3)
            sp.dma_start(e.pens[EP:EP + P].rearrange("(a f) -> a f", a=1), tri[0:1, :]).then_inc(stored, 16)
            sp.wait_ge(stored, 16 * n)

        @block.gpsimd
        def _(pool):
            pool.iota(iota[:, :], [[1, P]], base=0, channel_multiplier=0,
                      allow_small_or_imprecise_dtypes=True).then_inc(consts, 1)
            pool.memset(e.ident[:, :], 0.0).then_inc(consts, 1)
            pool.memset(e.ones[:, :], 1.0).then_inc(consts, 1)
            pool.memset(e.mhalf[:, :], -0.5).then_inc(consts, 1)
            pool.wait_ge(consts, 4)
            pool.affine_select(out=e.ident[:, :], in_=e.ident[:, :], compare_op=ALU.not_equal, fill=1.0,
                               base=0, pattern=[[-1, P]], channel_multiplier=1).then_inc(consts, 1)
            pool.affine_select(out=tri[:, :], in_=e.ones[:, :], compare_op=ALU.is_ge, fill=0.0,
                               base=0, pattern=[[1, P]], channel_multiplier=-1).then_inc(consts, 1)

        @block.vector
        def _(dve):
            dve.wait_ge(loaded, 9 * 16)
            dve.wait_ge(consts, 6)
            nc.vector.tensor_scalar(hi_i[:, :], e.dst[:, :], 7, None, ALU.logical_shift_right).then_inc(vec, 1)
            dve.wait_ge(vec, 1)
            nc.vector.tensor_copy(hi[:, :], hi_i[:, :]).then_inc(vec, 1)
            dve.wait_ge(vec, 2)
            nc.vector.scalar_tensor_tensor(out=lo[:, :], in0=hi[:, :], scalar=-float(P), in1=e.dst[:, :],
                                           op0=ALU.mult, op1=ALU.add).then_inc(vec, 1)
            nc.vector.tensor_tensor(e.chain[:, :], ends[:, 1:T + 1], ends[:, 0:T], ALU.is_equal).then_inc(vec, 1)
            nc.vector.tensor_tensor(pen[:, :], run[:, 1:RW + 1], run[:, 0:RW], ALU.is_equal).then_inc(vec, 1)
            dve.wait_ge(vec, 5)
            nc.vector.tensor_scalar(pen[:, :], pen[:, :], 2 * BIG, -BIG, ALU.mult, ALU.add).then_inc(ready, 1)
            nc.vector.memset(zrow[:, :], 0.0).then_inc(ready, 1)

            def hots(r, b, n):
                if not early(r):
                    dve.wait_ge(counted, r - 1)
                nc.vector.tensor_tensor(is_lo[:, b], iota[:, :].unsqueeze(1).to_broadcast([P, G, P]),
                                        lo[:, bass.ds(r * G, G)].unsqueeze(2).to_broadcast([P, G, P]),
                                        ALU.is_equal).then_inc(hot, 1)
                nc.vector.tensor_tensor(is_hi[:, b], iota[:, 0:NT].unsqueeze(1).to_broadcast([P, G, NT]),
                                        hi[:, bass.ds(r * G, G)].unsqueeze(2).to_broadcast([P, G, NT]),
                                        ALU.is_equal).then_inc(hot, 1)

            rounds(dve, [(hots, 0)], S)
            dve.wait_ge(counted, S)
            nc.vector.tensor_copy(cnt[:, :], counts[:, 0:NT]).then_inc(vec, 1)
            dve.wait_ge(summed, 1)
            nc.vector.tensor_copy(tot[:, :], sums[:, 0:NT]).then_inc(vec, 1)
            nc.vector.memset(offs[:, 0:1], 0.0).then_inc(vec, 1)
            dve.wait_ge(vec, 8)
            nc.vector.tensor_tensor_scan(offs[:, 1:NT + 1], e.ones[:, 0:NT], tot[:, :], 0.0,
                                         ALU.mult, ALU.add).then_inc(vec, 1)
            dve.wait_ge(vec, 9)
            nc.vector.tensor_tensor(end[:, :], sums[:, P:P + NT], offs[:, 0:NT], ALU.add).then_inc(vec, 1)
            nc.vector.tensor_scalar(has[:, :], cnt[:, :], 0.0, None, ALU.is_gt).then_inc(vec, 1)
            dve.wait_ge(vec, 11)
            nc.vector.tensor_tensor(beg[:, :], end[:, :], cnt[:, :], ALU.subtract).then_inc(vec, 1)
            nc.vector.tensor_scalar(w0[:, :], end[:, :], float(-1 - ZERO_ROW), None, ALU.add).then_inc(vec, 1)
            dve.wait_ge(vec, 13)
            nc.vector.tensor_tensor(w0[:, :], w0[:, :], has[:, :], ALU.mult).then_inc(vec, 1)
            dve.wait_ge(vec, 14)
            nc.vector.tensor_scalar(e.last[:, :], w0[:, :], float(ZERO_ROW), None, ALU.add).then_inc(vec, 1)
            dve.wait_ge(vec, 15)
            nc.vector.tensor_scalar(til_i[:, :], e.last[:, :], 7, None, ALU.logical_shift_right).then_inc(vec, 1)
            dve.wait_ge(vec, 16)
            nc.vector.tensor_copy(til[:, :], til_i[:, :]).then_inc(vec, 1)
            dve.wait_ge(vec, 17)
            nc.vector.scalar_tensor_tensor(out=w1[:, :], in0=til[:, :], scalar=float(P), in1=beg[:, :],
                                           op0=ALU.mult, op1=ALU.is_gt).then_inc(vec, 1)
            dve.wait_ge(vec, 18)
            nc.vector.tensor_tensor(w1[:, :], w1[:, :], has[:, :], ALU.mult).then_inc(vec, 1)
            dve.wait_ge(vec, 19)
            nc.vector.scalar_tensor_tensor(out=w0[:, :], in0=til[:, :], scalar=float(-ZERO_CARRY), in1=w1[:, :],
                                           op0=ALU.add, op1=ALU.mult).then_inc(vec, 1)
            dve.wait_ge(vec, 20)
            nc.vector.tensor_scalar(e.carry[:, :], w0[:, :], float(ZERO_CARRY), None, ALU.add).then_inc(vec, 1)
            dve.wait_ge(vec, 21)
            nc.vector.memset(tri[0:1, :], -BIG).then_inc(ready, 1)

        @block.tensor
        def _(pe):
            def count(r, b, n):
                pe.wait_ge(hot, 2 * r + 2)
                for g in range(G):
                    first = isinstance(r, int) and r == 0 and g == 0
                    final = isinstance(r, int) and r == S - 1 and g == G - 1
                    mm = nc.tensor.matmul(counts[:, 0:NT], is_lo[:, b, g], is_hi[:, b, g],
                                          start=first, stop=final)
                mm.then_inc(counted, 1)

            rounds(pe, [(count, 1)], S)
            pe.wait_ge(vec, 6)
            nc.tensor.matmul(sums[:, 0:NT], e.ones[:, :], cnt[:, :], start=True, stop=True)
            nc.tensor.matmul(sums[:, P:P + NT], tri[:, :], cnt[:, :], start=True, stop=True).then_inc(summed, 1)
    return e


def carry_phase(nc, e, layer, width, heads=0, per_s=0, per_v=0):
    tag = f"carry{layer}_"
    chunks = [(c, min(P, width - c)) for c in range(0, width, P)]
    TG = -(-T // P)
    with ExitStack() as loc:
        def tmp(name, shape, dt=F32):
            return loc.enter_context(nc.sbuf_tensor(tag + name, shape, dt))

        sems = []

        def sem(name):
            sems.append(loc.enter_context(nc.semaphore(tag + name)))
            return sems[-1]

        H = heads
        scanned = width - H if H else width
        lasts = tmp("lasts", [P, TG, width])
        state = tmp("state", [P, TG, width])
        fin = tmp("feat_in", [P, T])
        fout = tmp("feat_out", [P, T])
        ps = loc.enter_context(nc.psum_tensor(tag + "ps", [P, 4, 512], F32))
        loaded, stored = sem("loaded"), sem("stored")
        turned, copied, scans, back, final = sem("turned"), sem("copied"), sem("scans"), sem("back"), sem("final")
        if H:
            shifts = tmp("shifts", [H, T + 1])
            decay = tmp("decay", [H, T])
            wide = tmp("wide", [P, T])
            expand = tmp("expand", [H, 2 * P])
            sh_in, sh_out, dec, spread, widened = (sem("shift_turned"), sem("shift_copied"), sem("decayed"),
                                                   sem("spread"), sem("widened"))
            exped, zeroed, loadw = sem("exped"), sem("zeroed"), sem("loadw")
        loc.callback(clear, nc, sems)
        block = loc.enter_context(nc.Block())
        parts = [(i, min(HW, width - HW * i)) for i in range(-(-width // HW))]
        rows = [part[0:EP, :].rearrange("(t p) w -> t p w", p=P)[:, P - 1, :] for part in e.rows[layer]]
        full = T // P
        part = T - full * P
        tiles = [(k, P if k < full else part) for k in range(TG)]
        NQ = -(-T // 512)

        @block.sync
        def _(sp):
            for k, m in tiles:
                for i, w in parts:
                    sp.dma_start(lasts[0:m, k, HW * i:HW * i + w], rows[i][k * P:k * P + m, 0:w])\
                        .then_inc(loaded, 16)
            sp.wait_ge(final, len(chunks) * TG + (1 if H else 0))
            for k, m in tiles:
                sp.dma_start(e.carries[layer][1 + k * P:1 + k * P + m, :], state[0:m, k, :]).then_inc(stored, 16)
            sp.wait_ge(stored, 16 * TG)

        if H:
            @block.gpsimd
            def _(pool):
                pool.memset(expand[:, :], 1.0).then_inc(zeroed, 1)
                n = 1
                for a, b, per in ((0, C0, per_s), *((C0 + C1 * i, C0 + C1 * i + C1, per_v) for i in range(3)),
                                  (W, W + H, 1)):
                    v = expand[:, a:b]
                    pool.wait_ge(zeroed, n)
                    pool.affine_select(out=v, in_=v, compare_op=ALU.is_ge, fill=0.0, base=0,
                                       pattern=[[1, b - a]], channel_multiplier=-per).then_inc(zeroed, 1)
                    pool.wait_ge(zeroed, n + 1)
                    pool.affine_select(out=v, in_=v, compare_op=ALU.is_ge, fill=0.0, base=per - 1,
                                       pattern=[[-1, b - a]], channel_multiplier=per).then_inc(zeroed, 1)
                    n += 2

        @block.tensor
        def _(pe):
            pe.wait_ge(loaded, 16 * TG * len(parts))
            if H:
                for k, m in tiles:
                    mm = nc.tensor.transpose(ps[0:H, k // 4, (k % 4) * P:(k % 4) * P + m],
                                             lasts[0:m, k, width - H:width], e.ident[0:m, 0:m])
                mm.then_inc(sh_in, 1)
                pe.wait_ge(sh_out, 1)
            for c, (c0, cw) in enumerate(chunks):
                if H:
                    pe.wait_ge(zeroed, 11)
                    pe.wait_ge(exped, 2)
                    cs = min(cw, scanned - c0)
                    if c:
                        pe.wait_ge(final, c * TG)
                    for q in range(NQ):
                        n = min(512, T - 512 * q)
                        mm = nc.tensor.matmul(ps[0:cs, q, 0:n], expand[:, c0:c0 + cs],
                                              decay[:, 512 * q:512 * q + n], start=True, stop=True)
                    mm.then_inc(spread, 1)
                    pe.wait_ge(widened, c + 1)
                elif c:
                    pe.wait_ge(final, c * TG)
                for k, m in tiles:
                    mm = nc.tensor.transpose(ps[0:cw, k // 4, (k % 4) * P:(k % 4) * P + m],
                                             lasts[0:m, k, c0:c0 + cw], e.ident[0:m, 0:m])
                mm.then_inc(turned, 1)
                pe.wait_ge(scans, c + 1)
                for k, m in tiles:
                    if k >= 4:
                        pe.wait_ge(final, c * TG + k - 3)
                    else:
                        pe.wait_ge(copied, c + 1)
                    nc.tensor.transpose(ps[0:m, k % 4, 0:cw], fout[0:cw, k * P:k * P + m],
                                        e.ident[0:cw, 0:cw]).then_inc(back, 1)

        @block.scalar
        def _(act):
            if H:
                act.wait_ge(dec, 2)
                nc.scalar.activation(decay[:, :], decay[:, :], ACT.Exp).then_inc(exped, 1)

        @block.vector
        def _(dve):
            n = 0
            if H:
                nc.vector.memset(shifts[:, 0:1], 0.0).then_inc(dec, 1)
                dve.wait_ge(sh_in, 1)
                nc.vector.tensor_copy(shifts[:, 1:T + 1],
                                      ps[0:H, :, :].rearrange("p a b -> p (a b)")[:, 0:T]).then_inc(sh_out, 1)
                dve.wait_ge(sh_out, 1)
                dve.wait_ge(dec, 1)
                nc.vector.tensor_tensor(decay[:, :], shifts[:, 0:T], shifts[:, 1:T + 1], ALU.subtract)\
                    .then_inc(loadw, 1)
                dve.wait_ge(loadw, 1)
                nc.vector.tensor_scalar(decay[:, :], decay[:, :], 0.0, None, ALU.min).then_inc(dec, 1)
                dve.wait_ge(exped, 1)
                nc.vector.tensor_tensor(decay[:, :], decay[:, :], e.chain[0:H, :], ALU.mult).then_inc(exped, 1)
            for c, (c0, cw) in enumerate(chunks):
                cs = min(cw, scanned - c0)
                if H:
                    dve.wait_ge(spread, c + 1)
                    nc.vector.tensor_copy(wide[0:cs, :], ps[0:cs, :, :].rearrange("p a b -> p (a b)")[:, 0:T])\
                        .then_inc(widened, 1)
                dve.wait_ge(turned, c + 1)
                if c:
                    dve.wait_ge(back, c * TG)
                nc.vector.tensor_copy(fin[0:cw, :], ps[0:cw, :, :].rearrange("p a b -> p (a b)")[:, 0:T])\
                    .then_inc(copied, 1)
                dve.wait_ge(copied, c + 1)
                if H:
                    dve.wait_ge(widened, c + 1)
                    if cs < cw:
                        nc.vector.tensor_copy(fout[0:cw, :], fin[0:cw, :]).then_inc(loadw, 1)
                        dve.wait_ge(loadw, 2)
                    nc.vector.tensor_tensor_scan(fout[0:cs, :], wide[0:cs, :], fin[0:cs, :], 0.0,
                                                 ALU.mult, ALU.add).then_inc(scans, 1)
                else:
                    nc.vector.tensor_tensor_scan(fout[0:cs, :], e.chain[0:cs, :], fin[0:cs, :], 0.0,
                                                 ALU.mult, ALU.add).then_inc(scans, 1)
                for k, m in tiles:
                    dve.wait_ge(back, c * TG + k + 1)
                    nc.vector.tensor_copy(state[0:m, k, c0:c0 + cw], ps[0:m, k % 4, 0:cw]).then_inc(final, 1)
            if H:
                nc.vector.memset(shifts[:, 0:1], 0.0).then_inc(final, 1)


def dst_same(nc, dve, e, same, dst_b, r, b):
    return nc.vector.tensor_tensor(same[:, b], dst_b[:, b].rearrange("p (g i) -> p g i", g=G),
                                   e.dst[:, bass.ds(r * G, G)].unsqueeze(2).to_broadcast([P, G, P]),
                                   ALU.is_equal)


def edge_conv(nc, e, d, layer):
    L0 = layer == 0
    tag = f"edge{layer}_"
    TW = W if L0 else 384
    MW = 384 if L0 else W
    KE = 10 if L0 else 17
    parts = [(i, min(HW, MW - HW * i)) for i in range(-(-MW // HW))]
    with ExitStack() as loc:
        def tmp(name, shape, dt=F32):
            return loc.enter_context(nc.sbuf_tensor(tag + name, shape, dt))

        sems = []

        def sem(name):
            sems.append(loc.enter_context(nc.semaphore(tag + name)))
            return sems[-1]

        def ps(name, shape):
            return loc.enter_context(nc.psum_tensor(tag + name, shape, F32))

        idx = tmp("idx", [P, 2, G], I32)
        row = tmp("row", [P, 2, G, TW])
        feat = tmp("feat", [KE, 2, SB])
        dst_b = tmp("dst_b", [P, 2, SB], I32)
        same = tmp("same", [P, 2, G, P])
        msg = tmp("msg", [P, 2, G, MW])
        out = tmp("out", [P, 2, G, MW])
        if L0:
            w_a = tmp("w_fc1", [10, 100])
            w_b = tmp("w_fc2", [100, 192])
            hid = tmp("hid", [100, 2, SB])
            wy = tmp("wy", [P, G, 2, C0])
            we = tmp("we", [P, G, C1])
            dot = tmp("dot", [P, G, 3, C1])
            ps_h = ps("ps_h", [P, 512])
        else:
            w_a = tmp("w_rad", [17, W])
            sig = tmp("sig", [P, 2, G, W])
            u = tmp("u", [P, G, 4, C0])
            q = tmp("q", [P, G, 3, C1])
            r_ = tmp("r_", [P, G, 3, C1])
        ps_w = ps("ps_w", [P, G, 256])
        ps_a = ps("ps_a", [P, G, 512 if L0 else 256])
        loadw, scaled = sem("weights_loaded"), sem("weights_scaled")
        picked = sem("indices_copied")
        rows_in = [e.pool_dma_sem(tag + f"rows_in{b}") for b in range(2)]
        feat_in = [sem(f"feat_in{b}") for b in range(2)]
        dst_in = [sem(f"dst_in{b}") for b in range(2)]
        out_sent = [sem(f"out_sent{b}") for b in range(2)]
        if L0:
            V = Steps(sem("vec_msg"), ["same", "wy", "we", "dot", "m0", "m1", "m2", "dot1", "dot2", "m3"])
        else:
            V = Steps(sem("vec_msg"), ["same", "u", "q", "r", "u2", "v", "us", "ms", "mv"])
        PA = Steps(sem("pe_weights"), ["hid", "w"] if L0 else ["w"])
        PB = Steps(sem("pe_sums"), ["sums"])
        A = Steps(sem("act_weights"), ["hid"] if L0 else ["sig"])
        B = Steps(sem("act_sums"), ["lo", "hi"])
        first = "hid" if L0 else "sig"
        lastv = V.names[-1]
        readers_row = V.names[-1]
        loc.callback(clear, nc, sems)
        block = loc.enter_context(nc.Block())

        @block.sync
        def _(sp):
            if L0:
                load_blocks(sp, loadw, [(w_a[:, :], d["L0_gnn_W_fc1"]), (w_b[:, :], d["L0_gnn_W_fc2"])])
            else:
                load_blocks(sp, loadw, [(w_a[:, :], d["L2_rad"])])

            def load(r, b, n):
                if not early(r):
                    wait(sp, PA, r - 2, PA.names[0])
                sp.dma_start(feat[:, b], (d["ea10_rows"] if L0 else d["ea16_rows"])[0:KE, bass.ds(r * SB, SB)])\
                    .then_inc(feat_in[b], 16)
                if not early(r):
                    wait(sp, V, r - 2, "same")
                sp.dma_start(dst_b[:, b], d["dst_rows"][0:1, bass.ds(r * SB, SB)].to_broadcast([P, SB]))\
                    .then_inc(dst_in[b], 16)

            def store(r, b, n):
                wait(sp, B, r, "hi")
                for i, w in parts:
                    sp.dma_start(e.rows[layer][i][bass.ds(r * SB, SB), :].rearrange("(g p) w -> p g w", p=P),
                                 out[:, b, :, HW * i:HW * i + w]).then_inc(out_sent[b], 16)

            rounds(sp, [(load, 0), (store, 2)], S)
            for b in range(2):
                sp.wait_ge(out_sent[b], 16 * len(parts) * (S // 2))

        @block.gpsimd
        def _(pool):
            def fetch(r, b, n):
                if not early(r):
                    wait(pool, V, r - 2, readers_row)
                    pool.wait_ge(rows_in[b], 16 * G * n)
                    pool.nop(nofuse=True)
                nc.gpsimd.tensor_copy(idx[:, b, :], e.src[:, bass.ds(r * G, G)]).then_inc(picked, 1)
                pool.wait_ge(picked, r + 1)
                pool.nop(nofuse=True)
                for g in range(G):
                    pool.indirect_dma_start(row[:, b, g, :], None, e.tsrc[layer],
                                            bass.IndirectOffsetOnAxis(ap=idx[:, b, g:g + 1], axis=0))\
                        .then_inc(rows_in[b], 16)

            rounds(pool, [(fetch, 0)], S)

        @block.tensor
        def _(pe):
            pe.wait_ge(loadw, 32 if L0 else 16)
            if L0:
                pe.wait_ge(scaled, 1)

            def weights(r, b, n):
                pe.wait_ge(feat_in[b], 16 * (n + 1))
                if L0:
                    if not early(r, 1):
                        wait(pe, A, r - 1, "hid")
                    nc.tensor.matmul(ps_h[0:100, :], w_a[:, :], feat[:, b], start=True, stop=True)\
                        .then_inc(PA.sem, 1)
                    wait(pe, A, r, "hid")
                if not early(r, 1):
                    if L0:
                        wait(pe, V, r - 1, "m3")
                    else:
                        wait(pe, A, r - 1, "sig")
                for g in range(G):
                    lhs = hid[:, b, g * P:(g + 1) * P] if L0 else feat[:, b, g * P:(g + 1) * P]
                    mm = nc.tensor.matmul(ps_w[:, g, 0:(192 if L0 else W)], lhs, w_b[:, :] if L0 else w_a[:, :],
                                          start=True, stop=True)
                mm.then_inc(PA.sem, 1)

            def sums(r, b, n):
                wait(pe, V, r, lastv)
                if not early(r, 1):
                    wait(pe, B, r - 1, "hi")
                for g in range(G):
                    mm = nc.tensor.matmul(ps_a[:, g, 0:MW], same[:, b, g], msg[:, b, g], start=True, stop=True)
                mm.then_inc(PB.sem, 1)

            rounds(pe, [(weights, 0), (sums, 1)], S)

        @block.scalar
        def _(act):
            def weights(r, b, n):
                wait(act, PA, r, "hid" if L0 else "w")
                if L0:
                    if not early(r):
                        wait(act, PA, r - 2, "w")
                    nc.scalar.activation(hid[:, b], ps_h[0:100, :], ACT.Relu, scale=1.0 / np.sqrt(10.0))\
                        .then_inc(A.sem, 1)
                else:
                    if not early(r):
                        wait(act, V, r - 2, "mv")
                    nc.scalar.activation(sig[:, b], ps_w[:, :, 0:W], ACT.Sigmoid).then_inc(A.sem, 1)

            def sums(r, b, n):
                wait(act, PB, r, "sums")
                if not early(r):
                    act.wait_ge(out_sent[b], 16 * len(parts) * n)
                for h in range(2):
                    nc.scalar.copy(out[:, b, 2 * h:2 * h + 2], ps_a[:, 2 * h:2 * h + 2, 0:MW]).then_inc(B.sem, 1)

            rounds(act, [(weights, 0), (sums, 1)], S)

        @block.vector
        def _(dve):
            if L0:
                dve.wait_ge(loadw, 32)
                nc.vector.tensor_scalar(w_b[:, :], w_b[:, :], float(np.sqrt(2.0) / 10.0), None, ALU.mult)\
                    .then_inc(scaled, 1)

            def att(r, i0, i1):
                return e.ea4[:, bass.ds(r * G, G), i0:i1]

            def done(ins):
                ins.then_inc(V.sem, 1)

            def messages0(r, b, n):
                tt = nc.vector.tensor_tensor
                if not early(r, 1):
                    wait(dve, V, r - 1, V.names[-1])
                dve.wait_ge(dst_in[b], 16 * (n + 1))
                if not early(r):
                    wait(dve, PB, r - 2, "sums")
                done(dst_same(nc, dve, e, same, dst_b, r, b))
                wait(dve, PA, r, "w")
                dve.wait_ge(rows_in[b], 16 * G * (n + 1))
                y = row[:, b]
                yv = y[:, :, C0:W].rearrange("p g (d c) -> p g d c", d=3)
                done(tt(wy[:, :, :, :], ps_w[:, :, 0:128].rearrange("p g (a c) -> p g a c", a=2),
                        y[:, :, 0:C0].unsqueeze(2).to_broadcast([P, G, 2, C0]), ALU.mult))
                done(tt(we[:, :, :], ps_w[:, :, 128:160], att(r, 0, 1).to_broadcast([P, G, C1]), ALU.mult))
                done(tt(dot[:, :, :, :], yv, att(r, 1, 4).unsqueeze(3).to_broadcast([P, G, 3, C1]), ALU.mult))
                wait(dve, V, r, "wy")
                done(tt(msg[:, b, :, 0:C0], wy[:, :, 0, :], att(r, 0, 1).to_broadcast([P, G, C0]), ALU.mult))
                m = msg[:, b, :, 96:384].rearrange("p g (d c) -> p g d c", d=3)
                done(tt(m[:, :, :, 0:C0], wy[:, :, 1, :].unsqueeze(2).to_broadcast([P, G, 3, C0]),
                        att(r, 1, 4).unsqueeze(3).to_broadcast([P, G, 3, C0]), ALU.mult))
                wait(dve, V, r, "dot")
                done(tt(m[:, :, :, C0:96], we[:, :, :].unsqueeze(2).to_broadcast([P, G, 3, C1]), yv, ALU.mult))
                done(tt(dot[:, :, 0, :], dot[:, :, 0, :], dot[:, :, 1, :], ALU.add))
                wait(dve, V, r, "dot1")
                done(tt(dot[:, :, 0, :], dot[:, :, 0, :], dot[:, :, 2, :], ALU.add))
                wait(dve, V, r, "dot2")
                done(tt(msg[:, b, :, C0:96], dot[:, :, 0, :], ps_w[:, :, 160:192], ALU.mult))

            def messages2(r, b, n):
                tt = nc.vector.tensor_tensor
                if not early(r, 1):
                    wait(dve, V, r - 1, V.names[-1])
                dve.wait_ge(dst_in[b], 16 * (n + 1))
                if not early(r):
                    wait(dve, PB, r - 2, "sums")
                done(dst_same(nc, dve, e, same, dst_b, r, b))
                dve.wait_ge(rows_in[b], 16 * G * (n + 1))
                y = row[:, b]
                done(tt(u[:, :, :, :], y[:, :, 0:256].rearrange("p g (k c) -> p g k c", k=4),
                        att(r, 0, 4).unsqueeze(3).to_broadcast([P, G, 4, C0]), ALU.mult))
                done(tt(q[:, :, :, :], y[:, :, 256:288].unsqueeze(2).to_broadcast([P, G, 3, C1]),
                        att(r, 1, 4).unsqueeze(3).to_broadcast([P, G, 3, C1]), ALU.mult))
                done(tt(r_[:, :, :, :].rearrange("p g d c -> p g (d c)"), y[:, :, 288:384],
                        att(r, 0, 1).to_broadcast([P, G, 96]), ALU.mult))
                wait(dve, V, r, "u")
                done(tt(u[:, :, 0:2, :], u[:, :, 0:2, :], u[:, :, 2:4, :], ALU.add))
                wait(dve, V, r, "r")
                done(tt(q[:, :, :, :], q[:, :, :, :], r_[:, :, :, :], ALU.add))
                wait(dve, V, r, "u2")
                done(tt(u[:, :, 0, :], u[:, :, 0, :], u[:, :, 1, :], ALU.add))
                wait(dve, A, r, "sig")
                wait(dve, V, r, "us")
                done(tt(msg[:, b, :, 0:C0], u[:, :, 0, :], sig[:, b, :, 0:C0], ALU.mult))
                done(tt(msg[:, b, :, C0:W], q[:, :, :, :].rearrange("p g d c -> p g (d c)"),
                        sig[:, b, :, C0:W], ALU.mult))

            rounds(dve, [(messages0 if L0 else messages2, 0)], S)


def edge_attention(nc, e, d, layer):
    L1 = layer == 1
    tag = f"edge{layer}_"
    H = HEADS[layer]
    per_s, per_v = C0 // H, C1 // H
    MW = W + H
    RW = W + 2 * H
    KE = 16 if L1 else 65
    KB = 96 if L1 else 97
    r2, r3 = 1.0 / float(np.sqrt(2.0)), 1.0 / float(np.sqrt(3.0))
    with ExitStack() as loc:
        def tmp(name, shape, dt=F32):
            return loc.enter_context(nc.sbuf_tensor(tag + name, shape, dt))

        sems = []

        def sem(name):
            sems.append(loc.enter_context(nc.semaphore(tag + name)))
            return sems[-1]

        def ps(name, shape):
            return loc.enter_context(nc.psum_tensor(tag + name, shape, F32))

        idx = tmp("idx", [P, 2, 2, G], I32)
        row = tmp("row", [P, 2, 2, G, W])
        feat = tmp("feat", [KE, 2, SB])
        dst_b = tmp("dst_b", [P, 2, SB], I32)
        pen = tmp("pen", [H, 2, SB + 1])
        m = tmp("m", [P, G, C0 + 5 * C1])
        y5 = tmp("y5", [P, G, 5])
        t1 = tmp("t1", [P, G, 3, C1])
        t2 = tmp("t2", [P, G, 3, C1])
        t3 = tmp("t3", [P, G, 3, C1])
        dot = tmp("dot", [P, G, 3, C1])
        x1 = tmp("x1", [P, G, 96])
        x23 = tmp("x23", [P, G, 256])
        x1t = tmp("x1t", [KB, SB])
        x2t = tmp("x2t", [P, SB])
        x3t = tmp("x3t", [P, SB])
        bend = tmp("bend", [C0, SB])
        soft = tmp("soft", [C0, SB])
        shf = tmp("shf", [H, 2, SB])
        shb = tmp("shb", [H, SB])
        arg = tmp("arg", [H, SB])
        es = tmp("es", [32 + H, SB])
        exs = tmp("exs", [P, G, 32 + H])
        exv = tmp("exv", [P, G, C1])
        same = tmp("same", [P, 2, G, P])
        msg = tmp("msg", [P, 2, G, MW])
        out = tmp("out", [P, 2, G, RW])
        w_rad = tmp("w_rad", [KE, 224])
        w_al = tmp("w_al", [KB, C0])
        w_ad = tmp("w_ad", [C0, H])
        w_s = tmp("w_s", [KB, C0])
        w_v = tmp("w_v", [P, 2, C0])
        ps_w = ps("ps_w", [P, G, 256])
        ps_n = ps("ps_n", [P, 512])
        ps_a = ps("ps_a", [P, 2, 256])
        ps_x = ps("ps_x", [P, 512])
        ps_l = ps("ps_l", [P, 512])
        ps_v = ps("ps_v", [P, G, 128])
        ps_s = ps("ps_s", [P, 512])
        out_s = ps_s[:, 0:256].rearrange("p (g c) -> p g c", g=G)
        ex_p = ps_s[:, 256:256 + G * (32 + H)].rearrange("p (g c) -> p g c", g=G)
        if L1:
            wy = tmp("wy", [P, G, 96])
            vt = tmp("vt", [C0, SB])
            gate = tmp("gate", [P, G, C1])
            gh = tmp("gh", [P, G, C1])
            sh = tmp("sh", [P, G, C0])
            v5 = tmp("v5", [P, G, 5, C1])
            w_g = tmp("w_g", [C0, C1])
            w_s2 = tmp("w_s2", [96, C0])
            w_v2 = tmp("w_v2", [P, 2, C0])
            c_s2 = tmp("c_s2", [96, 1])
            c_v2 = tmp("c_v2", [P, 2, 1])
        else:
            ea4_flat = e.ea4[:, :, :].rearrange("p t k -> p (t k)")
            y3 = ea4_flat[:, 0:3 * T].rearrange("p (t k) -> p t k", k=3)
            part = ea4_flat[:, 3 * T:4 * T]
            len2 = tmp("len2", [P, T])
            w1 = tmp("w1", [65, C0])
            w2 = tmp("w2", [65, C0])
            w3 = tmp("w3", [65, 224])
            mean = tmp("mean", [65, 2])
            gb = tmp("gb", [C0, 4])
            gbh = tmp("gbh", [C0, 4])
            sq = tmp("sq", [P, G, C0])
            ve = tmp("ve", [P, G])
            rs = tmp("rs", [P, G])
            zn = tmp("zn", [P, G, C0])
            hu = tmp("hu", [C0, SB])
            th = tmp("th", [C0, SB])
            h1t = tmp("h1t", [65, SB])
            h2t = tmp("h2t", [65, 2, SB])

        loadw, zeroed, prepped, chained, pooled = (sem("weights_loaded"), sem("zeroed"), sem("weights_ready"),
                                                   sem("prep_chain"), sem("prep_pool"))
        picked = sem("indices_copied")
        rows_in = [e.pool_dma_sem(tag + f"rows_in{b}") for b in range(2)]
        feat_in = [sem(f"feat_in{b}") for b in range(2)]
        dst_in = [sem(f"dst_in{b}") for b in range(2)]
        pen_in = [sem(f"pen_in{b}") for b in range(2)]
        out_sent = [sem(f"out_sent{b}") for b in range(2)]
        VP = Steps(sem("vec_product"), ["m", "m5", "y5", "y5b"] + (["wy"] if L1 else []) +
                   ["dot", "t1", "t2", "s", "q", "vs", "dot1", "t12", "dot2", "cross", "o0b"])
        VM = Steps(sem("vec_maps"), ["soft"] + (["zy", "bc", "gate", "q", "v5", "v5b", "dot", "t1", "t2", "s", "vs",
                                                 "dot1", "cross", "o0b"] if L1 else []) +
                   ["fwd", "bwd", "arg"])
        VJ = Steps(sem("vec_joint"), ["same", "exs", "exv", "s", "zy", "bc", "v", "w"])
        PP = Steps(sem("pe_product"), ["w", "x1", "x2", "x3"])
        PM = Steps(sem("pe_maps"), ["al", "s"] + (["vt"] if L1 else []) + ["v", "at"] +
                   (["gate", "x1", "x2", "x3", "s2"] if L1 else []))
        PJ = Steps(sem("pe_joint"), ["ex", "lo", "hi"])
        AP_ = Steps(sem("act_product"), ["x1", "x2", "x3"])
        AM = Steps(sem("act_maps"), ["bend"] + (["vt", "sh", "gh", "x1", "x2", "x3"] if L1 else []) + ["ex", "sh2"])
        AJ = Steps(sem("act_joint"), ["shift", "lo", "hi"])
        if not L1:
            VN = Steps(sem("vec_norms"), ["ss1", "ve1", "zn1", "h1", "ss2", "ve2", "zn2", "h2"])
            PN = Steps(sem("pe_norms"), ["z1", "zt1", "z2", "zt2"])
            AN = Steps(sem("act_norms"), ["sq1", "hu1", "th1", "sq2", "hu2", "th2"])
            KN = Steps(sem("pool_norms"), ["rs1", "rs2"])
        def c1(ap):
            return ap.rearrange("(p a) -> p a", a=1)

        def maps_loads(w_v, wv):
            return [(w_v[0:64, 0, 0:32], wv[0:64, :]), (w_v[64:128, 0, 32:64], wv[64:128, :]),
                    (w_v[0:64, 1, 0:32], wv[64:128, :]), (w_v[64:128, 1, 32:64], wv[64:128, :])]

        def rad_loads(w, src, k):
            return [(w[0:k, 0:64], src[:, 0:64]), (w[0:k, 64:96], src[:, 128:160]), (w[0:k, 96:160], src[:, 64:128]),
                    (w[0:k, 160:224], src[:, 160:224])]

        wload = []
        if L1:
            wload += rad_loads(w_rad, d["L1_gnn_W_rbf"], 16)
            wload += [(w_al[:, :], d["L1_gnn_W_alpha"]), (w_s[:, :], d["L1_gnn_Ws_val"]), (w_g[:, :], d["L1_gnn_Wg"]),
                      (w_s2[:, :], d["L1_gnn_Ws_vlin"])]
            wload += maps_loads(w_v, d["L1_gnn_Wv_val"]) + maps_loads(w_v2, d["L1_gnn_Wv_vlin"])
            wload += [(c_s2[0:64, :], c1(d["L1_gnn_w2_ss"])), (c_s2[64:96, :], c1(d["L1_gnn_w2_vv0"])),
                      (c_v2[0:64, 0, :], c1(d["L1_gnn_w2_sv"]))]
            for p0, k in ((64, 0), (0, 1), (64, 1)):
                wload += [(c_v2[p0:p0 + 32, k, :], c1(d["L1_gnn_w2_vs"])),
                          (c_v2[p0 + 32:p0 + 64, k, :], c1(d["L1_gnn_w2_vv1"]))]
            adot = d["L1_gnn_alpha_dot"]
        else:
            wload += rad_loads(w3, d["L3_gnn_rw3"], 64)
            roff = d["L3_gnn_roff"].rearrange("(a b) -> a b", a=1)
            wload += rad_loads(w3[64:65, :], roff, 1)
            c = lambda n: d["L3_gnn_" + n].rearrange("(a b) -> a b", a=1)
            wload += [(w1[0:64, :], d["L3_gnn_rw1"]), (w1[64:65, :], c("rb1")),
                      (w2[0:64, :], d["L3_gnn_rw2"]), (w2[64:65, :], c("rb2")),
                      (w_al[0:96, :], d["L3_gnn_lin_ws"][:, 0:64]), (w_al[96:97, :], c("lin_bs")[:, 0:64]),
                      (w_s[0:96, :], d["L3_gnn_lin_ws"][:, 64:128]), (w_s[96:97, :], c("lin_bs")[:, 64:128]),
                      (y3[:, :, :], d["ea3_cols"])]
            wload += maps_loads(w_v, d["L3_gnn_lin_wv"])
            wload += [(gb[:, i:i + 1], c1(d["L3_gnn_" + n])) for i, n in enumerate(("rg1", "rbe1", "rg2", "rbe2"))]
            adot = d["L3_gnn_alpha_dot"]
        for h in range(H):
            wload += [(w_ad[per_s * h:per_s * h + per_s, h:h + 1],
                       adot[(0, h) if len(adot.shape) == 3 else h].rearrange("(p a) -> p a", a=1))]
        zero = [w_v[:, :, :], w_ad[:, :], es[:, :]] + ([w_v2[:, :, :]] if L1 else [])
        loc.callback(clear, nc, sems)
        block = loc.enter_context(nc.Block())

        @block.sync
        def _(sp):
            sp.wait_ge(zeroed, len(zero))
            load_blocks(sp, loadw, wload)

            def load(r, b, n):
                if not early(r):
                    wait(sp, PP if L1 else PN, r - 2, "w" if L1 else "z1")
                sp.dma_start(feat[:, b], d["ea16_rows" if L1 else "ea64_rows"][0:KE, bass.ds(r * SB, SB)])\
                    .then_inc(feat_in[b], 16)
                if not early(r):
                    wait(sp, VJ, r - 2, "same")
                sp.dma_start(dst_b[:, b], d["dst_rows"][0:1, bass.ds(r * SB, SB)].to_broadcast([P, SB]))\
                    .then_inc(dst_in[b], 16)
                if not early(r):
                    wait(sp, VM, r - 2, "bwd")
                sp.dma_start(pen[:, b], e.pens[bass.ds(r * SB, SB + 1)].rearrange("(a f) -> a f", a=1)
                             .to_broadcast([H, SB + 1])).then_inc(pen_in[b], 16)

            def store(r, b, n):
                wait(sp, AJ, r, "hi")
                sp.dma_start(e.rows[layer][0][bass.ds(r * SB, SB), :].rearrange("(g p) w -> p g w", p=P),
                             out[:, b]).then_inc(out_sent[b], 16)

            rounds(sp, [(load, 0), (store, 2 if L1 else 3)], S)
            for b in range(2):
                sp.wait_ge(out_sent[b], 16 * (S // 2))

        @block.gpsimd
        def _(pool):
            for z in zero:
                pool.memset(z, 0.0).then_inc(zeroed, 1)
            if not L1:
                pool.wait_ge(chained, 5)
                nc.gpsimd.tensor_tensor(part[:, :], len2[:, :], e.mhalf[:, 0:1].to_broadcast([P, T]), ALU.pow)\
                    .then_inc(pooled, 1)

            def fetch(r, b, n):
                if not early(r):
                    wait(pool, VP, r - 2, "m5")
                    pool.wait_ge(rows_in[b], 32 * G * n)
                    pool.nop(nofuse=True)
                for k, cols in enumerate((e.src, e.dst)):
                    nc.gpsimd.tensor_copy(idx[:, b, k, :], cols[:, bass.ds(r * G, G)]).then_inc(picked, 1)
                pool.wait_ge(picked, 2 * r + 2)
                pool.nop(nofuse=True)
                for k, table in enumerate((e.tsrc[layer], e.tdst)):
                    for g in range(G):
                        pool.indirect_dma_start(row[:, b, k, g, :], None, table,
                                                bass.IndirectOffsetOnAxis(ap=idx[:, b, k, g:g + 1], axis=0))\
                            .then_inc(rows_in[b], 16)

            def power(r, b, n):
                for k in (1, 2):
                    wait(pool, VN, r, f"ve{k}")
                    nc.gpsimd.tensor_tensor(rs[:, :], ve[:, :], e.mhalf[:, 0:G], ALU.pow).then_inc(KN.sem, 1)

            rounds(pool, [(fetch, 0)] + ([] if L1 else [(power, 0)]), S)

        @block.tensor
        def _(pe):
            mm, tp = nc.tensor.matmul, nc.tensor.transpose
            pe.wait_ge(loadw, 16 * len(wload))
            pe.wait_ge(prepped, 1)

            def turn_x(steps, r, act_steps, act_last):
                for k in range(3):
                    if k == 0:
                        if act_last is not None:
                            wait(pe, *act_last)
                    else:
                        wait(pe, act_steps, r, f"x{k}")
                    for g in range(G):
                        if k == 0:
                            t = tp(ps_x[0:96, g * P:(g + 1) * P], x1[:, g, :], e.ident[:, :])
                        else:
                            t = tp(ps_x[:, g * P:(g + 1) * P], x23[:, g, P * (k - 1):P * k], e.ident[:, :])
                    t.then_inc(steps.sem, 1)

            def norms(r, b, n):
                pe.wait_ge(feat_in[b], 16 * (n + 1))
                if not early(r, 1):
                    wait(pe, AN, r - 1, "th2")
                for k in (1, 2):
                    if k == 2:
                        wait(pe, VN, r, "h1")
                    for g in range(G):
                        lhs = feat[:, b, g * P:(g + 1) * P] if k == 1 else h1t[:, g * P:(g + 1) * P]
                        t = mm(ps_n[:, C0 * g:C0 * (g + 1)], lhs, (w1 if k == 1 else w2)[:, :], start=True, stop=True)
                    t.then_inc(PN.sem, 1)
                    wait(pe, VN, r, f"zn{k}")
                    pe.nop(nofuse=True)
                    for g in range(G):
                        t = tp(ps_n[0:C0, P * g:P * (g + 1)], zn[:, g, :], e.ident[:, :])
                    t.then_inc(PN.sem, 1)

            def product(r, b, n):
                if L1:
                    pe.wait_ge(feat_in[b], 16 * (n + 1))
                else:
                    wait(pe, VN, r, "h2")
                if not early(r, 1):
                    wait(pe, VP, r - 1, "o0b")
                for g in range(G):
                    lhs = feat[:, b, g * P:(g + 1) * P] if L1 else h2t[:, b, g * P:(g + 1) * P]
                    t = mm(ps_w[:, g, 0:224], lhs, (w_rad if L1 else w3)[:, :], start=True, stop=True)
                t.then_inc(PP.sem, 1)
                wait(pe, VP, r, "o0b")
                turn_x(PP, r, AP_, None if early(r, 1) else (AM if L1 else AP_, r - 1, "x3"))

            def joint(r, b, n):
                wait(pe, AM, r, "sh2")
                if not early(r, 1):
                    wait(pe, VJ, r - 1, "exs")
                pe.nop(nofuse=True)
                for g in range(G):
                    t = tp(ex_p[:, g, :], es[:, g * P:(g + 1) * P], e.ident[0:32 + H, 0:32 + H])
                t.then_inc(PJ.sem, 1)
                wait(pe, VJ, r, "w")
                for k in range(2):
                    if k:
                        wait(pe, AJ, r, "lo")
                    elif not early(r, 1):
                        wait(pe, AJ, r - 1, "hi")
                    for g in range(2):
                        t = mm(ps_a[:, g, 0:MW], same[:, b, 2 * k + g], msg[:, b, 2 * k + g], start=True, stop=True)
                    t.then_inc(PJ.sem, 1)

            def out_maps(ws, wv, after_s):
                for g in range(G):
                    t = mm(out_s[:, g, :], x1t[:, g * P:(g + 1) * P] if ws is w_s else x1t[0:96, g * P:(g + 1) * P],
                           ws[:, :], start=True, stop=True)
                if after_s:
                    t.then_inc(PM.sem, 1)
                return t

            def vec_maps(wv):
                for g in range(G):
                    mm(ps_v[:, g, 0:64], x2t[:, g * P:(g + 1) * P], wv[:, 0, :], start=True, stop=True)
                    t = mm(ps_v[:, g, 64:128], x3t[:, g * P:(g + 1) * P], wv[:, 1, :], start=True, stop=True)
                return t

            def maps(r, b, n):
                wait(pe, AP_, r, "x3")
                if not early(r, 1):
                    wait(pe, VM, r - 1, "arg")
                mm(ps_l[0:C0, :], w_al[:, :], x1t[:, :], start=True, stop=True).then_inc(PM.sem, 1)
                if not early(r, 1):
                    wait(pe, VJ, r - 1, "w")
                out_maps(w_s, None, True)
                if L1:
                    if not early(r, 1):
                        wait(pe, AM, r - 1, "gh")
                    mm(ps_n[0:C0, :], w_s[:, :], x1t[:, :], start=True, stop=True).then_inc(PM.sem, 1)
                vec_maps(w_v).then_inc(PM.sem, 1)
                wait(pe, VM, r, "soft")
                pe.nop(nofuse=True)
                mm(ps_l[0:H, :], w_ad[:, :], bend[:, :], start=True, stop=True).then_inc(PM.sem, 1)
                if L1:
                    wait(pe, AM, r, "vt")
                    pe.nop(nofuse=True)
                    for g in range(G):
                        t = mm(ps_n[:, C1 * g:C1 * (g + 1)], vt[:, g * P:(g + 1) * P], w_g[:, :], start=True, stop=True)
                    t.then_inc(PM.sem, 1)
                    wait(pe, VM, r, "o0b")
                    turn_x(PM, r, AM, (AP_, r, "x3"))
                    wait(pe, AM, r, "x3")
                    out_maps(w_s2, None, False)
                    vec_maps(w_v2).then_inc(PM.sem, 1)

            rounds(pe, [(product, 0), (joint, 1), (maps, 0)] if L1 else
                   [(norms, 0), (product, 1), (joint, 2), (maps, 1)], S)

        @block.scalar
        def _(act):
            copy, af = nc.scalar.copy, nc.scalar.activation
            act.wait_ge(prepped, 1)

            def norms(r, b, n):
                for k in (1, 2):
                    wait(act, PN, r, f"z{k}")
                    if k == 2:
                        wait(act, VN, r, "ss1")
                    elif not early(r, 1):
                        wait(act, VN, r - 1, "ss2")
                    af(sq[:, :, :].rearrange("p g c -> p (g c)"), ps_n[:, 0:256], ACT.Square).then_inc(AN.sem, 1)
                    wait(act, PN, r, f"zt{k}")
                    if k == 2:
                        wait(act, VN, r, "h1")
                    elif not early(r, 1):
                        wait(act, VN, r - 1, "h2")
                    af(hu[:, :], ps_n[0:C0, :], ACT.Identity, scale=gb[:, 2 * k - 2:2 * k - 1],
                       bias=gb[:, 2 * k - 1:2 * k]).then_inc(AN.sem, 1)
                    af(th[:, :], ps_n[0:C0, :], ACT.Tanh, scale=gbh[:, 2 * k - 2:2 * k - 1],
                       bias=gbh[:, 2 * k - 1:2 * k]).then_inc(AN.sem, 1)

            def copy_x(psteps, steps, r):
                for k, (dst, rows) in enumerate(((x1t, 96), (x2t, P), (x3t, P))):
                    wait(act, psteps, r, f"x{k + 1}")
                    copy(dst[0:rows, :], ps_x[0:rows, :]).then_inc(steps.sem, 1)

            def product(r, b, n):
                if not early(r, 1):
                    wait(act, PM, r - 1, PM.names[-1])
                copy_x(PP, AP_, r)

            def joint(r, b, n):
                wait(act, VJ, r, "exs")
                if not early(r):
                    act.wait_ge(out_sent[b], 16 * n)
                copy(out[:, b, :, MW:RW], exs[:, :, 32:32 + H]).then_inc(AJ.sem, 1)
                for k, name in enumerate(("lo", "hi")):
                    wait(act, PJ, r, name)
                    copy(out[:, b, 2 * k:2 * k + 2, 0:MW], ps_a[:, :, 0:MW]).then_inc(AJ.sem, 1)

            def maps(r, b, n):
                wait(act, PM, r, "al")
                if not early(r, 1):
                    wait(act, VM, r - 1, "soft")
                if L1:
                    af(soft[:, :], ps_l[0:C0, :], ACT.Relu).then_inc(AM.sem, 1)
                    wait(act, PM, r, "vt")
                    copy(vt[:, :], ps_n[0:C0, :]).then_inc(AM.sem, 1)
                    af(sh[:, :, :], out_s, ACT.Tanh, scale=0.5).then_inc(AM.sem, 1)
                    wait(act, PM, r, "gate")
                    af(gh[:, :, :].rearrange("p g c -> p (g c)"), ps_n[:, 0:G * C1], ACT.Tanh, scale=0.5)\
                        .then_inc(AM.sem, 1)
                    copy_x(PM, AM, r)
                else:
                    af(soft[:, :], ps_l[0:C0, :], ACT.Tanh, scale=0.5).then_inc(AM.sem, 1)
                wait(act, VM, r, "arg")
                if not early(r, 1):
                    wait(act, PJ, r - 1, "ex")
                af(es[0:H, :], arg[:, :], ACT.Exp).then_inc(AM.sem, 1)
                copy(es[32:32 + H, :], shb[:, :]).then_inc(AM.sem, 1)

            rounds(act, [(product, 0), (joint, 1), (maps, 0)] if L1 else
                   [(norms, 0), (product, 1), (joint, 2), (maps, 1)], S)

        @block.vector
        def _(dve):
            tt, ts, stt = nc.vector.tensor_tensor, nc.vector.tensor_scalar, nc.vector.scalar_tensor_tensor
            dve.wait_ge(loadw, 16 * len(wload))
            n_ch = [0]

            def link(ins):
                ins.then_inc(chained, 1)
                n_ch[0] += 1
                dve.wait_ge(chained, n_ch[0])

            if not L1:
                link(tt(len2[:, :], y3[:, :, 0], y3[:, :, 0], ALU.mult))
                link(tt(part[:, :], y3[:, :, 1], y3[:, :, 1], ALU.mult))
                link(tt(len2[:, :], len2[:, :], part[:, :], ALU.add))
                link(tt(part[:, :], y3[:, :, 2], y3[:, :, 2], ALU.mult))
                link(stt(out=len2[:, :], in0=part[:, :], scalar=1e-12, in1=len2[:, :], op0=ALU.add, op1=ALU.add))
                dve.wait_ge(pooled, 1)
                for i in range(3):
                    link(stt(out=y3[:, :, i], in0=y3[:, :, i], scalar=float(np.sqrt(3.0)), in1=part[:, :],
                             op0=ALU.mult, op1=ALU.mult))
                link(ts(w2[0:64, :], w2[0:64, :], 0.5, None, ALU.mult))
                link(ts(w3[0:64, :], w3[0:64, :], 0.5, None, ALU.mult))
                for k, w in enumerate((w1, w2)):
                    link(nc.vector.tensor_reduce(mean[:, k:k + 1], w[:, :], AX.X, ALU.add))
                    link(ts(mean[:, k:k + 1], mean[:, k:k + 1], 1.0 / C0, None, ALU.mult))
                    link(ts(w[:, :], w[:, :], mean[:, k:k + 1], None, ALU.subtract))
                link(ts(gbh[:, :], gb[:, :], 0.5, None, ALU.mult))
                link(nc.vector.memset(h1t[64:65, :], 1.0))
                link(nc.vector.memset(h2t[64:65, :, :], 1.0))
                link(nc.vector.memset(x1t[96:97, :], 1.0))
            wr = w_rad if L1 else w3
            link(ts(wr[:, 160:192], wr[:, 160:192], r3, None, ALU.mult))
            link(ts(wr[:, 192:224], wr[:, 192:224], r2, None, ALU.mult))
            link(ts(w_ad[:, :], w_ad[:, :], 0.2 if L1 else 0.4, None, ALU.mult))
            if L1:
                link(ts(w_s2[:, :], w_s2[:, :], c_s2[:, :], None, ALU.mult))
                link(ts(w_s2[64:96, :], w_s2[64:96, :], r3, None, ALU.mult))
                for k in range(2):
                    link(ts(w_v2[:, k, :], w_v2[:, k, :], c_v2[:, k, :], None, ALU.mult))
                for p0, k in ((96, 0), (32, 1), (96, 1)):
                    link(ts(w_v2[p0:p0 + 32, k, :], w_v2[p0:p0 + 32, k, :], r2, None, ALU.mult))
            nc.vector.memset(shf[:, 1, SB - 1:SB], -BIG).then_inc(prepped, 1)

            def y_of(k, n, width):
                return y5[:, :, k:k + n].unsqueeze(3).to_broadcast([P, G, n, width])

            def comps(ap):
                return ap.rearrange("p g (d c) -> p g d c", c=C1)

            def steps_of(steps):
                def done(ins):
                    ins.then_inc(steps.sem, 1)
                return done

            def norms(r, b, n):
                done = steps_of(VN)
                for k in (1, 2):
                    wait(dve, AN, r, f"sq{k}")
                    if k == 1 and not early(r, 1):
                        wait(dve, VN, r - 1, "h2")
                    done(nc.vector.tensor_reduce(ve[:, :], sq[:, :, :], AX.X, ALU.add))
                    wait(dve, VN, r, f"ss{k}")
                    done(ts(ve[:, :], ve[:, :], 1.0 / C0, EPS, ALU.mult, ALU.add))
                    wait(dve, KN, r, f"rs{k}")
                    if k == 1 and not early(r, 1):
                        wait(dve, PN, r - 1, "zt2")
                    done(tt(zn[:, :, :], ps_n[:, 0:256].rearrange("p (g c) -> p g c", g=G),
                            rs[:, :].unsqueeze(2).to_broadcast([P, G, C0]), ALU.mult))
                    wait(dve, AN, r, f"th{k}")
                    if k == 2 and not early(r):
                        wait(dve, PP, r - 2, "w")
                    done(stt(out=h1t[0:C0, :] if k == 1 else h2t[0:C0, b], in0=th[:, :], scalar=1.0, in1=hu[:, :],
                             op0=ALU.add, op1=ALU.mult))

            def product(r, b, n):
                done = steps_of(VP)
                dve.wait_ge(rows_in[b], 32 * G * (n + 1))
                if not early(r, 1):
                    wait(dve, VM, r - 1, "arg")
                    wait(dve, PM if L1 else PP, r - 1, "x3")
                done(tt(m[:, :, 0:W], row[:, b, 0], row[:, b, 1], ALU.add))
                done(tt(m[:, :, W:W + 64], row[:, b, 0, :, 64:128], row[:, b, 1, :, 64:128], ALU.add))
                yr = e.ea4[:, bass.ds(r * G, G), 1:4] if L1 else y3[:, bass.ds(r * G, G), :]
                yr2 = e.ea4[:, bass.ds(r * G, G), 1:3] if L1 else y3[:, bass.ds(r * G, G), 0:2]
                done(nc.vector.tensor_copy(y5[:, :, 0:3], yr))
                done(nc.vector.tensor_copy(y5[:, :, 3:5], yr2))
                wait(dve, PP, r, "w")
                if L1:
                    done(tt(wy[:, :, :], ps_w[:, :, 0:96],
                            e.ea4[:, bass.ds(r * G, G), 0:1].to_broadcast([P, G, 96]), ALU.mult))
                wait(dve, VP, r, "y5b")
                v = comps(m[:, :, 64:224])
                done(tt(dot[:, :, :, :], v[:, :, 0:3], y_of(0, 3, C1), ALU.mult))
                done(tt(t1[:, :, :, :], v[:, :, 1:4], y_of(2, 3, C1), ALU.mult))
                done(tt(t2[:, :, :, :], v[:, :, 2:5], y_of(1, 3, C1), ALU.mult))
                if L1:
                    wait(dve, VP, r, "wy")
                ws = wy if L1 else ps_w
                done(tt(x1[:, :, 0:C0], m[:, :, 0:C0], ws[:, :, 0:C0], ALU.mult))
                done(tt(x23[:, :, 0:C0], m[:, :, 0:C0], ps_w[:, :, 96:160], ALU.mult))
                done(tt(x23v(0), v[:, :, 0:3], ws[:, :, 64:96].unsqueeze(2).to_broadcast([P, G, 3, C1]), ALU.mult))
                tail(done, VP, r, ps_w[:, :, 192:224].unsqueeze(2).to_broadcast([P, G, 3, C1]), ps_w[:, :, 160:192])

            def x23v(k):
                return x23[:, :, 64:256].rearrange("p g (d k c) -> p g d k c", d=3, k=2)[:, :, :, k, :]

            def tail(done, steps, r, w_cross, w_dot):
                wait(dve, steps, r, "dot")
                done(tt(dot[:, :, 0, :], dot[:, :, 0, :], dot[:, :, 1, :], ALU.add))
                wait(dve, steps, r, "t2")
                done(tt(x23v(1) if w_cross is None else t1[:, :, :, :], t1[:, :, :, :], t2[:, :, :, :], ALU.subtract))
                wait(dve, steps, r, "dot1")
                done(tt(dot[:, :, 0, :] if w_dot is not None else x1[:, :, 64:96], dot[:, :, 0, :], dot[:, :, 2, :],
                        ALU.add))
                wait(dve, steps, r, "t12")
                if w_cross is not None:
                    done(tt(x23v(1), t1[:, :, :, :], w_cross, ALU.mult))
                    wait(dve, steps, r, "dot2")
                    done(tt(x1[:, :, 64:96], dot[:, :, 0, :], w_dot, ALU.mult))

            def vec_out(done, steps, r, to, y):
                done(tt(to[:, :, :, :], ps_v[:, :, 0:32].unsqueeze(2).to_broadcast([P, G, 3, C1]), y, ALU.mult))
                wait(dve, steps, r, "zy")
                done(tt(to[:, :, :, :], to[:, :, :, :], comps(ps_v[:, :, 32:128]), ALU.add))
                wait(dve, steps, r, "bc")

            def joint(r, b, n):
                done = steps_of(VJ)
                dve.wait_ge(dst_in[b], 16 * (n + 1))
                if not early(r):
                    wait(dve, PJ, r - 2, "hi")
                done(dst_same(nc, dve, e, same, dst_b, r, b))
                wait(dve, PJ, r, "ex")
                if not early(r, 1):
                    wait(dve, AJ, r - 1, "shift")
                    wait(dve, VJ, r - 1, "w")
                done(nc.vector.tensor_copy(exs[:, :, :], ex_p))
                wait(dve, VJ, r, "exs")
                exb = exs[:, :, 0:H]
                done(nc.vector.tensor_copy(exv[:, :, :].rearrange("p g (h k) -> p g h k", h=H),
                                           exb.unsqueeze(3).to_broadcast([P, G, H, per_v])))
                done(tt(msg[:, b, :, 0:C0].rearrange("p g (h k) -> p g h k", h=H),
                        out_s.rearrange("p g (h k) -> p g h k", h=H),
                        exb.unsqueeze(3).to_broadcast([P, G, H, per_s]), ALU.mult))
                src = e.ea4[:, bass.ds(r * G, G), 1:4] if L1 else y3[:, bass.ds(r * G, G), :]
                vec_out(done, VJ, r, t3, src.unsqueeze(3).to_broadcast([P, G, 3, C1]))
                done(tt(comps(msg[:, b, :, C0:W]), t3[:, :, :, :],
                        exv[:, :, :].unsqueeze(2).to_broadcast([P, G, 3, C1]), ALU.mult))
                done(nc.vector.tensor_copy(msg[:, b, :, W:MW], exb))

            def maps(r, b, n):
                done = steps_of(VM)
                wait(dve, AM, r, "bend")
                if not early(r, 1):
                    wait(dve, PM, r - 1, "at")
                if L1:
                    done(stt(out=bend[:, :], in0=soft[:, :], scalar=4.0, in1=ps_l[0:C0, :], op0=ALU.mult, op1=ALU.add))
                    wait(dve, PM, r, "v")
                    wait(dve, VP, r, "o0b")
                    vec_out(done, VM, r, t1, y_of(0, 3, C1))
                    wait(dve, AM, r, "gh")
                    done(ts(gate[:, :, :], gh[:, :, :], 0.5, 0.5, ALU.mult, ALU.add))
                    wait(dve, PP, r, "x3")
                    done(ts(x23[:, :, 0:C0], sh[:, :, :], 0.5, 0.5, ALU.mult, ALU.add))
                    wait(dve, VM, r, "gate")
                    gb_ = gate[:, :, :].unsqueeze(2)
                    done(tt(v5[:, :, 0:3, :], t1[:, :, :, :], gb_.to_broadcast([P, G, 3, C1]), ALU.mult))
                    done(tt(v5[:, :, 3:5, :], t1[:, :, 0:2, :], gb_.to_broadcast([P, G, 2, C1]), ALU.mult))
                    wait(dve, VM, r, "v5b")
                    y0 = e.ea4[:, bass.ds(r * G, G), 0:1]
                    done(tt(dot[:, :, :, :], v5[:, :, 0:3], y_of(0, 3, C1), ALU.mult))
                    done(tt(t1[:, :, :, :], v5[:, :, 1:4], y_of(2, 3, C1), ALU.mult))
                    done(tt(t2[:, :, :, :], v5[:, :, 2:5], y_of(1, 3, C1), ALU.mult))
                    done(tt(x1[:, :, 0:C0], x23[:, :, 0:C0], y0.to_broadcast([P, G, C0]), ALU.mult))
                    done(tt(x23v(0), v5[:, :, 0:3], y0.unsqueeze(3).to_broadcast([P, G, 3, C1]), ALU.mult))
                    wait(dve, VM, r, "dot")
                    done(tt(dot[:, :, 0, :], dot[:, :, 0, :], dot[:, :, 1, :], ALU.add))
                    wait(dve, VM, r, "t2")
                    done(tt(x23v(1), t1[:, :, :, :], t2[:, :, :, :], ALU.subtract))
                    wait(dve, VM, r, "dot1")
                    done(tt(x1[:, :, 64:96], dot[:, :, 0, :], dot[:, :, 2, :], ALU.add))
                else:
                    done(stt(out=bend[:, :], in0=soft[:, :], scalar=1.5, in1=ps_l[0:C0, :], op0=ALU.add, op1=ALU.mult))
                wait(dve, PM, r, "at")
                dve.wait_ge(pen_in[b], 16 * (n + 1))
                done(nc.vector.tensor_tensor_scan(shf[:, b, :], pen[:, b, 0:SB], ps_l[0:H, :],
                                                  shf[:, 1 - b, SB - 1:SB], ALU.min, ALU.max))
                wait(dve, VM, r, "fwd")
                if not early(r, 1):
                    wait(dve, AM, r - 1, "sh2")
                done(nc.vector.tensor_tensor_scan(shb[:, ::-1], pen[:, b, SB:0:-1], shf[:, b, ::-1],
                                                  -BIG, ALU.min, ALU.max))
                wait(dve, VM, r, "bwd")
                done(tt(arg[:, :], ps_l[0:H, :], shb[:, :], ALU.subtract))

            rounds(dve, [(product, 0), (joint, 1), (maps, 0)] if L1 else
                   [(norms, 0), (product, 1), (joint, 2), (maps, 1)], S)


def block_loads(big, cols, ws, wv):
    c = cols
    return [(big[0:64, 0, c:c + 64], ws), (big[64:96, 0, c + 64:c + 96], wv),
            (big[96:128, 0, c + 96:c + 128], wv), (big[0:32, 1, c + 128:c + 160], wv)]


def col_loads(col, j, s, v):
    s, v = s.rearrange("(p a) -> p a", a=1), v.rearrange("(p a) -> p a", a=1)
    return [(col[0:64, 0, j:j + 1], s), (col[64:96, 0, j:j + 1], v), (col[96:128, 0, j:j + 1], v),
            (col[0:32, 1, j:j + 1], v)]


def node_phase(nc, e, d, layer):
    prev = layer - 1
    tag = f"node{layer}_"
    join, opens = prev >= 0, layer < LAYERS
    H = {1: 4, 3: 8}.get(prev, 0)
    per_s, per_v = {1: (16, 8), 3: (8, 4)}.get(prev, (1, 1))
    DW = 384 if prev == 0 else W + 2 * H
    inner = layer in (1, 3)
    TW = 384 if layer == 2 else W
    OW = 0 if not opens else TW + W
    ffn = prev == 3
    parts = [(i, min(HW, DW - HW * i)) for i in range(-(-DW // HW))]
    nfetch = len(parts) + 1
    with ExitStack() as loc:
        def tmp(name, shape, dt=F32):
            return loc.enter_context(nc.sbuf_tensor(tag + name, shape, dt))

        sems = []

        def sem(name):
            sems.append(loc.enter_context(nc.semaphore(tag + name)))
            return sems[-1]

        def ps(name, shape):
            return loc.enter_context(nc.psum_tensor(tag + name, shape, F32))

        loadw, zeroed, prepped, biased, ready = (sem("weights_loaded"), sem("weights_zeroed"), sem("weights_ready"),
                                                 sem("bias_rows"), sem("bias_ready"))
        wload, wprep, wbias = [], [], []
        nz = 0
        if join:
            idx = tmp("idx", [P, 2, 2], I32)
            r_last = tmp("r_last", [P, 2, DW])
            r_carry = tmp("r_carry", [P, 2, DW])
            tot = tmp("tot", [P, DW])
            tot_t = tmp("tot_t", [P, 512])
            ps_t = ps("ps_t", [P, 512])
            ps_j = ps("ps_j", [P, 512])
            fj = tmp("fj", [P, 8])
            den = tmp("den", [P, 8])
            if prev == 0:
                wj = tmp("w_join", [96, 96])
            else:
                wj = tmp("w_join", [P, 2, W])
            if ffn:
                hrow = tmp("hrow", [P, 2, W])
                xp = tmp("xp", [P, W])
                st2 = tmp("st2", [P, 6])
                mv2 = tmp("mv2", [P, 2])
                ve2 = tmp("ve2", [P, 2])
                rs2 = tmp("rs2", [P, 2])
                sq2 = tmp("sq2", [P, 96])
                n2 = tmp("n2", [P, W])
                n2_t = tmp("n2_t", [P, 256])
                wf1 = tmp("w_f1", [P, 2, 384])
                bf1 = tmp("b_f1", [1, 384])
                bfj = tmp("b_j", [1, W])
                bf2 = tmp("b_f2", [1, W])
                wf2s = tmp("w_f2s", [P, 64])
                wf2v = tmp("w_f2v", [P, 2, 64])
                gcol2 = tmp("gcol2", [P, 2, 2])
                f1 = tmp("f1", [P, 384])
                th = tmp("th", [P, 192])
                f1_t = tmp("f1_t", [P, 3, P])
                ps_f = ps("ps_f", [P, 512])
                ps_g = ps("ps_g", [P, 512])
                oo = tmp("oo", [P, 2, W])
        if opens:
            st = tmp("st", [P, 6])
            mv = tmp("mv", [P, 2])
            ve = tmp("ve", [P, 1])
            rs = tmp("rs", [P, 1])
            h = tmp("h", [P, 2, W])
            h_t = tmp("h_t", [P, 2, 2 * P])
            tab = tmp("tab", [P, 2, OW])
            wo = tmp("w_open", [P, 2, OW])
            ps_h = ps("ps_h", [P, 512])
            ps_o = ps("ps_o", [P, 2, 512])
            if inner:
                sti = tmp("sti", [P, 6])
                mvi = tmp("mvi", [P, 2])
                vei = tmp("vei", [P, 2])
                rsi = tmp("rsi", [P, 2])
                sqi = tmp("sqi", [P, 96])
                hn = tmp("hn", [P, W])
                gcol = tmp("gcol", [P, 2, 2])
                brow = tmp("brow", [1, 2 * W])
        if join:
            J = Steps(sem("vec_join"),
                      {0: ["tot", "y", "x"], 2: ["tot", "x"]}.get(prev, None) or
                      ["d", "dm", "cs", "cv", "cd", "tot", "den", "rden", "ns", "nv"] +
                      (["x"] if not ffn else
                       ["xp", "st", "mv", "ve", "sq", "s", "v", "f1", "th", "sc", "fv", "o1", "oo"]))
            PJ = Steps(sem("pe_join"), ["t", "j"] + (["t2", "f1", "t3", "f2"] if ffn else []))
            AJ = Steps(sem("act_join"), (["exp"] if H else []) + ["t"] + (["t2", "tanh", "t3"] if ffn else []))
            KJ = Steps(sem("pool_join"), ["idx", "idx2"] + (["rs"] if ffn else []))
            joined_in = [e.pool_dma_sem(tag + f"joined_in{b}") for b in range(2)]
            h_in = [sem(f"h_in{b}") for b in range(2)]
            oo_sent = [sem(f"oo_sent{b}") for b in range(2)]
        if opens:
            O = Steps(sem("vec_open"), ["st", "mv", "ve", "c", "h"] +
                      (["sti", "mvi", "vei", "sq", "ns", "nv"] if inner else []) + ["tab", "x"])
            PO = Steps(sem("pe_open"), ["t", "o"])
            AO = Steps(sem("act_open"), ["t1", "t2"])
            KO = Steps(sem("pool_open"), ["rs"] + (["rsi"] if inner else []))
            tab_sent = [sem(f"tab_sent{b}") for b in range(2)]
            h_sent = [sem(f"h_sent{b}") for b in range(2)]
            ntab = {0: 1, 1: 2, 2: 1, 3: 2}[layer]

        zero = []
        c3 = lambda ap: ap.rearrange("(a b) -> a b", a=1)
        if join and prev == 0:
            wload += [(wj[0:64, 0:64], d["L0_gnn_W_l2_00"]), (wj[64:96, 0:64], d["L0_gnn_W_l2_10"]),
                      (wj[0:64, 64:96], d["L0_gnn_W_l2_01"]), (wj[64:96, 64:96], d["L0_gnn_W_l2_11"])]
            k0 = 0.25 * 0.5 / float(np.sqrt(96.0))
            wprep += [(wj[:, :], k0), (wj[64:96, 0:64], 1.0 / float(np.sqrt(3.0)))]
        elif join:
            zero += [wj[:, :, :]]
            if prev == 1:
                wload += block_loads(wj, 0, d["L1_gnn_Wps"], d["L1_gnn_Wpv"])
            elif prev == 2:
                wload += block_loads(wj, 0, d["L2_gnn_L_s"], d["L2_gnn_L_v"])
                wprep += [(wj[:, :, 0:64], 0.125), (wj[:, :, 64:160], 1.0 / float(np.sqrt(32.0)))]
            else:
                wload += block_loads(wj, 0, d["L3_gnn_proj_ws"], d["L3_gnn_proj_wv"])
                zero += [wf1[:, :, :], bf1[:, :], bfj[:, :], bf2[:, :], wf2v[:, :, :]]
                f1v, f2v = d["L3_gnn_f1_wv"], d["L3_gnn_f2_wv"]
                wload += [(wf1[0:64, 0, 0:192], d["L3_gnn_f1_ws"]), (wf1[64:96, 0, 192:256], f1v),
                          (wf1[96:128, 0, 256:320], f1v), (wf1[0:32, 1, 320:384], f1v),
                          (bf1[:, 0:192], c3(d["L3_gnn_f1_bs"])), (bfj[:, 0:64], c3(d["L3_gnn_proj_bs"])),
                          (bf2[:, 0:64], c3(d["L3_gnn_f2_bs"])), (wf2s[:, :], d["L3_gnn_f2_ws"]),
                          (wf2v[0:64, 0, 0:32], f2v), (wf2v[64:128, 0, 32:64], f2v), (wf2v[0:64, 1, 0:32], f2v)]
                wload += col_loads(gcol2, 0, d["L3_gnn_ln2_w0"], d["L3_gnn_ln2_w1"])
                zero += [gcol2[:, :, :]]
                wload += [(gcol2[0:64, 0, 1:2], d["L3_gnn_ln2_b0"].rearrange("(p a) -> p a", a=1))]
                wbias += [(gcol2, wf1, bf1, 384)]
        if opens:
            zero += [wo[:, :, :]]
            if layer == 0:
                wload += block_loads(wo, 0, d["L0_gnn_W_l1_0"], d["L0_gnn_W_l1_1"])
                wload += block_loads(wo, W, d["L0_gnn_W_si0"], d["L0_gnn_W_si1"])
                for c in (0, W):
                    wprep += [(wo[:, :, c:c + 64], 0.125), (wo[:, :, c + 64:c + 160], 1.0 / float(np.sqrt(32.0)))]
            elif layer == 1:
                wload += block_loads(wo, 0, d["L1_gnn_Ws_src"], d["L1_gnn_Wv_src"])
                wload += block_loads(wo, W, d["L1_gnn_Ws_dst"], d["L1_gnn_Wv_dst"])
                wload += col_loads(gcol, 0, d["L1_gnn_gamma_s"], d["L1_gnn_gamma_v"])
                wload += [(gcol[0:64, 0, 1:2], d["L1_gnn_beta_s"].rearrange("(p a) -> p a", a=1))]
            elif layer == 2:
                vv, sv, vs = d["L2_gnn_W_vv"], d["L2_gnn_W_sv"], d["L2_gnn_W_vs"]
                rows = [(0, 64, 96), (0, 96, 128), (1, 0, 32)]
                wload += [(wo[0:64, 0, 0:64], d["L2_gnn_W_ss"]), (wo[0:64, 0, 256:288], sv)]
                for i, (k, a, b) in enumerate(rows):
                    wload += [(wo[a:b, k, 64 + 64 * i:128 + 64 * i], vv),
                              (wo[a:b, k, 288 + 32 * i:320 + 32 * i], vs)]
                wload += block_loads(wo, 384, d["L2_gnn_L_s"], d["L2_gnn_L_v"])
                i2, i3 = 1.0 / float(np.sqrt(2.0)), 1.0 / float(np.sqrt(3.0))
                r32 = 1.0 / float(np.sqrt(32.0))
                wprep += [(wo[:, :, 0:64], 0.125 * i2), (wo[:, :, 64:256], i3 * r32 * i2),
                          (wo[:, :, 256:288], i3 * 0.125 * i2), (wo[:, :, 288:384], i3 * r32 * i2),
                          (wo[:, :, 384:448], 0.125), (wo[:, :, 448:544], r32)]
            else:
                wload += block_loads(wo, 0, d["L3_gnn_msrc_ws"], d["L3_gnn_msrc_wv"])
                wload += block_loads(wo, W, d["L3_gnn_mdst_ws"], d["L3_gnn_mdst_wv"])
                wload += col_loads(gcol, 0, d["L3_gnn_ln1_w0"], d["L3_gnn_ln1_w1"])
                wload += [(gcol[0:64, 0, 1:2], d["L3_gnn_ln1_b0"].rearrange("(p a) -> p a", a=1)),
                          (brow[:, W:W + 64], c3(d["L3_gnn_mdst_bs"]))]
            if inner:
                zero += [gcol[:, :, :], brow[:, :]]
                wbias += [(gcol, wo, brow, 2 * W)]
        nprep = len(wprep) + 3 * len(wbias)
        loc.callback(clear, nc, sems)
        block = loc.enter_context(nc.Block())

        @block.sync
        def _(sp):
            sp.wait_ge(zeroed, len(zero)) if zero else None
            load_blocks(sp, loadw, wload)

            def fetch_h(r, b, n):
                if not early(r):
                    wait(sp, J, r - 2, "xp")
                sp.dma_start(hrow[:, b], e.h3[bass.ds(r * P, P), :]).then_inc(h_in[b], 16)

            def store_out(r, b, n):
                wait(sp, J, r, "oo")
                sp.dma_start(d["out"][bass.ds(r * P, P), :], oo[:, b]).then_inc(oo_sent[b], 16)

            def store_tab(r, b, n):
                wait(sp, O, r, "tab")
                sp.dma_start(e.tsrc[layer][bass.ds(r * P, P), :], tab[:, b, 0:TW]).then_inc(tab_sent[b], 16)
                if inner:
                    sp.dma_start(e.tdst[bass.ds(r * P, P), :], tab[:, b, W:2 * W]).then_inc(tab_sent[b], 16)
                if layer == 3:
                    sp.dma_start(e.h3[bass.ds(r * P, P), :], h[:, b]).then_inc(h_sent[b], 16)

            if ffn:
                rounds(sp, [(fetch_h, 0), (store_out, 2)], NT)
                for b in range(2):
                    sp.wait_ge(oo_sent[b], 16 * (NT // 2))
            else:
                rounds(sp, [(store_tab, 2)], NT)
                for b in range(2):
                    sp.wait_ge(tab_sent[b], 16 * ntab * (NT // 2))
                    if layer == 3:
                        sp.wait_ge(h_sent[b], 16 * (NT // 2))

        @block.gpsimd
        def _(pool):
            for z in zero:
                pool.memset(z, 0.0).then_inc(zeroed, 1)

            def fetch(r, b, n):
                if not early(r):
                    wait(pool, J, r - 2, "tot")
                    pool.wait_ge(joined_in[b], 16 * nfetch * n)
                    pool.nop(nofuse=True)
                nc.gpsimd.tensor_copy(idx[:, b, 0:1], e.last[:, bass.ds(r, 1)]).then_inc(KJ.sem, 1)
                nc.gpsimd.tensor_copy(idx[:, b, 1:2], e.carry[:, bass.ds(r, 1)]).then_inc(KJ.sem, 1)
                wait(pool, KJ, r, "idx2")
                pool.nop(nofuse=True)
                for i, w in parts:
                    pool.indirect_dma_start(r_last[:, b, HW * i:HW * i + w], None, e.rows[prev][i],
                                            bass.IndirectOffsetOnAxis(ap=idx[:, b, 0:1], axis=0))\
                        .then_inc(joined_in[b], 16)
                pool.indirect_dma_start(r_carry[:, b, :], None, e.carries[prev],
                                        bass.IndirectOffsetOnAxis(ap=idx[:, b, 1:2], axis=0))\
                        .then_inc(joined_in[b], 16)

            def power(r, b, n):
                wait(pool, O, r, "ve")
                nc.gpsimd.tensor_tensor(rs[:, :], ve[:, :], e.mhalf[:, 0:1], ALU.pow).then_inc(KO.sem, 1)
                if inner:
                    wait(pool, O, r, "sq")
                    nc.gpsimd.tensor_tensor(rsi[:, :], vei[:, :], e.mhalf[:, 0:2], ALU.pow).then_inc(KO.sem, 1)

            def power2(r, b, n):
                wait(pool, J, r, "sq")
                nc.gpsimd.tensor_tensor(rs2[:, :], ve2[:, :], e.mhalf[:, 0:2], ALU.pow).then_inc(KJ.sem, 1)

            rounds(pool, ([(fetch, 0)] if join else []) + ([(power, 1 if join else 0)] if opens else []) +
                   ([(power2, 0)] if ffn else []), NT)

        @block.tensor
        def _(pe):
            for k, (g, w, row, n) in enumerate(wbias):
                pe.wait_ge(loadw, 16 * len(wload))
                if k == 0 and wprep:
                    pe.wait_ge(prepped, len(wprep))
                t = ps_f if ffn else ps_h
                nc.tensor.matmul(t[0:1, 0:n], g[:, 0, 1:2], w[:, 0, 0:n], start=True, stop=False)
                nc.tensor.matmul(t[0:1, 0:n], g[0:32, 1, 1:2], w[0:32, 1, 0:n], start=False, stop=True)\
                    .then_inc(biased, 1)
            pe.wait_ge(prepped, nprep)

            def joins(r, b, n):
                wait(pe, J, r, "tot" if not H else "nv")
                if not early(r, 1):
                    wait(pe, AJ, r - 1, "t")
                if prev == 0:
                    for k in range(4):
                        mm = nc.tensor.transpose(ps_t[0:96, k * P:(k + 1) * P], tot[:, 96 * k:96 * k + 96],
                                                 e.ident[:, :])
                else:
                    nc.tensor.transpose(ps_t[:, 0:P], tot[:, 0:P], e.ident[:, :])
                    mm = nc.tensor.transpose(ps_t[0:32, P:2 * P], tot[:, P:W], e.ident[:, :])
                mm.then_inc(PJ.sem, 1)
                wait(pe, AJ, r, "t")
                if not early(r, 1):
                    wait(pe, J, r - 1, "xp" if ffn else "x" if prev else "y")
                if prev == 0:
                    for k in range(4):
                        o = ps_j[:, 0:64] if k == 0 else ps_j[:, 32 + 32 * k:64 + 32 * k]
                        mm = nc.tensor.matmul(o, tot_t[0:96, k * P:(k + 1) * P],
                                              wj[:, 0:64] if k == 0 else wj[:, 64:96], start=True, stop=True)
                else:
                    nc.tensor.matmul(ps_j[:, 0:W], tot_t[:, 0:P], wj[:, 0, :], start=True, stop=False)
                    mm = nc.tensor.matmul(ps_j[:, 0:W], tot_t[0:32, P:2 * P], wj[0:32, 1, :], start=False,
                                          stop=not ffn)
                    if ffn:
                        mm = nc.tensor.matmul(ps_j[:, 0:W], e.ones[0:1, :], bfj[:, :], start=False, stop=True)
                mm.then_inc(PJ.sem, 1)
                if ffn:
                    wait(pe, J, r, "v")
                    nc.tensor.transpose(ps_t[:, 0:P], n2[:, 0:P], e.ident[:, :])
                    nc.tensor.transpose(ps_t[0:32, P:2 * P], n2[:, P:W], e.ident[:, :]).then_inc(PJ.sem, 1)
                    wait(pe, AJ, r, "t2")
                    nc.tensor.matmul(ps_f[:, 0:384], n2_t[:, 0:P], wf1[:, 0, :], start=True, stop=False)
                    nc.tensor.matmul(ps_f[:, 0:384], n2_t[0:32, P:2 * P], wf1[0:32, 1, :], start=False, stop=False)
                    nc.tensor.matmul(ps_f[:, 0:384], e.ones[0:1, :], bf1[:, :], start=False, stop=True)\
                        .then_inc(PJ.sem, 1)
                    wait(pe, J, r, "fv")
                    nc.tensor.transpose(ps_t[:, 0:P], f1[:, 0:P], e.ident[:, :])
                    nc.tensor.transpose(ps_t[:, P:2 * P], f1[:, 192:320], e.ident[:, :])
                    nc.tensor.transpose(ps_t[0:64, 2 * P:3 * P], f1[:, 320:384], e.ident[:, :]).then_inc(PJ.sem, 1)
                    wait(pe, AJ, r, "t3")
                    nc.tensor.matmul(ps_g[:, 0:64], f1_t[:, 0, :], wf2s[:, :], start=True, stop=False)
                    nc.tensor.matmul(ps_g[:, 0:64], e.ones[0:1, :], bf2[:, 0:64], start=False, stop=True)
                    nc.tensor.matmul(ps_g[:, 64:128], f1_t[:, 1, :], wf2v[:, 0, :], start=True, stop=True)
                    nc.tensor.matmul(ps_g[:, 128:160], f1_t[0:64, 2, :], wf2v[0:64, 1, 0:32], start=True, stop=True)\
                        .then_inc(PJ.sem, 1)

            def opening(r, b, n):
                wait(pe, O, r, "nv" if inner else "h")
                src = hn[:, :] if inner else h[:, b]
                if not early(r, 1):
                    wait(pe, AO, r - 1, "t2")
                nc.tensor.transpose(ps_h[:, 0:P], src[:, 0:P], e.ident[:, :])
                nc.tensor.transpose(ps_h[0:32, P:2 * P], src[:, P:W], e.ident[:, :]).then_inc(PO.sem, 1)
                wait(pe, AO, r, "t2")
                if not early(r, 1):
                    wait(pe, O, r - 1, "x")
                for o, c0, cw in ((0, 0, TW), (1, TW, W)):
                    nc.tensor.matmul(ps_o[:, o, 0:cw], h_t[:, b, 0:P], wo[:, 0, c0:c0 + cw], start=True, stop=False)
                    mm = nc.tensor.matmul(ps_o[:, o, 0:cw], h_t[0:32, b, P:2 * P], wo[0:32, 1, c0:c0 + cw],
                                          start=False, stop=not inner)
                    if inner:
                        mm = nc.tensor.matmul(ps_o[:, o, 0:cw], e.ones[0:1, :], brow[:, c0:c0 + cw],
                                              start=False, stop=True)
                mm.then_inc(PO.sem, 1)

            rounds(pe, ([(joins, 0)] if join else []) + ([(opening, 1 if join else 0)] if opens else []), NT)

        @block.scalar
        def _(act):
            def joins(r, b, n):
                if H:
                    wait(act, J, r, "dm")
                    nc.scalar.activation(fj[:, 0:H], fj[:, 0:H], ACT.Exp).then_inc(AJ.sem, 1)
                wait(act, PJ, r, "t")
                if not early(r, 1):
                    wait(act, PJ, r - 1, "j")
                if prev == 0:
                    nc.scalar.copy(tot_t[0:96, :], ps_t[0:96, :]).then_inc(AJ.sem, 1)
                else:
                    nc.scalar.copy(tot_t[:, 0:P], ps_t[:, 0:P]).then_inc(ready, 1)
                    nc.scalar.copy(tot_t[0:32, P:2 * P], ps_t[0:32, P:2 * P]).then_inc(AJ.sem, 1)
                if ffn:
                    wait(act, PJ, r, "t2")
                    nc.scalar.copy(n2_t[:, 0:P], ps_t[:, 0:P]).then_inc(ready, 1)
                    nc.scalar.copy(n2_t[0:32, P:2 * P], ps_t[0:32, P:2 * P]).then_inc(AJ.sem, 1)
                    wait(act, J, r, "f1")
                    nc.scalar.activation(th[:, :], f1[:, 0:192], ACT.Tanh, scale=0.5).then_inc(AJ.sem, 1)
                    wait(act, PJ, r, "t3")
                    nc.scalar.copy(f1_t[:, 0:2, :], ps_t[:, 0:2 * P].rearrange("p (a b) -> p a b", a=2))\
                        .then_inc(ready, 1)
                    nc.scalar.copy(f1_t[0:64, 2, :], ps_t[0:64, 2 * P:3 * P]).then_inc(AJ.sem, 1)

            def opening(r, b, n):
                wait(act, PO, r, "t")
                if not early(r):
                    wait(act, PO, r - 2, "o")
                nc.scalar.copy(h_t[:, b, 0:P], ps_h[:, 0:P]).then_inc(AO.sem, 1)
                nc.scalar.copy(h_t[0:32, b, P:2 * P], ps_h[0:32, P:2 * P]).then_inc(AO.sem, 1)

            rounds(act, ([(joins, 0)] if join else []) + ([(opening, 1 if join else 0)] if opens else []), NT)

        @block.vector
        def _(dve):
            tt, ts = nc.vector.tensor_tensor, nc.vector.tensor_scalar
            dve.wait_ge(loadw, 16 * len(wload))
            for k, (ap, c) in enumerate(wprep):
                dve.wait_ge(prepped, k) if k else None
                ts(ap, ap, c, None, ALU.mult).then_inc(prepped, 1)
            m = len(wprep)
            for k, (g, w, row, n) in enumerate(wbias):
                dve.wait_ge(biased, k + 1)
                t = ps_f if ffn else ps_h
                tt(row[0:1, 0:n], row[0:1, 0:n], t[0:1, 0:n], ALU.add).then_inc(prepped, 1)
                ts(w[:, 0, 0:n], w[:, 0, 0:n], g[:, 0, 0:1], None, ALU.mult).then_inc(prepped, 1)
                ts(w[0:32, 1, 0:n], w[0:32, 1, 0:n], g[0:32, 1, 0:1], None, ALU.mult).then_inc(prepped, 1)
                m += 3

            def xs(r):
                return e.x[:, bass.ds(r, 1), :].rearrange("p a w -> p (a w)")

            def attr(r, n):
                return e.attr[:, bass.ds(r, 1)].to_broadcast([P, n])

            def heads(ap, f):
                return ((ap[:, 0:C0].rearrange("p (h k) -> p h k", h=H),
                         f[:, 0:H].unsqueeze(2).to_broadcast([P, H, per_s])),
                        (ap[:, C0:W].rearrange("p (c h k) -> p c h k", c=3, h=H),
                         f[:, 0:H].unsqueeze(1).unsqueeze(3).to_broadcast([P, 3, H, per_v])))

            def joins(r, b, n):
                def done(ins):
                    ins.then_inc(J.sem, 1)

                dve.wait_ge(joined_in[b], 16 * nfetch * (n + 1))
                if not early(r, 1):
                    wait(dve, J, r - 1, J.names[-1])
                D, C = r_last[:, b], r_carry[:, b]
                if not early(r, 1):
                    wait(dve, PJ, r - 1, "t")
                if H:
                    done(tt(fj[:, 0:H], C[:, W + H:W + 2 * H], D[:, W + H:W + 2 * H], ALU.subtract))
                    wait(dve, J, r, "d")
                    done(ts(fj[:, 0:H], fj[:, 0:H], 0.0, None, ALU.min))
                    wait(dve, AJ, r, "exp")
                    for v, f in heads(C, fj):
                        done(tt(v, v, f, ALU.mult))
                    done(tt(C[:, W:W + H], C[:, W:W + H], fj[:, 0:H], ALU.mult))
                    wait(dve, J, r, "cd")
                    done(tt(tot[:, 0:W + H], D[:, 0:W + H], C[:, 0:W + H], ALU.add))
                    wait(dve, J, r, "tot")
                    done(ts(den[:, 0:H], tot[:, W:W + H], 1e-16 if prev == 1 else 1e-12, None, ALU.add))
                    wait(dve, J, r, "den")
                    done(nc.vector.reciprocal(den[:, 0:H], den[:, 0:H]))
                    wait(dve, J, r, "rden")
                    for v, f in heads(tot, den):
                        done(tt(v, v, f, ALU.mult))
                else:
                    done(tt(tot[:, :], D, C, ALU.add))
                wait(dve, PJ, r, "j")
                if prev == 0:
                    done(tt(tot[:, 0:W], ps_j[:, 0:W], attr(r, W), ALU.mult))
                    wait(dve, J, r, "y")
                    done(tt(xs(r), xs(r), tot[:, 0:W], ALU.add))
                elif not ffn:
                    done(tt(xs(r), xs(r), ps_j[:, 0:W], ALU.add))
                else:
                    dve.wait_ge(h_in[b], 16 * (n + 1))
                    done(tt(xp[:, :], hrow[:, b], ps_j[:, 0:W], ALU.add))
                    wait(dve, J, r, "xp")
                    done(nc.vector.bn_stats(st2[:, :], xp[:, 0:C0]))
                    wait(dve, J, r, "st")
                    dve.nop(nofuse=True)
                    done(nc.vector.bn_aggr(mv2[:, :], st2[:, :]))
                    wait(dve, J, r, "mv")
                    done(ts(ve2[:, 0:1], mv2[:, 1:2], EPS, None, ALU.add))
                    done(nc.vector.tensor_tensor_reduce(out=sq2[:, :], in0=xp[:, C0:W], in1=xp[:, C0:W],
                                                        scale=1.0 / 96, scalar=EPS, op0=ALU.mult, op1=ALU.add,
                                                        accum_out=ve2[:, 1:2]))
                    wait(dve, KJ, r, "rs")
                    done(ts(n2[:, 0:C0], xp[:, 0:C0], mv2[:, 0:1], rs2[:, 0:1], ALU.subtract, ALU.mult))
                    done(ts(n2[:, C0:W], xp[:, C0:W], rs2[:, 1:2], None, ALU.mult))
                    wait(dve, PJ, r, "f1")
                    done(tt(f1[:, :], ps_f[:, 0:384], attr(r, 384), ALU.mult))
                    wait(dve, AJ, r, "tanh")
                    done(ts(th[:, :], th[:, :], 0.5, 0.5, ALU.mult, ALU.add))
                    wait(dve, J, r, "th")
                    done(tt(f1[:, 0:128], f1[:, 0:128], th[:, 0:128], ALU.mult))
                    fv = f1[:, 192:384].rearrange("p (c k) -> p c k", c=3)
                    done(tt(fv, fv, th[:, 128:192].unsqueeze(1).to_broadcast([P, 3, 64]), ALU.mult))
                    wait(dve, PJ, r, "f2")
                    if not early(r):
                        dve.wait_ge(oo_sent[b], 16 * n)
                    done(tt(oo[:, b], ps_g[:, 0:W], attr(r, W), ALU.mult))
                    dve.wait_ge(J.sem, J.at(r, "o1"))
                    tt(oo[:, b], oo[:, b], xp[:, :], ALU.add).then_inc(zeroed, 1)
                    dve.wait_ge(zeroed, len(zero) + r + 1)
                    done(tt(oo[:, b], oo[:, b], xs(r), ALU.add))

            def opening(r, b, n):
                def done(ins):
                    ins.then_inc(O.sem, 1)

                if join:
                    wait(dve, J, r, J.names[-1])
                if not early(r, 1):
                    wait(dve, O, r - 1, O.names[-1])
                dve.nop(nofuse=True)
                done(nc.vector.bn_stats(st[:, :], xs(r)))
                wait(dve, O, r, "st")
                dve.nop(nofuse=True)
                done(nc.vector.bn_aggr(mv[:, :], st[:, :]))
                wait(dve, O, r, "mv")
                done(ts(ve[:, :], mv[:, 1:2], EPS, None, ALU.add))
                wait(dve, KO, r, "rs")
                if not early(r):
                    wait(dve, PO, r - 2, "t")
                    if layer == 3:
                        dve.wait_ge(h_sent[b], 16 * n)
                done(ts(h[:, b], xs(r), mv[:, 0:1], rs[:, 0:1], ALU.subtract, ALU.mult))
                wait(dve, O, r, "c")
                done(ts(h[:, b], h[:, b], 0.0, None, ALU.max))
                if inner:
                    wait(dve, O, r, "h")
                    done(nc.vector.bn_stats(sti[:, :], h[:, b, 0:C0]))
                    wait(dve, O, r, "sti")
                    dve.nop(nofuse=True)
                    done(nc.vector.bn_aggr(mvi[:, :], sti[:, :]))
                    wait(dve, O, r, "mvi")
                    done(ts(vei[:, 0:1], mvi[:, 1:2], EPS, None, ALU.add))
                    done(nc.vector.tensor_tensor_reduce(out=sqi[:, :], in0=h[:, b, C0:W], in1=h[:, b, C0:W],
                                                        scale=1.0 / (32 if layer == 1 else 96), scalar=EPS,
                                                        op0=ALU.mult, op1=ALU.add, accum_out=vei[:, 1:2]))
                    wait(dve, KO, r, "rsi")
                    if not early(r, 1):
                        wait(dve, PO, r - 1, "t")
                    done(ts(hn[:, 0:C0], h[:, b, 0:C0], mvi[:, 0:1], rsi[:, 0:1], ALU.subtract, ALU.mult))
                    done(ts(hn[:, C0:W], h[:, b, C0:W], rsi[:, 1:2], None, ALU.mult))
                wait(dve, PO, r, "o")
                if not early(r):
                    dve.wait_ge(tab_sent[b], 16 * ntab * n)
                if layer == 0:
                    done(tt(tab[:, b, 0:W], ps_o[:, 0, 0:W], attr(r, W), ALU.mult))
                    tt(tab[:, b, W:2 * W], ps_o[:, 1, 0:W], attr(r, W), ALU.mult).then_inc(zeroed, 1)
                    dve.wait_ge(zeroed, len(zero) + r + 1)
                    done(tt(xs(r), xs(r), tab[:, b, W:2 * W], ALU.add))
                elif layer == 2:
                    done(nc.vector.tensor_copy(tab[:, b, 0:TW], ps_o[:, 0, 0:TW]))
                    done(tt(xs(r), xs(r), ps_o[:, 1, 0:W], ALU.add))
                else:
                    done(nc.vector.tensor_copy(tab[:, b, 0:2 * W].rearrange("p (a w) -> p a w", a=2),
                                               ps_o[:, :, 0:W]))
                    done(tt(xs(r), xs(r), h[:, b], ALU.add) if layer == 1 else
                         nc.vector.memset(sqi[:, 0:1], 0.0))

            rounds(dve, ([(joins, 0)] if join else []) + ([(opening, 1 if join else 0)] if opens else []), NT)


def build(nc, d):
    with ExitStack() as ctx:
        ctx.enter_context(nc.allow_non_contiguous_dma(reason="columns of a few words, read once"))
        e = setup(nc, ctx, d)
        for layer in range(LAYERS + 1):
            node_phase(nc, e, d, layer)
            if layer == LAYERS:
                break
            if layer in (0, 2):
                edge_conv(nc, e, d, layer)
                carry_phase(nc, e, layer, 384 if layer == 0 else W)
            else:
                edge_attention(nc, e, d, layer)
                H = 4 if layer == 1 else 8
                carry_phase(nc, e, layer, W + 2 * H, H, C0 // H, C1 // H)


def kernel(**inputs):
    import concourse.bacc as _bacc
    from concourse.bass_utils import run_bass_kernel_spmd as _run

    a = {k: np.asarray(v) for k, v in inputs.items()}

    def pad(v, rows, fill=0):
        out = np.full((rows,) + v.shape[1:], fill, v.dtype)
        out[:len(v)] = v
        return out

    def cols(v):
        return np.ascontiguousarray(np.swapaxes(v.reshape(T, P, *v.shape[1:]), 0, 1))

    def comp_major(v):
        tail = v[..., C0:].reshape(*v.shape[:-1], C1, 3)
        return np.concatenate([v[..., :C0], np.swapaxes(tail, -1, -2).reshape(*v.shape[:-1], 3 * C1)], -1)

    def with_ones(v):
        return np.concatenate([v, np.ones((1,) + v.shape[1:], v.dtype)], 0)

    dst = pad(a["dst"], EP, N)
    arrays = {
        "x": np.ascontiguousarray(np.swapaxes(pad(comp_major(a["x"]), NP).reshape(NT, P, W), 0, 1)),
        "attr": np.ascontiguousarray(pad(a["node_vec1"][:, 0], NP).reshape(NT, P).T),
        "src_cols": cols(pad(a["src"], EP)),
        "dst_cols": cols(dst),
        "dst_rows": dst.reshape(1, EP),
        "dst_run": np.concatenate([np.array([-1], dst.dtype), dst, np.full(EP // P, -1, dst.dtype)]),
        "ea4_cols": cols(pad(a["edge_attr_4"], EP)),
        "ea3_cols": cols(pad(a["edge_attr_3"], EP, 1)),
        "ea10_rows": np.ascontiguousarray(pad(a["edge_attr_10"], EP).T),
        "ea16_rows": with_ones(pad(a["edge_attr_16"], EP).T),
        "ea64_rows": with_ones(pad(a["edge_attr_64"], EP).T),
    }
    arrays["L2_rad"] = comp_major(np.concatenate([a["L2_gnn_W_rad"].T, a["L2_gnn_b_rad"][None]]))
    for k, v in a.items():
        if "_gnn_" in k:
            arrays[k] = v
    arrays = {k: np.ascontiguousarray(v) for k, v in arrays.items()}
    nc = _bacc.Bacc("TRN2", target_bir_lowering=False, num_devices=1)
    d = {k: nc.dram_tensor(f"in_{k}", v.shape, mybir.dt.from_np(v.dtype), kind="ExternalInput").ap()
         for k, v in arrays.items()}
    d["out"] = nc.dram_tensor("out_nodes", (NP, W), F32, kind="ExternalOutput").ap()
    build(nc, d)
    r = _run(nc, [{f"in_{k}": v for k, v in arrays.items()}], core_ids=[0])
    got = np.asarray(r.results[0]["out_nodes"])[:N]
    tail = np.swapaxes(got[:, C0:].reshape(N, 3, C1), 1, 2).reshape(N, 3 * C1)
    return np.concatenate([got[:, :C0], tail], 1)
```

```python
from contextlib import ExitStack

import numpy as np

import concourse.bass as bass
from concourse import mybir

F32 = mybir.dt.float32
BF16 = mybir.dt.bfloat16
I32 = mybir.dt.int32
ALU = mybir.AluOpType
ACT = mybir.ActivationFunctionType
AX = mybir.AxisListType

P = 128
N = 12500
NT = -(-N // P)
NP = NT * P
E = 200000
G = 4
SB = G * P
S = -(-E // (2 * SB)) * 2
T = S * G
EP = T * P
C0, C1 = 64, 32
W = C0 + 3 * C1
EPS = 1e-5
BIG = 1e30
LAYERS = 4

HW = 192
HEADS = (0, 4, 0, 8)
ROW_W = (384, W + 2 * 4, W, W + 2 * 8)
ZERO_ROW = EP
ZERO_CARRY = T + 1


class Steps:

    def __init__(self, sem, names):
        self.sem, self.names, self.n = sem, names, len(names)

    def at(self, r, name):
        return r * self.n + (self.names.index(name) + 1)




def wait(eng, steps, r, name):
    eng.wait_ge(steps.sem, steps.at(r, name))


def rounds(eng, stages, total):
    lag = max(l for _, l in stages)

    def turn(i, par, k):
        for fn, l in stages:
            if not isinstance(i, int) or 0 <= i - l < total:
                fn(i - l, (par - l) % 2, k + (par - l) // 2)

    head = lag + 2
    head += head % 2
    tail = total - (total - head) % 2
    for i in range(head):
        turn(i, i % 2, i // 2)
    with eng.Fori(head // 2, tail // 2) as k:
        turn(2 * k, 0, k)
        turn(2 * k + 1, 1, k)
    for i in range(tail, total + lag):
        turn(i, i % 2, i // 2)


def early(r, n=2):
    return isinstance(r, int) and r < n


class Env:
    pass


def clear(nc, sems):
    with nc.Block() as block:
        @block.gpsimd
        def _(pool):
            for s in sems:
                pool.sem_clear(s)


def load_blocks(sp, sem, pairs):
    for out, src in pairs:
        sp.dma_start(out, src).then_inc(sem, 16)
    return 16 * len(pairs)


def setup(nc, ctx, d):
    e = Env()

    def pool_dma_sem(name):
        return ctx.enter_context(nc.semaphore(name))

    e.pool_dma_sem = pool_dma_sem
    tag = "setup_"

    def sb(name, shape, dt=F32):
        return ctx.enter_context(nc.sbuf_tensor(tag + name, shape, dt))

    e.x = sb("x_nodes", [P, NT, W])
    e.src = sb("src_cols", [P, T], I32)
    e.dst = sb("dst_cols", [P, T], I32)
    e.ea4 = sb("ea4_cols", [P, T, 4])
    e.chain = sb("chain", [P, T])
    e.last = sb("last_row", [P, NT], I32)
    e.carry = sb("carry_row", [P, NT], I32)
    e.ident = sb("ident", [P, P])
    e.ones = sb("ones", [P, P])
    e.mhalf = sb("minus_half", [P, 8])
    e.attr = sb("node_attr", [P, NT])
    e.rows, e.carries, e.tsrc = [], [], []
    for layer, w in enumerate(ROW_W):
        e.rows.append([nc.dram_tensor(f"edge_rows{layer}_{i}", [EP + 1, min(w, HW)], F32, kind="Internal").ap()
                       for i in range(-(-w // HW))])
        e.carries.append(nc.dram_tensor(f"carry_rows{layer}", [T + 2, w], F32, kind="Internal").ap())
        e.tsrc.append(nc.dram_tensor(f"table_src{layer}", [NP, 384 if layer == 2 else W], F32,
                                     kind="Internal").ap())
    e.tdst = nc.dram_tensor("table_dst", [NP, W], F32, kind="Internal").ap()
    e.pens = nc.dram_tensor("resets", [EP + P], F32, kind="Internal").ap()
    e.h3 = nc.dram_tensor("h_last", [NP, W], F32, kind="Internal").ap()

    with ExitStack() as loc:
        def tmp(name, shape, dt=F32):
            return loc.enter_context(nc.sbuf_tensor(tag + name, shape, dt))

        sems = []

        def sem(name):
            sems.append(loc.enter_context(nc.semaphore(tag + name)))
            return sems[-1]

        RW = EP // P
        iota = tmp("iota", [P, P])
        hi_i = tmp("hi_i", [P, T], I32)
        hi = tmp("hi", [P, T])
        lo = tmp("lo", [P, T])
        is_lo = tmp("is_lo", [P, 2, G, P], BF16)
        is_hi = tmp("is_hi", [P, 2, G, NT], BF16)
        ends = tmp("ends", [P, T + 1], I32)
        run = tmp("run", [P, RW + 1], I32)
        pen = tmp("pen", [P, RW])
        tri = tmp("tri", [P, P])
        cnt = tmp("cnt", [P, NT])
        tot = tmp("tot", [P, NT])
        offs = tmp("offs", [P, NT + 1])
        end = tmp("end", [P, NT])
        beg = tmp("beg", [P, NT])
        has = tmp("has", [P, NT])
        w0 = tmp("w0", [P, NT])
        w1 = tmp("w1", [P, NT])
        til = tmp("til", [P, NT])
        til_i = tmp("til_i", [P, NT], I32)
        zrow = tmp("zrow", [P, 3 * P])
        counts = loc.enter_context(nc.psum_tensor("counts", [P, 512], F32))
        sums = loc.enter_context(nc.psum_tensor("sums", [P, 512], F32))
        loaded, stored = sem("loaded"), sem("stored")
        consts, ready = sem("consts"), sem("ready")
        hot, counted, summed, vec = sem("one_hots"), sem("counted"), sem("summed"), sem("vec")
        loc.callback(clear, nc, sems)
        block = loc.enter_context(nc.Block())

        @block.sync
        def _(sp):
            load_blocks(sp, loaded, [
                (e.dst[:, :], d["dst_cols"]), (e.src[:, :], d["src_cols"]),
                (ends[:, 1:T + 1], d["dst_cols"][P - 1:P, :].to_broadcast([P, T])),
                (ends[:, 0:1], d["dst_run"][0:1].rearrange("(a b) -> a b", a=1).to_broadcast([P, 1])),
                (run[:, 0:RW], d["dst_run"][0:EP].rearrange("(p f) -> p f", p=P)),
                (run[:, RW:RW + 1], d["dst_run"][RW:RW + EP].rearrange("(p f) -> p f", p=P)[:, 0:1]),
                (e.ea4[:, :, :], d["ea4_cols"]), (e.x[:, :, :], d["x"]), (e.attr[:, :], d["attr"])])
            sp.wait_ge(ready, 1)
            sp.dma_start(e.pens[0:EP].rearrange("(p f) -> p f", p=P), pen[:, :]).then_inc(stored, 16)
            sp.wait_ge(ready, 2)
            n = 2
            for rows, carries, w in zip(e.rows, e.carries, ROW_W):
                for part in rows:
                    sp.dma_start(part[EP:EP + 1, :], zrow[0:1, 0:min(w, HW)]).then_inc(stored, 16)
                    n += 1
                for k in (0, ZERO_CARRY):
                    sp.dma_start(carries[k:k + 1, :], zrow[0:1, 0:w]).then_inc(stored, 16)
                    n += 1
            sp.wait_ge(ready, 3)
            sp.dma_start(e.pens[EP:EP + P].rearrange("(a f) -> a f", a=1), tri[0:1, :]).then_inc(stored, 16)
            sp.wait_ge(stored, 16 * n)

        @block.gpsimd
        def _(pool):
            pool.iota(iota[:, :], [[1, P]], base=0, channel_multiplier=0,
                      allow_small_or_imprecise_dtypes=True).then_inc(consts, 1)
            pool.memset(e.ident[:, :], 0.0).then_inc(consts, 1)
            pool.memset(e.ones[:, :], 1.0).then_inc(consts, 1)
            pool.memset(e.mhalf[:, :], -0.5).then_inc(consts, 1)
            pool.wait_ge(consts, 4)
            pool.affine_select(out=e.ident[:, :], in_=e.ident[:, :], compare_op=ALU.not_equal, fill=1.0,
                               base=0, pattern=[[-1, P]], channel_multiplier=1).then_inc(consts, 1)
            pool.affine_select(out=tri[:, :], in_=e.ones[:, :], compare_op=ALU.is_ge, fill=0.0,
                               base=0, pattern=[[1, P]], channel_multiplier=-1).then_inc(consts, 1)

        @block.vector
        def _(dve):
            dve.wait_ge(loaded, 9 * 16)
            dve.wait_ge(consts, 6)
            nc.vector.tensor_scalar(hi_i[:, :], e.dst[:, :], 7, None, ALU.logical_shift_right).then_inc(vec, 1)
            dve.wait_ge(vec, 1)
            nc.vector.tensor_copy(hi[:, :], hi_i[:, :]).then_inc(vec, 1)
            dve.wait_ge(vec, 2)
            nc.vector.scalar_tensor_tensor(out=lo[:, :], in0=hi[:, :], scalar=-float(P), in1=e.dst[:, :],
                                           op0=ALU.mult, op1=ALU.add).then_inc(vec, 1)
            nc.vector.tensor_tensor(e.chain[:, :], ends[:, 1:T + 1], ends[:, 0:T], ALU.is_equal).then_inc(vec, 1)
            nc.vector.tensor_tensor(pen[:, :], run[:, 1:RW + 1], run[:, 0:RW], ALU.is_equal).then_inc(vec, 1)
            dve.wait_ge(vec, 5)
            nc.vector.tensor_scalar(pen[:, :], pen[:, :], 2 * BIG, -BIG, ALU.mult, ALU.add).then_inc(ready, 1)
            nc.vector.memset(zrow[:, :], 0.0).then_inc(ready, 1)

            def hots(r, b, n):
                if not early(r):
                    dve.wait_ge(counted, r - 1)
                nc.vector.tensor_tensor(is_lo[:, b], iota[:, :].unsqueeze(1).to_broadcast([P, G, P]),
                                        lo[:, bass.ds(r * G, G)].unsqueeze(2).to_broadcast([P, G, P]),
                                        ALU.is_equal).then_inc(hot, 1)
                nc.vector.tensor_tensor(is_hi[:, b], iota[:, 0:NT].unsqueeze(1).to_broadcast([P, G, NT]),
                                        hi[:, bass.ds(r * G, G)].unsqueeze(2).to_broadcast([P, G, NT]),
                                        ALU.is_equal).then_inc(hot, 1)

            rounds(dve, [(hots, 0)], S)
            dve.wait_ge(counted, S)
            nc.vector.tensor_copy(cnt[:, :], counts[:, 0:NT]).then_inc(vec, 1)
            dve.wait_ge(summed, 1)
            nc.vector.tensor_copy(tot[:, :], sums[:, 0:NT]).then_inc(vec, 1)
            nc.vector.memset(offs[:, 0:1], 0.0).then_inc(vec, 1)
            dve.wait_ge(vec, 8)
            nc.vector.tensor_tensor_scan(offs[:, 1:NT + 1], e.ones[:, 0:NT], tot[:, :], 0.0,
                                         ALU.mult, ALU.add).then_inc(vec, 1)
            dve.wait_ge(vec, 9)
            nc.vector.tensor_tensor(end[:, :], sums[:, P:P + NT], offs[:, 0:NT], ALU.add).then_inc(vec, 1)
            nc.vector.tensor_scalar(has[:, :], cnt[:, :], 0.0, None, ALU.is_gt).then_inc(vec, 1)
            dve.wait_ge(vec, 11)
            nc.vector.tensor_tensor(beg[:, :], end[:, :], cnt[:, :], ALU.subtract).then_inc(vec, 1)
            nc.vector.tensor_scalar(w0[:, :], end[:, :], float(-1 - ZERO_ROW), None, ALU.add).then_inc(vec, 1)
            dve.wait_ge(vec, 13)
            nc.vector.tensor_tensor(w0[:, :], w0[:, :], has[:, :], ALU.mult).then_inc(vec, 1)
            dve.wait_ge(vec, 14)
            nc.vector.tensor_scalar(e.last[:, :], w0[:, :], float(ZERO_ROW), None, ALU.add).then_inc(vec, 1)
            dve.wait_ge(vec, 15)
            nc.vector.tensor_scalar(til_i[:, :], e.last[:, :], 7, None, ALU.logical_shift_right).then_inc(vec, 1)
            dve.wait_ge(vec, 16)
            nc.vector.tensor_copy(til[:, :], til_i[:, :]).then_inc(vec, 1)
            dve.wait_ge(vec, 17)
            nc.vector.scalar_tensor_tensor(out=w1[:, :], in0=til[:, :], scalar=float(P), in1=beg[:, :],
                                           op0=ALU.mult, op1=ALU.is_gt).then_inc(vec, 1)
            dve.wait_ge(vec, 18)
            nc.vector.tensor_tensor(w1[:, :], w1[:, :], has[:, :], ALU.mult).then_inc(vec, 1)
            dve.wait_ge(vec, 19)
            nc.vector.scalar_tensor_tensor(out=w0[:, :], in0=til[:, :], scalar=float(-ZERO_CARRY), in1=w1[:, :],
                                           op0=ALU.add, op1=ALU.mult).then_inc(vec, 1)
            dve.wait_ge(vec, 20)
            nc.vector.tensor_scalar(e.carry[:, :], w0[:, :], float(ZERO_CARRY), None, ALU.add).then_inc(vec, 1)
            dve.wait_ge(vec, 21)
            nc.vector.memset(tri[0:1, :], -BIG).then_inc(ready, 1)

        @block.tensor
        def _(pe):
            def count(r, b, n):
                pe.wait_ge(hot, 2 * r + 2)
                for g in range(G):
                    first = isinstance(r, int) and r == 0 and g == 0
                    final = isinstance(r, int) and r == S - 1 and g == G - 1
                    mm = nc.tensor.matmul(counts[:, 0:NT], is_lo[:, b, g], is_hi[:, b, g],
                                          start=first, stop=final)
                mm.then_inc(counted, 1)

            rounds(pe, [(count, 1)], S)
            pe.wait_ge(vec, 6)
            nc.tensor.matmul(sums[:, 0:NT], e.ones[:, :], cnt[:, :], start=True, stop=True)
            nc.tensor.matmul(sums[:, P:P + NT], tri[:, :], cnt[:, :], start=True, stop=True).then_inc(summed, 1)
    return e


def carry_phase(nc, e, layer, width, heads=0, per_s=0, per_v=0):
    tag = f"carry{layer}_"
    chunks = [(c, min(P, width - c)) for c in range(0, width, P)]
    TG = -(-T // P)
    with ExitStack() as loc:
        def tmp(name, shape, dt=F32):
            return loc.enter_context(nc.sbuf_tensor(tag + name, shape, dt))

        sems = []

        def sem(name):
            sems.append(loc.enter_context(nc.semaphore(tag + name)))
            return sems[-1]

        H = heads
        scanned = width - H if H else width
        lasts = tmp("lasts", [P, TG, width])
        state = tmp("state", [P, TG, width])
        fin = tmp("feat_in", [P, T])
        fout = tmp("feat_out", [P, T])
        ps = loc.enter_context(nc.psum_tensor(tag + "ps", [P, 4, 512], F32))
        loaded, stored = sem("loaded"), sem("stored")
        turned, copied, scans, back, final = sem("turned"), sem("copied"), sem("scans"), sem("back"), sem("final")
        if H:
            shifts = tmp("shifts", [H, T + 1])
            decay = tmp("decay", [H, T])
            wide = tmp("wide", [P, T])
            expand = tmp("expand", [H, 2 * P])
            sh_in, sh_out, dec, spread, widened = (sem("shift_turned"), sem("shift_copied"), sem("decayed"),
                                                   sem("spread"), sem("widened"))
            exped, zeroed, loadw = sem("exped"), sem("zeroed"), sem("loadw")
        loc.callback(clear, nc, sems)
        block = loc.enter_context(nc.Block())
        parts = [(i, min(HW, width - HW * i)) for i in range(-(-width // HW))]
        rows = [part[0:EP, :].rearrange("(t p) w -> t p w", p=P)[:, P - 1, :] for part in e.rows[layer]]
        full = T // P
        part = T - full * P
        tiles = [(k, P if k < full else part) for k in range(TG)]
        NQ = -(-T // 512)

        @block.sync
        def _(sp):
            for k, m in tiles:
                for i, w in parts:
                    sp.dma_start(lasts[0:m, k, HW * i:HW * i + w], rows[i][k * P:k * P + m, 0:w])\
                        .then_inc(loaded, 16)
            sp.wait_ge(final, len(chunks) * TG + (1 if H else 0))
            for k, m in tiles:
                sp.dma_start(e.carries[layer][1 + k * P:1 + k * P + m, :], state[0:m, k, :]).then_inc(stored, 16)
            sp.wait_ge(stored, 16 * TG)

        if H:
            @block.gpsimd
            def _(pool):
                pool.memset(expand[:, :], 1.0).then_inc(zeroed, 1)
                n = 1
                for a, b, per in ((0, C0, per_s), *((C0 + C1 * i, C0 + C1 * i + C1, per_v) for i in range(3)),
                                  (W, W + H, 1)):
                    v = expand[:, a:b]
                    pool.wait_ge(zeroed, n)
                    pool.affine_select(out=v, in_=v, compare_op=ALU.is_ge, fill=0.0, base=0,
                                       pattern=[[1, b - a]], channel_multiplier=-per).then_inc(zeroed, 1)
                    pool.wait_ge(zeroed, n + 1)
                    pool.affine_select(out=v, in_=v, compare_op=ALU.is_ge, fill=0.0, base=per - 1,
                                       pattern=[[-1, b - a]], channel_multiplier=per).then_inc(zeroed, 1)
                    n += 2

        @block.tensor
        def _(pe):
            pe.wait_ge(loaded, 16 * TG * len(parts))
            if H:
                for k, m in tiles:
                    mm = nc.tensor.transpose(ps[0:H, k // 4, (k % 4) * P:(k % 4) * P + m],
                                             lasts[0:m, k, width - H:width], e.ident[0:m, 0:m])
                mm.then_inc(sh_in, 1)
                pe.wait_ge(sh_out, 1)
            for c, (c0, cw) in enumerate(chunks):
                if H:
                    pe.wait_ge(zeroed, 11)
                    pe.wait_ge(exped, 2)
                    cs = min(cw, scanned - c0)
                    if c:
                        pe.wait_ge(final, c * TG)
                    for q in range(NQ):
                        n = min(512, T - 512 * q)
                        mm = nc.tensor.matmul(ps[0:cs, q, 0:n], expand[:, c0:c0 + cs],
                                              decay[:, 512 * q:512 * q + n], start=True, stop=True)
                    mm.then_inc(spread, 1)
                    pe.wait_ge(widened, c + 1)
                elif c:
                    pe.wait_ge(final, c * TG)
                for k, m in tiles:
                    mm = nc.tensor.transpose(ps[0:cw, k // 4, (k % 4) * P:(k % 4) * P + m],
                                             lasts[0:m, k, c0:c0 + cw], e.ident[0:m, 0:m])
                mm.then_inc(turned, 1)
                pe.wait_ge(scans, c + 1)
                for k, m in tiles:
                    if k >= 4:
                        pe.wait_ge(final, c * TG + k - 3)
                    else:
                        pe.wait_ge(copied, c + 1)
                    nc.tensor.transpose(ps[0:m, k % 4, 0:cw], fout[0:cw, k * P:k * P + m],
                                        e.ident[0:cw, 0:cw]).then_inc(back, 1)

        @block.scalar
        def _(act):
            if H:
                act.wait_ge(dec, 2)
                nc.scalar.activation(decay[:, :], decay[:, :], ACT.Exp).then_inc(exped, 1)

        @block.vector
        def _(dve):
            n = 0
            if H:
                nc.vector.memset(shifts[:, 0:1], 0.0).then_inc(dec, 1)
                dve.wait_ge(sh_in, 1)
                nc.vector.tensor_copy(shifts[:, 1:T + 1],
                                      ps[0:H, :, :].rearrange("p a b -> p (a b)")[:, 0:T]).then_inc(sh_out, 1)
                dve.wait_ge(sh_out, 1)
                dve.wait_ge(dec, 1)
                nc.vector.tensor_tensor(decay[:, :], shifts[:, 0:T], shifts[:, 1:T + 1], ALU.subtract)\
                    .then_inc(loadw, 1)
                dve.wait_ge(loadw, 1)
                nc.vector.tensor_scalar(decay[:, :], decay[:, :], 0.0, None, ALU.min).then_inc(dec, 1)
                dve.wait_ge(exped, 1)
                nc.vector.tensor_tensor(decay[:, :], decay[:, :], e.chain[0:H, :], ALU.mult).then_inc(exped, 1)
            for c, (c0, cw) in enumerate(chunks):
                cs = min(cw, scanned - c0)
                if H:
                    dve.wait_ge(spread, c + 1)
                    nc.vector.tensor_copy(wide[0:cs, :], ps[0:cs, :, :].rearrange("p a b -> p (a b)")[:, 0:T])\
                        .then_inc(widened, 1)
                dve.wait_ge(turned, c + 1)
                if c:
                    dve.wait_ge(back, c * TG)
                nc.vector.tensor_copy(fin[0:cw, :], ps[0:cw, :, :].rearrange("p a b -> p (a b)")[:, 0:T])\
                    .then_inc(copied, 1)
                dve.wait_ge(copied, c + 1)
                if H:
                    dve.wait_ge(widened, c + 1)
                    if cs < cw:
                        nc.vector.tensor_copy(fout[0:cw, :], fin[0:cw, :]).then_inc(loadw, 1)
                        dve.wait_ge(loadw, 2)
                    nc.vector.tensor_tensor_scan(fout[0:cs, :], wide[0:cs, :], fin[0:cs, :], 0.0,
                                                 ALU.mult, ALU.add).then_inc(scans, 1)
                else:
                    nc.vector.tensor_tensor_scan(fout[0:cs, :], e.chain[0:cs, :], fin[0:cs, :], 0.0,
                                                 ALU.mult, ALU.add).then_inc(scans, 1)
                for k, m in tiles:
                    dve.wait_ge(back, c * TG + k + 1)
                    nc.vector.tensor_copy(state[0:m, k, c0:c0 + cw], ps[0:m, k % 4, 0:cw]).then_inc(final, 1)
            if H:
                nc.vector.memset(shifts[:, 0:1], 0.0).then_inc(final, 1)


def dst_same(nc, dve, e, same, dst_b, r, b):
    return nc.vector.tensor_tensor(same[:, b], dst_b[:, b].rearrange("p (g i) -> p g i", g=G),
                                   e.dst[:, bass.ds(r * G, G)].unsqueeze(2).to_broadcast([P, G, P]),
                                   ALU.is_equal)


def edge_conv(nc, e, d, layer):
    L0 = layer == 0
    tag = f"edge{layer}_"
    TW = W if L0 else 384
    MW = 384 if L0 else W
    KE = 10 if L0 else 17
    parts = [(i, min(HW, MW - HW * i)) for i in range(-(-MW // HW))]
    with ExitStack() as loc:
        def tmp(name, shape, dt=F32):
            return loc.enter_context(nc.sbuf_tensor(tag + name, shape, dt))

        sems = []

        def sem(name):
            sems.append(loc.enter_context(nc.semaphore(tag + name)))
            return sems[-1]

        def ps(name, shape):
            return loc.enter_context(nc.psum_tensor(tag + name, shape, F32))

        idx = tmp("idx", [P, 2, G], I32)
        row = tmp("row", [P, 2, G, TW])
        feat = tmp("feat", [KE, 2, SB])
        dst_b = tmp("dst_b", [P, 2, SB], I32)
        same = tmp("same", [P, 2, G, P])
        msg = tmp("msg", [P, 2, G, MW])
        out = tmp("out", [P, 2, G, MW])
        if L0:
            w_a = tmp("w_fc1", [10, 100])
            w_b = tmp("w_fc2", [100, 192])
            hid = tmp("hid", [100, 2, SB])
            wy = tmp("wy", [P, G, 2, C0])
            we = tmp("we", [P, G, C1])
            dot = tmp("dot", [P, G, 3, C1])
            ps_h = ps("ps_h", [P, 512])
        else:
            w_a = tmp("w_rad", [17, W])
            sig = tmp("sig", [P, 2, G, W])
            u = tmp("u", [P, G, 4, C0])
            q = tmp("q", [P, G, 3, C1])
            r_ = tmp("r_", [P, G, 3, C1])
        ps_w = ps("ps_w", [P, G, 256])
        ps_a = ps("ps_a", [P, G, 512 if L0 else 256])
        loadw, scaled = sem("weights_loaded"), sem("weights_scaled")
        picked = sem("indices_copied")
        rows_in = [e.pool_dma_sem(tag + f"rows_in{b}") for b in range(2)]
        feat_in = [sem(f"feat_in{b}") for b in range(2)]
        dst_in = [sem(f"dst_in{b}") for b in range(2)]
        out_sent = [sem(f"out_sent{b}") for b in range(2)]
        if L0:
            V = Steps(sem("vec_msg"), ["same", "wy", "we", "dot", "m0", "m1", "m2", "dot1", "dot2", "m3"])
        else:
            V = Steps(sem("vec_msg"), ["same", "u", "q", "r", "u2", "v", "us", "ms", "mv"])
        PA = Steps(sem("pe_weights"), ["hid", "w"] if L0 else ["w"])
        PB = Steps(sem("pe_sums"), ["sums"])
        A = Steps(sem("act_weights"), ["hid"] if L0 else ["sig"])
        B = Steps(sem("act_sums"), ["lo", "hi"])
        first = "hid" if L0 else "sig"
        lastv = V.names[-1]
        readers_row = V.names[-1]
        loc.callback(clear, nc, sems)
        block = loc.enter_context(nc.Block())

        @block.sync
        def _(sp):
            if L0:
                load_blocks(sp, loadw, [(w_a[:, :], d["L0_gnn_W_fc1"]), (w_b[:, :], d["L0_gnn_W_fc2"])])
            else:
                load_blocks(sp, loadw, [(w_a[:, :], d["L2_rad"])])

            def load(r, b, n):
                if not early(r):
                    wait(sp, PA, r - 2, PA.names[0])
                sp.dma_start(feat[:, b], (d["ea10_rows"] if L0 else d["ea16_rows"])[0:KE, bass.ds(r * SB, SB)])\
                    .then_inc(feat_in[b], 16)
                if not early(r):
                    wait(sp, V, r - 2, "same")
                sp.dma_start(dst_b[:, b], d["dst_rows"][0:1, bass.ds(r * SB, SB)].to_broadcast([P, SB]))\
                    .then_inc(dst_in[b], 16)

            def store(r, b, n):
                wait(sp, B, r, "hi")
                for i, w in parts:
                    sp.dma_start(e.rows[layer][i][bass.ds(r * SB, SB), :].rearrange("(g p) w -> p g w", p=P),
                                 out[:, b, :, HW * i:HW * i + w]).then_inc(out_sent[b], 16)

            rounds(sp, [(load, 0), (store, 2)], S)
            for b in range(2):
                sp.wait_ge(out_sent[b], 16 * len(parts) * (S // 2))

        @block.gpsimd
        def _(pool):
            def fetch(r, b, n):
                if not early(r):
                    wait(pool, V, r - 2, readers_row)
                    pool.wait_ge(rows_in[b], 16 * G * n)
                    pool.nop(nofuse=True)
                nc.gpsimd.tensor_copy(idx[:, b, :], e.src[:, bass.ds(r * G, G)]).then_inc(picked, 1)
                pool.wait_ge(picked, r + 1)
                pool.nop(nofuse=True)
                for g in range(G):
                    pool.indirect_dma_start(row[:, b, g, :], None, e.tsrc[layer],
                                            bass.IndirectOffsetOnAxis(ap=idx[:, b, g:g + 1], axis=0))\
                        .then_inc(rows_in[b], 16)

            rounds(pool, [(fetch, 0)], S)

        @block.tensor
        def _(pe):
            pe.wait_ge(loadw, 32 if L0 else 16)
            if L0:
                pe.wait_ge(scaled, 1)

            def weights(r, b, n):
                pe.wait_ge(feat_in[b], 16 * (n + 1))
                if L0:
                    if not early(r, 1):
                        wait(pe, A, r - 1, "hid")
                    nc.tensor.matmul(ps_h[0:100, :], w_a[:, :], feat[:, b], start=True, stop=True)\
                        .then_inc(PA.sem, 1)
                    wait(pe, A, r, "hid")
                if not early(r, 1):
                    if L0:
                        wait(pe, V, r - 1, "m3")
                    else:
                        wait(pe, A, r - 1, "sig")
                for g in range(G):
                    lhs = hid[:, b, g * P:(g + 1) * P] if L0 else feat[:, b, g * P:(g + 1) * P]
                    mm = nc.tensor.matmul(ps_w[:, g, 0:(192 if L0 else W)], lhs, w_b[:, :] if L0 else w_a[:, :],
                                          start=True, stop=True)
                mm.then_inc(PA.sem, 1)

            def sums(r, b, n):
                wait(pe, V, r, lastv)
                if not early(r, 1):
                    wait(pe, B, r - 1, "hi")
                for g in range(G):
                    mm = nc.tensor.matmul(ps_a[:, g, 0:MW], same[:, b, g], msg[:, b, g], start=True, stop=True)
                mm.then_inc(PB.sem, 1)

            rounds(pe, [(weights, 0), (sums, 1)], S)

        @block.scalar
        def _(act):
            def weights(r, b, n):
                wait(act, PA, r, "hid" if L0 else "w")
                if L0:
                    if not early(r):
                        wait(act, PA, r - 2, "w")
                    nc.scalar.activation(hid[:, b], ps_h[0:100, :], ACT.Relu, scale=1.0 / np.sqrt(10.0))\
                        .then_inc(A.sem, 1)
                else:
                    if not early(r):
                        wait(act, V, r - 2, "mv")
                    nc.scalar.activation(sig[:, b], ps_w[:, :, 0:W], ACT.Sigmoid).then_inc(A.sem, 1)

            def sums(r, b, n):
                wait(act, PB, r, "sums")
                if not early(r):
                    act.wait_ge(out_sent[b], 16 * len(parts) * n)
                for h in range(2):
                    nc.scalar.copy(out[:, b, 2 * h:2 * h + 2], ps_a[:, 2 * h:2 * h + 2, 0:MW]).then_inc(B.sem, 1)

            rounds(act, [(weights, 0), (sums, 1)], S)

        @block.vector
        def _(dve):
            if L0:
                dve.wait_ge(loadw, 32)
                nc.vector.tensor_scalar(w_b[:, :], w_b[:, :], float(np.sqrt(2.0) / 10.0), None, ALU.mult)\
                    .then_inc(scaled, 1)

            def att(r, i0, i1):
                return e.ea4[:, bass.ds(r * G, G), i0:i1]

            def done(ins):
                ins.then_inc(V.sem, 1)

            def messages0(r, b, n):
                tt = nc.vector.tensor_tensor
                if not early(r, 1):
                    wait(dve, V, r - 1, V.names[-1])
                dve.wait_ge(dst_in[b], 16 * (n + 1))
                if not early(r):
                    wait(dve, PB, r - 2, "sums")
                done(dst_same(nc, dve, e, same, dst_b, r, b))
                wait(dve, PA, r, "w")
                dve.wait_ge(rows_in[b], 16 * G * (n + 1))
                y = row[:, b]
                yv = y[:, :, C0:W].rearrange("p g (d c) -> p g d c", d=3)
                done(tt(wy[:, :, :, :], ps_w[:, :, 0:128].rearrange("p g (a c) -> p g a c", a=2),
                        y[:, :, 0:C0].unsqueeze(2).to_broadcast([P, G, 2, C0]), ALU.mult))
                done(tt(we[:, :, :], ps_w[:, :, 128:160], att(r, 0, 1).to_broadcast([P, G, C1]), ALU.mult))
                done(tt(dot[:, :, :, :], yv, att(r, 1, 4).unsqueeze(3).to_broadcast([P, G, 3, C1]), ALU.mult))
                wait(dve, V, r, "wy")
                done(tt(msg[:, b, :, 0:C0], wy[:, :, 0, :], att(r, 0, 1).to_broadcast([P, G, C0]), ALU.mult))
                m = msg[:, b, :, 96:384].rearrange("p g (d c) -> p g d c", d=3)
                done(tt(m[:, :, :, 0:C0], wy[:, :, 1, :].unsqueeze(2).to_broadcast([P, G, 3, C0]),
                        att(r, 1, 4).unsqueeze(3).to_broadcast([P, G, 3, C0]), ALU.mult))
                wait(dve, V, r, "dot")
                done(tt(m[:, :, :, C0:96], we[:, :, :].unsqueeze(2).to_broadcast([P, G, 3, C1]), yv, ALU.mult))
                done(tt(dot[:, :, 0, :], dot[:, :, 0, :], dot[:, :, 1, :], ALU.add))
                wait(dve, V, r, "dot1")
                done(tt(dot[:, :, 0, :], dot[:, :, 0, :], dot[:, :, 2, :], ALU.add))
                wait(dve, V, r, "dot2")
                done(tt(msg[:, b, :, C0:96], dot[:, :, 0, :], ps_w[:, :, 160:192], ALU.mult))

            def messages2(r, b, n):
                tt = nc.vector.tensor_tensor
                if not early(r, 1):
                    wait(dve, V, r - 1, V.names[-1])
                dve.wait_ge(dst_in[b], 16 * (n + 1))
                if not early(r):
                    wait(dve, PB, r - 2, "sums")
                done(dst_same(nc, dve, e, same, dst_b, r, b))
                dve.wait_ge(rows_in[b], 16 * G * (n + 1))
                y = row[:, b]
                done(tt(u[:, :, :, :], y[:, :, 0:256].rearrange("p g (k c) -> p g k c", k=4),
                        att(r, 0, 4).unsqueeze(3).to_broadcast([P, G, 4, C0]), ALU.mult))
                done(tt(q[:, :, :, :], y[:, :, 256:288].unsqueeze(2).to_broadcast([P, G, 3, C1]),
                        att(r, 1, 4).unsqueeze(3).to_broadcast([P, G, 3, C1]), ALU.mult))
                done(tt(r_[:, :, :, :].rearrange("p g d c -> p g (d c)"), y[:, :, 288:384],
                        att(r, 0, 1).to_broadcast([P, G, 96]), ALU.mult))
                wait(dve, V, r, "u")
                done(tt(u[:, :, 0:2, :], u[:, :, 0:2, :], u[:, :, 2:4, :], ALU.add))
                wait(dve, V, r, "r")
                done(tt(q[:, :, :, :], q[:, :, :, :], r_[:, :, :, :], ALU.add))
                wait(dve, V, r, "u2")
                done(tt(u[:, :, 0, :], u[:, :, 0, :], u[:, :, 1, :], ALU.add))
                wait(dve, A, r, "sig")
                wait(dve, V, r, "us")
                done(tt(msg[:, b, :, 0:C0], u[:, :, 0, :], sig[:, b, :, 0:C0], ALU.mult))
                done(tt(msg[:, b, :, C0:W], q[:, :, :, :].rearrange("p g d c -> p g (d c)"),
                        sig[:, b, :, C0:W], ALU.mult))

            rounds(dve, [(messages0 if L0 else messages2, 0)], S)


def edge_attention(nc, e, d, layer):
    L1 = layer == 1
    tag = f"edge{layer}_"
    H = HEADS[layer]
    per_s, per_v = C0 // H, C1 // H
    MW = W + H
    RW = W + 2 * H
    KE = 16 if L1 else 65
    KB = 96 if L1 else 97
    LW = 0 if L1 else 3
    LP, LT, LJ = LW + 1, LW + 2, LW + 3
    NX = 2 if L1 else 1
    r2, r3 = 1.0 / float(np.sqrt(2.0)), 1.0 / float(np.sqrt(3.0))
    with ExitStack() as loc:
        def tmp(name, shape, dt=F32):
            return loc.enter_context(nc.sbuf_tensor(tag + name, shape, dt))

        sems = []

        def sem(name):
            sems.append(loc.enter_context(nc.semaphore(tag + name)))
            return sems[-1]

        def ps(name, shape):
            return loc.enter_context(nc.psum_tensor(tag + name, shape, F32))

        idx = tmp("idx", [P, 2, 2, G], I32)
        row = tmp("row", [P, 2, 2, G, W])
        feat = tmp("feat", [KE, 2, SB])
        dst_b = tmp("dst_b", [P, 2, SB], I32)
        pen = tmp("pen", [H, 2, SB + 1])
        m = tmp("m", [P, G, C0 + 5 * C1])
        y5 = tmp("y5", [P, 2, G, 5])
        t1 = tmp("t1", [P, G, 3, C1])
        t2 = tmp("t2", [P, G, 3, C1])
        t3 = tmp("t3", [P, G, 3, C1])
        dot = tmp("dot", [P, G, 3, C1])
        x1 = tmp("x1", [P, NX, G, 96])
        x23 = tmp("x23", [P, NX, G, 256])
        x1t = tmp("x1t", [KB, SB])
        x2t = tmp("x2t", [P, SB])
        x3t = tmp("x3t", [P, SB])
        bend = tmp("bend", [C0, SB])
        soft = tmp("soft", [C0, SB])
        shf = tmp("shf", [H, 2, SB])
        shb = tmp("shb", [H, SB])
        arg = tmp("arg", [H, SB])
        es = tmp("es", [32 + H, SB])
        exs = tmp("exs", [P, G, 32 + H])
        exv = tmp("exv", [P, G, C1])
        same = tmp("same", [P, 2, G, P])
        msg = tmp("msg", [P, 2, G, MW])
        out = tmp("out", [P, 2, G, RW])
        w_rad = tmp("w_rad", [KE, 224])
        w_al = tmp("w_al", [KB, C0])
        w_ad = tmp("w_ad", [C0, H])
        w_s = tmp("w_s", [KB, C0])
        w_v = tmp("w_v", [P, 2, C0])
        ps_w = ps("ps_w", [P, G, 256])
        ps_n = ps("ps_n", [P, 512])
        ring = [ps(f"ring{i}", [P, 512]) for i in range(2)]
        ps_l = ps("ps_l", [P, 512])
        ps_v = ps("ps_v", [P, G, 128])
        ps_s = ps("ps_s", [P, 512])
        out_s = ps_s[:, 0:256].rearrange("p (g c) -> p g c", g=G)
        ex_p = ps_s[:, 256:256 + G * (32 + H)].rearrange("p (g c) -> p g c", g=G)
        if L1:
            wy = tmp("wy", [P, G, 96])
            vt = tmp("vt", [C0, SB])
            gate = tmp("gate", [P, G, C1])
            gh = tmp("gh", [P, G, C1])
            sh = tmp("sh", [P, G, C0])
            v5 = tmp("v5", [P, G, 5, C1])
            z1 = tmp("z1", [P, G, 96])
            z23 = tmp("z23", [P, G, 256])
            z1t = tmp("z1t", [96, SB])
            z2t = tmp("z2t", [P, SB])
            z3t = tmp("z3t", [P, SB])
            w_g = tmp("w_g", [C0, C1])
            w_s2 = tmp("w_s2", [96, C0])
            w_v2 = tmp("w_v2", [P, 2, C0])
            c_s2 = tmp("c_s2", [96, 1])
            c_v2 = tmp("c_v2", [P, 2, 1])
        else:
            ea4_flat = e.ea4[:, :, :].rearrange("p t k -> p (t k)")
            y3 = ea4_flat[:, 0:3 * T].rearrange("p (t k) -> p t k", k=3)
            part = ea4_flat[:, 3 * T:4 * T]
            len2 = tmp("len2", [P, T])
            w1 = tmp("w1", [65, C0])
            w2 = tmp("w2", [65, C0])
            w3 = tmp("w3", [65, 224])
            mean = tmp("mean", [65, 2])
            gb = tmp("gb", [C0, 4])
            gbh = tmp("gbh", [C0, 4])
            sq = tmp("sq", [P, 2, G, C0])
            ve = tmp("ve", [P, 2, G])
            rs = tmp("rs", [P, 2, G])
            zn = tmp("zn", [P, 2, G, C0])
            hu = tmp("hu", [C0, 2, SB])
            th = tmp("th", [C0, 2, SB])
            h1t = tmp("h1t", [65, SB])
            h2t = tmp("h2t", [65, 2, SB])

        loadw, zeroed, prepped, chained, pooled = (sem("weights_loaded"), sem("zeroed"), sem("weights_ready"),
                                                   sem("prep_chain"), sem("prep_pool"))
        picked = sem("indices_copied")
        rows_in = [e.pool_dma_sem(tag + f"rows_in{b}") for b in range(2)]
        feat_in = [sem(f"feat_in{b}") for b in range(2)]
        dst_in = [sem(f"dst_in{b}") for b in range(2)]
        pen_in = [sem(f"pen_in{b}") for b in range(2)]
        out_sent = [sem(f"out_sent{b}") for b in range(2)]
        VP = Steps(sem("vec_product"), ["m", "m5", "y5", "y5b"] + (["wy"] if L1 else []) +
                   ["dot", "t1", "t2", "s", "q", "vs", "dot1", "t12", "dot2", "cross", "o0b"])
        VM = Steps(sem("vec_maps"), ["soft"] + (["zy", "bc", "gate", "q", "v5", "v5b", "dot", "t1", "t2", "s", "vs",
                                                 "dot1", "cross", "o0b"] if L1 else []) +
                   ["fwd", "bwd", "arg"])
        VJ = Steps(sem("vec_joint"), ["same", "exs", "exv", "s", "zy", "bc", "v", "w"])
        PW = Steps(sem("pe_weights"), ["w"])
        PX = Steps(sem("pe_turn"), ["x1", "x2", "x3"])
        PM = Steps(sem("pe_maps"), ["al"] + (["vt"] if L1 else []) + ["s", "v", "at"] + (["gate"] if L1 else []))
        PE_ = Steps(sem("pe_ex"), ["ex"])
        PJ = Steps(sem("pe_joint"), ["lo", "hi"])
        AT = Steps(sem("act_turn"), ["x1", "x2", "x3"])
        AM = Steps(sem("act_maps"), ["bend"] + (["vt", "sh", "gh"] if L1 else []))
        AE = Steps(sem("act_ex"), ["ex", "sh2"])
        AJ = Steps(sem("act_joint"), ["shift", "lo", "hi"])
        if L1:
            PZ = Steps(sem("pe_turn2"), ["x1", "x2", "x3", "v"])
            AZ = Steps(sem("act_turn2"), ["x1", "x2", "x3"])
        else:
            VZ = [Steps(sem(f"vec_z{k}"), ["ss", "ve"]) for k in (1, 2)]
            VN = [Steps(sem(f"vec_zn{k}"), ["zn"]) for k in (1, 2)]
            VH = [Steps(sem(f"vec_h{k}"), ["h"]) for k in (1, 2)]
            PZ_ = [Steps(sem(f"pe_z{k}"), ["z"]) for k in (1, 2)]
            PT = [Steps(sem(f"pe_zt{k}"), ["zt"]) for k in (1, 2)]
            AQ = [Steps(sem(f"act_sq{k}"), ["sq"]) for k in (1, 2)]
            AH = [Steps(sem(f"act_h{k}"), ["hu", "th"]) for k in (1, 2)]
            KN = [Steps(sem(f"pool_rs{k}"), ["rs"]) for k in (1, 2)]

        def last(r, n=1):
            return isinstance(r, int) and r + n >= S

        def c1(ap):
            return ap.rearrange("(p a) -> p a", a=1)

        def maps_loads(w_v, wv):
            return [(w_v[0:64, 0, 0:32], wv[0:64, :]), (w_v[64:128, 0, 32:64], wv[64:128, :]),
                    (w_v[0:64, 1, 0:32], wv[64:128, :]), (w_v[64:128, 1, 32:64], wv[64:128, :])]

        def rad_loads(w, src, k):
            return [(w[0:k, 0:64], src[:, 0:64]), (w[0:k, 64:96], src[:, 128:160]), (w[0:k, 96:160], src[:, 64:128]),
                    (w[0:k, 160:224], src[:, 160:224])]

        wload = []
        if L1:
            wload += rad_loads(w_rad, d["L1_gnn_W_rbf"], 16)
            wload += [(w_al[:, :], d["L1_gnn_W_alpha"]), (w_s[:, :], d["L1_gnn_Ws_val"]), (w_g[:, :], d["L1_gnn_Wg"]),
                      (w_s2[:, :], d["L1_gnn_Ws_vlin"])]
            wload += maps_loads(w_v, d["L1_gnn_Wv_val"]) + maps_loads(w_v2, d["L1_gnn_Wv_vlin"])
            wload += [(c_s2[0:64, :], c1(d["L1_gnn_w2_ss"])), (c_s2[64:96, :], c1(d["L1_gnn_w2_vv0"])),
                      (c_v2[0:64, 0, :], c1(d["L1_gnn_w2_sv"]))]
            for p0, k in ((64, 0), (0, 1), (64, 1)):
                wload += [(c_v2[p0:p0 + 32, k, :], c1(d["L1_gnn_w2_vs"])),
                          (c_v2[p0 + 32:p0 + 64, k, :], c1(d["L1_gnn_w2_vv1"]))]
            adot = d["L1_gnn_alpha_dot"]
        else:
            wload += rad_loads(w3, d["L3_gnn_rw3"], 64)
            roff = d["L3_gnn_roff"].rearrange("(a b) -> a b", a=1)
            wload += rad_loads(w3[64:65, :], roff, 1)
            c = lambda n: d["L3_gnn_" + n].rearrange("(a b) -> a b", a=1)
            wload += [(w1[0:64, :], d["L3_gnn_rw1"]), (w1[64:65, :], c("rb1")),
                      (w2[0:64, :], d["L3_gnn_rw2"]), (w2[64:65, :], c("rb2")),
                      (w_al[0:96, :], d["L3_gnn_lin_ws"][:, 0:64]), (w_al[96:97, :], c("lin_bs")[:, 0:64]),
                      (w_s[0:96, :], d["L3_gnn_lin_ws"][:, 64:128]), (w_s[96:97, :], c("lin_bs")[:, 64:128]),
                      (y3[:, :, :], d["ea3_cols"])]
            wload += maps_loads(w_v, d["L3_gnn_lin_wv"])
            wload += [(gb[:, i:i + 1], c1(d["L3_gnn_" + n])) for i, n in enumerate(("rg1", "rbe1", "rg2", "rbe2"))]
            adot = d["L3_gnn_alpha_dot"]
        for h in range(H):
            wload += [(w_ad[per_s * h:per_s * h + per_s, h:h + 1],
                       adot[(0, h) if len(adot.shape) == 3 else h].rearrange("(p a) -> p a", a=1))]
        zero = [w_v[:, :, :], w_ad[:, :], es[:, :]] + ([w_v2[:, :, :]] if L1 else [])
        loc.callback(clear, nc, sems)
        block = loc.enter_context(nc.Block())

        @block.sync
        def _(sp):
            sp.wait_ge(zeroed, len(zero))
            load_blocks(sp, loadw, wload)

            def load_feat(r, b, n):
                if not early(r):
                    wait(sp, PW if L1 else PZ_[0], r - 2, "w" if L1 else "z")
                sp.dma_start(feat[:, b], d["ea16_rows" if L1 else "ea64_rows"][0:KE, bass.ds(r * SB, SB)])\
                    .then_inc(feat_in[b], 16)

            def load_pen(r, b, n):
                if not early(r):
                    wait(sp, VM, r - 2, "bwd")
                sp.dma_start(pen[:, b], e.pens[bass.ds(r * SB, SB + 1)].rearrange("(a f) -> a f", a=1)
                             .to_broadcast([H, SB + 1])).then_inc(pen_in[b], 16)

            def load_dst(r, b, n):
                if not early(r):
                    wait(sp, VJ, r - 2, "same")
                sp.dma_start(dst_b[:, b], d["dst_rows"][0:1, bass.ds(r * SB, SB)].to_broadcast([P, SB]))\
                    .then_inc(dst_in[b], 16)

            def store(r, b, n):
                wait(sp, AJ, r, "hi")
                sp.dma_start(e.rows[layer][0][bass.ds(r * SB, SB), :].rearrange("(g p) w -> p g w", p=P),
                             out[:, b]).then_inc(out_sent[b], 16)

            rounds(sp, [(load_feat, 0), (load_pen, LT - 1), (load_dst, LJ - 1), (store, LJ + 1)], S)
            for b in range(2):
                sp.wait_ge(out_sent[b], 16 * (S // 2))

        @block.gpsimd
        def _(pool):
            for z in zero:
                pool.memset(z, 0.0).then_inc(zeroed, 1)
            if not L1:
                pool.wait_ge(chained, 5)
                nc.gpsimd.tensor_tensor(part[:, :], len2[:, :], e.mhalf[:, 0:1].to_broadcast([P, T]), ALU.pow)\
                    .then_inc(pooled, 1)

            def fetch(r, b, n):
                if not early(r):
                    wait(pool, VP, r - 2, "m5")
                    pool.wait_ge(rows_in[b], 32 * G * n)
                    pool.nop(nofuse=True)
                for k, cols in enumerate((e.src, e.dst)):
                    nc.gpsimd.tensor_copy(idx[:, b, k, :], cols[:, bass.ds(r * G, G)]).then_inc(picked, 1)
                pool.wait_ge(picked, 2 * r + 2)
                pool.nop(nofuse=True)
                for k, table in enumerate((e.tsrc[layer], e.tdst)):
                    for g in range(G):
                        pool.indirect_dma_start(row[:, b, k, g, :], None, table,
                                                bass.IndirectOffsetOnAxis(ap=idx[:, b, k, g:g + 1], axis=0))\
                            .then_inc(rows_in[b], 16)

            def power(k):
                def fn(r, b, n):
                    wait(pool, VZ[k], r, "ve")
                    nc.gpsimd.tensor_tensor(rs[:, k, :], ve[:, k, :], e.mhalf[:, 0:G], ALU.pow).then_inc(KN[k].sem, 1)
                return fn

            rounds(pool, [(fetch, 0)] if L1 else [(power(0), 0), (power(1), 2), (fetch, LW)], S)

        @block.tensor
        def _(pe):
            mm, tp = nc.tensor.matmul, nc.tensor.transpose
            pe.wait_ge(loadw, 16 * len(wload))
            pe.wait_ge(prepped, 1)

            def turn_x(steps, a, a2, first, second, third, r):
                for k, (i, waits) in enumerate((first, second, third)):
                    for w in waits:
                        wait(pe, *w)
                    if waits:
                        pe.nop(nofuse=True)
                    for g in range(G):
                        if k == 0:
                            t = tp(ring[i][0:96, g * P:(g + 1) * P], a[:, g, :], e.ident[:, :])
                        else:
                            t = tp(ring[i][:, g * P:(g + 1) * P], a2[:, g, P * (k - 1):P * k], e.ident[:, :])
                    t.then_inc(steps.sem, 1)

            def z(k):
                def fn(r, b, n):
                    if k == 0:
                        pe.wait_ge(feat_in[b], 16 * (n + 1))
                    else:
                        wait(pe, VH[0], r, "h")
                    if not early(r, 1):
                        wait(pe, VN[k], r - 1, "zn")
                    if k == 0 and not early(r, 3):
                        wait(pe, VN[1], r - 3, "zn")
                    if k == 1 and not last(r):
                        wait(pe, VN[0], r + 1, "zn")
                    pe.nop(nofuse=True)
                    for g in range(G):
                        lhs = feat[:, b, g * P:(g + 1) * P] if k == 0 else h1t[:, g * P:(g + 1) * P]
                        t = mm(ps_n[:, 256 * k + C0 * g:256 * k + C0 * (g + 1)], lhs, (w2 if k else w1)[:, :],
                               start=True, stop=True)
                    t.then_inc(PZ_[k].sem, 1)
                return fn

            def zt(k):
                def fn(r, b, n):
                    lag = 4 if k == 0 else 2
                    if not early(r, lag):
                        wait(pe, AT, r - lag, "x3" if k else "x2")
                    elif r > 0:
                        wait(pe, AH[k], r - 1, "th")
                    wait(pe, VN[k], r, "zn")
                    pe.nop(nofuse=True)
                    for g in range(G):
                        t = tp(ring[1 - k][0:C0, P * g:P * (g + 1)], zn[:, k, g, :], e.ident[:, :])
                    t.then_inc(PT[k].sem, 1)
                return fn

            def weights(r, b, n):
                if L1:
                    pe.wait_ge(feat_in[b], 16 * (n + 1))
                else:
                    wait(pe, VH[1], r, "h")
                if not early(r, 1):
                    wait(pe, VP, r - 1, "o0b")
                for g in range(G):
                    lhs = feat[:, b, g * P:(g + 1) * P] if L1 else h2t[:, b, g * P:(g + 1) * P]
                    t = mm(ps_w[:, g, 0:224], lhs, (w_rad if L1 else w3)[:, :], start=True, stop=True)
                t.then_inc(PW.sem, 1)

            def turn(r, b, n):
                wait(pe, VP, r, "o0b")
                xb = b if L1 else 0
                if L1:
                    if early(r, 1):
                        uses = (1, []), (0, []), (1, [(AT, r, "x1")])
                    else:
                        uses = (1, [(AZ, r - 1, "x2")] if not early(r, 1) else []), \
                               (0, [(AZ, r - 1, "x3")]), (1, [(AT, r, "x1")])
                else:
                    uses = (0, [(AH[1], r + 1, "th")] if early(r) else [(AJ, r - 2, "hi")]), (1, []), \
                           (0, [(AT, r, "x1")])
                turn_x(PX, x1[:, xb], x23[:, xb], *uses, r)

            def turn2(r, b, n):
                wait(pe, VM, r, "o0b")
                turn_x(PZ, z1, z23, (0, [(AT, r, "x3")] if early(r, 1) else [(AJ, r - 1, "lo")]),
                       (1, [] if early(r, 1) else [(AJ, r - 1, "hi")]), (0, [(AZ, r, "x1")]), r)

            def ex(r, b, n):
                wait(pe, AE, r, "sh2")
                if L1:
                    wait(pe, AM, r, "sh")
                if not early(r, 1):
                    wait(pe, VJ, r - 1, "w")
                pe.nop(nofuse=True)
                for g in range(G):
                    t = tp(ex_p[:, g, :], es[:, g * P:(g + 1) * P], e.ident[0:32 + H, 0:32 + H])
                t.then_inc(PE_.sem, 1)

            def sums(r, b, n):
                wait(pe, VJ, r, "w")
                for k, name in enumerate(("lo", "hi")):
                    if L1:
                        wait(pe, *((AZ, r, "x3") if last(r) else (AT, r + 1, "x3" if k else "x2")))
                    elif not last(r, 3 if k else 5):
                        wait(pe, AH[k], r + (3 if k else 5), "th")
                    elif not last(r):
                        wait(pe, AT, r + 1, "x3" if k else "x2")
                    else:
                        wait(pe, AJ, r - 1, name)
                    bank = ring[k if L1 else 1 - k]
                    for g in range(2):
                        t = mm(bank[:, 256 * g:256 * g + MW], same[:, b, 2 * k + g], msg[:, b, 2 * k + g],
                               start=True, stop=True)
                    t.then_inc(PJ.sem, 1)

            def out_maps(xt, ws):
                for g in range(G):
                    t = mm(out_s[:, g, :], xt[:, g * P:(g + 1) * P], ws[:, :], start=True, stop=True)
                return t

            def vec_maps(xt, yt, wv):
                for g in range(G):
                    mm(ps_v[:, g, 0:64], xt[:, g * P:(g + 1) * P], wv[:, 0, :], start=True, stop=True)
                    t = mm(ps_v[:, g, 64:128], yt[:, g * P:(g + 1) * P], wv[:, 1, :], start=True, stop=True)
                return t

            def maps_al(r, b, n):
                wait(pe, AT, r, "x1")
                if not early(r, 1):
                    wait(pe, VM, r - 1, "arg")
                mm(ps_l[0:C0, :], w_al[:, :], x1t[:, :], start=True, stop=True).then_inc(PM.sem, 1)
                if L1:
                    if not early(r, 1):
                        wait(pe, AM, r - 1, "gh")
                    mm(ps_n[0:C0, :], w_s[:, :], x1t[:, :], start=True, stop=True).then_inc(PM.sem, 1)

            def maps_sv(r, b, n):
                wait(pe, AT, r, "x3")
                if not early(r, 1):
                    wait(pe, VJ, r - 1, "w")
                out_maps(x1t, w_s).then_inc(PM.sem, 1)
                vec_maps(x2t, x3t, w_v).then_inc(PM.sem, 1)

            def maps_at(r, b, n):
                wait(pe, VM, r, "soft")
                pe.nop(nofuse=True)
                mm(ps_l[0:H, :], w_ad[:, :], bend[:, :], start=True, stop=True).then_inc(PM.sem, 1)
                if L1:
                    wait(pe, AM, r, "vt")
                    pe.nop(nofuse=True)
                    for g in range(G):
                        t = mm(ps_n[:, C1 * g:C1 * (g + 1)], vt[:, g * P:(g + 1) * P], w_g[:, :], start=True, stop=True)
                    t.then_inc(PM.sem, 1)

            def maps2(r, b, n):
                wait(pe, AZ, r, "x3")
                wait(pe, AM, r, "sh")
                wait(pe, VM, r, "arg")
                out_maps(z1t, w_s2)
                vec_maps(z2t, z3t, w_v2).then_inc(PZ.sem, 1)

            rounds(pe, [(turn2, LJ), (ex, LJ), (maps2, LJ), (turn, LT), (maps_al, LT), (weights, LW),
                        (maps_sv, LT), (maps_at, LT), (sums, LJ)] if L1 else
                   [(turn, LT), (ex, LJ), (zt(0), 1), (zt(1), 3), (maps_al, LT), (z(0), 0), (z(1), 2),
                    (maps_sv, LT), (sums, LJ), (maps_at, LT), (weights, LW)], S)

        @block.scalar
        def _(act):
            copy, af = nc.scalar.copy, nc.scalar.activation
            act.wait_ge(prepped, 1)

            def squares(k):
                def fn(r, b, n):
                    wait(act, PZ_[k], r, "z")
                    if k == 0 and not early(r):
                        wait(act, PZ_[1], r - 2, "z")
                    if not early(r, 1):
                        wait(act, VZ[k], r - 1, "ss")
                    af(sq[:, k, :, :].rearrange("p g c -> p (g c)"), ps_n[:, 256 * k:256 * k + 256], ACT.Square)\
                        .then_inc(AQ[k].sem, 1)
                return fn

            def silu(k):
                def fn(r, b, n):
                    wait(act, PT[k], r, "zt")
                    if not early(r, 1):
                        wait(act, VH[k], r - 1, "h")
                    af(hu[:, k], ring[1 - k][0:C0, :], ACT.Identity, scale=gb[:, 2 * k:2 * k + 1],
                       bias=gb[:, 2 * k + 1:2 * k + 2]).then_inc(AH[k].sem, 1)
                    af(th[:, k], ring[1 - k][0:C0, :], ACT.Tanh, scale=gbh[:, 2 * k:2 * k + 1],
                       bias=gbh[:, 2 * k + 1:2 * k + 2]).then_inc(AH[k].sem, 1)
                return fn

            def copy_x(psteps, steps, r, outs, bank):
                for k, dst in enumerate(outs):
                    rows = 96 if k == 0 else P
                    wait(act, psteps, r, f"x{k + 1}")
                    copy(dst[0:rows, :], ring[(bank + k) % 2][0:rows, :]).then_inc(steps.sem, 1)

            def turn(r, b, n):
                if not early(r, 1):
                    wait(act, PM, r - 1, "v")
                copy_x(PX, AT, r, (x1t, x2t, x3t), 1 if L1 else 0)

            def turn2(r, b, n):
                if not early(r, 1):
                    wait(act, PZ, r - 1, "v")
                copy_x(PZ, AZ, r, (z1t, z2t, z3t), 0)

            def exps(r, b, n):
                wait(act, VM, r, "arg")
                if not early(r, 1):
                    wait(act, PE_, r - 1, "ex")
                af(es[0:H, :], arg[:, :], ACT.Exp).then_inc(AE.sem, 1)
                copy(es[32:32 + H, :], shb[:, :]).then_inc(AE.sem, 1)

            def joint(r, b, n):
                wait(act, VJ, r, "exs")
                if not early(r):
                    act.wait_ge(out_sent[b], 16 * n)
                copy(out[:, b, :, MW:RW], exs[:, :, 32:32 + H]).then_inc(AJ.sem, 1)
                for k, name in enumerate(("lo", "hi")):
                    bank = ring[k if L1 else 1 - k]
                    wait(act, PJ, r, name)
                    copy(out[:, b, 2 * k:2 * k + 2, 0:MW], bank[:, :].rearrange("p (g c) -> p g c", g=2)[:, :, 0:MW])\
                        .then_inc(AJ.sem, 1)

            def bends(r, b, n):
                wait(act, PM, r, "al")
                if not early(r, 1):
                    wait(act, VM, r - 1, "soft")
                if L1:
                    af(soft[:, :], ps_l[0:C0, :], ACT.Relu).then_inc(AM.sem, 1)
                    wait(act, PM, r, "vt")
                    if not early(r, 1):
                        wait(act, PM, r - 1, "gate")
                    copy(vt[:, :], ps_n[0:C0, :]).then_inc(AM.sem, 1)
                else:
                    af(soft[:, :], ps_l[0:C0, :], ACT.Tanh, scale=0.5).then_inc(AM.sem, 1)

            def gates(r, b, n):
                wait(act, PM, r, "s")
                if not early(r, 1):
                    wait(act, VM, r - 1, "o0b")
                af(sh[:, :, :], out_s, ACT.Tanh, scale=0.5).then_inc(AM.sem, 1)
                wait(act, PM, r, "gate")
                af(gh[:, :, :].rearrange("p g c -> p (g c)"), ps_n[:, 0:G * C1], ACT.Tanh, scale=0.5)\
                    .then_inc(AM.sem, 1)

            rounds(act, [(turn2, LJ), (exps, LJ), (turn, LT), (bends, LT), (gates, LT), (joint, LJ)] if L1 else
                   [(turn, LT), (exps, LJ), (silu(0), 1), (silu(1), 3), (bends, LT), (squares(0), 0),
                    (squares(1), 2), (joint, LJ)], S)

        @block.vector
        def _(dve):
            tt, ts, stt = nc.vector.tensor_tensor, nc.vector.tensor_scalar, nc.vector.scalar_tensor_tensor
            dve.wait_ge(loadw, 16 * len(wload))
            n_ch = [0]

            def link(ins):
                ins.then_inc(chained, 1)
                n_ch[0] += 1
                dve.wait_ge(chained, n_ch[0])

            if not L1:
                link(tt(len2[:, :], y3[:, :, 0], y3[:, :, 0], ALU.mult))
                link(tt(part[:, :], y3[:, :, 1], y3[:, :, 1], ALU.mult))
                link(tt(len2[:, :], len2[:, :], part[:, :], ALU.add))
                link(tt(part[:, :], y3[:, :, 2], y3[:, :, 2], ALU.mult))
                link(stt(out=len2[:, :], in0=part[:, :], scalar=1e-12, in1=len2[:, :], op0=ALU.add, op1=ALU.add))
                dve.wait_ge(pooled, 1)
                for i in range(3):
                    link(stt(out=y3[:, :, i], in0=y3[:, :, i], scalar=float(np.sqrt(3.0)), in1=part[:, :],
                             op0=ALU.mult, op1=ALU.mult))
                link(ts(w2[0:64, :], w2[0:64, :], 0.5, None, ALU.mult))
                link(ts(w3[0:64, :], w3[0:64, :], 0.5, None, ALU.mult))
                for k, w in enumerate((w1, w2)):
                    link(nc.vector.tensor_reduce(mean[:, k:k + 1], w[:, :], AX.X, ALU.add))
                    link(ts(mean[:, k:k + 1], mean[:, k:k + 1], 1.0 / C0, None, ALU.mult))
                    link(ts(w[:, :], w[:, :], mean[:, k:k + 1], None, ALU.subtract))
                link(ts(gbh[:, :], gb[:, :], 0.5, None, ALU.mult))
                link(nc.vector.memset(h1t[64:65, :], 1.0))
                link(nc.vector.memset(h2t[64:65, :, :], 1.0))
                link(nc.vector.memset(x1t[96:97, :], 1.0))
            wr = w_rad if L1 else w3
            link(ts(wr[:, 160:192], wr[:, 160:192], r3, None, ALU.mult))
            link(ts(wr[:, 192:224], wr[:, 192:224], r2, None, ALU.mult))
            link(ts(w_ad[:, :], w_ad[:, :], 0.2 if L1 else 0.4, None, ALU.mult))
            if L1:
                link(ts(w_s2[:, :], w_s2[:, :], c_s2[:, :], None, ALU.mult))
                link(ts(w_s2[64:96, :], w_s2[64:96, :], r3, None, ALU.mult))
                for k in range(2):
                    link(ts(w_v2[:, k, :], w_v2[:, k, :], c_v2[:, k, :], None, ALU.mult))
                for p0, k in ((96, 0), (32, 1), (96, 1)):
                    link(ts(w_v2[p0:p0 + 32, k, :], w_v2[p0:p0 + 32, k, :], r2, None, ALU.mult))
            nc.vector.memset(shf[:, 1, SB - 1:SB], -BIG).then_inc(prepped, 1)

            def y_of(b, k, n, width):
                return y5[:, b, :, k:k + n].unsqueeze(3).to_broadcast([P, G, n, width])

            def comps(ap):
                return ap.rearrange("p g (d c) -> p g d c", c=C1)

            def steps_of(steps):
                def done(ins):
                    ins.then_inc(steps.sem, 1)
                return done

            def variance(k):
                def fn(r, b, n):
                    done = steps_of(VZ[k])
                    wait(dve, AQ[k], r, "sq")
                    if not early(r, 1):
                        wait(dve, KN[k], r - 1, "rs")
                        wait(dve, VN[k], r - 1, "zn")
                    done(nc.vector.tensor_reduce(ve[:, k, :], sq[:, k, :, :], AX.X, ALU.add))
                    wait(dve, VZ[k], r, "ss")
                    done(ts(ve[:, k, :], ve[:, k, :], 1.0 / C0, EPS, ALU.mult, ALU.add))
                return fn

            def scaled(k):
                def fn(r, b, n):
                    wait(dve, KN[k], r, "rs")
                    if not early(r, 1):
                        wait(dve, PT[k], r - 1, "zt")
                    tt(zn[:, k, :, :], ps_n[:, 256 * k:256 * k + 256].rearrange("p (g c) -> p g c", g=G),
                       rs[:, k, :].unsqueeze(2).to_broadcast([P, G, C0]), ALU.mult).then_inc(VN[k].sem, 1)
                return fn

            def hidden(k):
                def fn(r, b, n):
                    wait(dve, AH[k], r, "th")
                    if k == 0 and not early(r, 1):
                        wait(dve, PZ_[1], r - 1, "z")
                    if k == 1 and not early(r):
                        wait(dve, PW, r - 2, "w")
                    stt(out=h2t[0:C0, b] if k else h1t[0:C0, :], in0=th[:, k], scalar=1.0, in1=hu[:, k],
                        op0=ALU.add, op1=ALU.mult).then_inc(VH[k].sem, 1)
                return fn

            def product_a(r, b, n):
                done = steps_of(VP)
                dve.wait_ge(rows_in[b], 32 * G * (n + 1))
                if not early(r, 1):
                    wait(dve, VP, r - 1, "o0b")
                if L1 and not early(r):
                    wait(dve, VM, r - 2, "arg")
                done(tt(m[:, :, 0:W], row[:, b, 0], row[:, b, 1], ALU.add))
                done(tt(m[:, :, W:W + 64], row[:, b, 0, :, 64:128], row[:, b, 1, :, 64:128], ALU.add))
                yr = e.ea4[:, bass.ds(r * G, G), 1:4] if L1 else y3[:, bass.ds(r * G, G), :]
                yr2 = e.ea4[:, bass.ds(r * G, G), 1:3] if L1 else y3[:, bass.ds(r * G, G), 0:2]
                done(nc.vector.tensor_copy(y5[:, b, :, 0:3], yr))
                done(nc.vector.tensor_copy(y5[:, b, :, 3:5], yr2))
                wait(dve, PW, r, "w")
                if L1:
                    done(tt(wy[:, :, :], ps_w[:, :, 0:96],
                            e.ea4[:, bass.ds(r * G, G), 0:1].to_broadcast([P, G, 96]), ALU.mult))
                wait(dve, VP, r, "y5b")
                v = comps(m[:, :, 64:224])
                done(tt(dot[:, :, :, :], v[:, :, 0:3], y_of(b, 0, 3, C1), ALU.mult))
                done(tt(t1[:, :, :, :], v[:, :, 1:4], y_of(b, 2, 3, C1), ALU.mult))
                done(tt(t2[:, :, :, :], v[:, :, 2:5], y_of(b, 1, 3, C1), ALU.mult))

            def product_b(r, b, n):
                done = steps_of(VP)
                v = comps(m[:, :, 64:224])
                xb = b if L1 else 0
                if not early(r, NX):
                    wait(dve, PX, r - NX, "x3")
                if L1:
                    wait(dve, VP, r, "wy")
                ws = wy if L1 else ps_w
                done(tt(x1[:, xb, :, 0:C0], m[:, :, 0:C0], ws[:, :, 0:C0], ALU.mult))
                done(tt(x23[:, xb, :, 0:C0], m[:, :, 0:C0], ps_w[:, :, 96:160], ALU.mult))
                done(tt(vectors(x23[:, xb], 0), v[:, :, 0:3], ws[:, :, 64:96].unsqueeze(2).to_broadcast([P, G, 3, C1]),
                        ALU.mult))
                wait(dve, VP, r, "dot")
                done(tt(dot[:, :, 0, :], dot[:, :, 0, :], dot[:, :, 1, :], ALU.add))
                wait(dve, VP, r, "t2")
                done(tt(t1[:, :, :, :], t1[:, :, :, :], t2[:, :, :, :], ALU.subtract))
                wait(dve, VP, r, "dot1")
                done(tt(dot[:, :, 0, :], dot[:, :, 0, :], dot[:, :, 2, :], ALU.add))
                wait(dve, VP, r, "t12")
                done(tt(vectors(x23[:, xb], 1), t1[:, :, :, :],
                        ps_w[:, :, 192:224].unsqueeze(2).to_broadcast([P, G, 3, C1]), ALU.mult))
                wait(dve, VP, r, "dot2")
                done(tt(x1[:, xb, :, 64:96], dot[:, :, 0, :], ps_w[:, :, 160:192], ALU.mult))

            def vectors(ap, k):
                return ap[:, :, 64:256].rearrange("p g (d k c) -> p g d k c", d=3, k=2)[:, :, :, k, :]

            def vec_out(done, steps, r, to, y):
                done(tt(to[:, :, :, :], ps_v[:, :, 0:32].unsqueeze(2).to_broadcast([P, G, 3, C1]), y, ALU.mult))
                wait(dve, steps, r, "zy")
                done(tt(to[:, :, :, :], to[:, :, :, :], comps(ps_v[:, :, 32:128]), ALU.add))
                wait(dve, steps, r, "bc")

            def joint(r, b, n):
                done = steps_of(VJ)
                dve.wait_ge(dst_in[b], 16 * (n + 1))
                if not early(r):
                    wait(dve, PJ, r - 2, "hi")
                done(dst_same(nc, dve, e, same, dst_b, r, b))
                wait(dve, PE_, r, "ex")
                wait(dve, *((PZ, r, "v") if L1 else (PM, r, "v")))
                if not early(r, 1):
                    wait(dve, AJ, r - 1, "shift")
                    wait(dve, VJ, r - 1, "w")
                done(nc.vector.tensor_copy(exs[:, :, :], ex_p))
                wait(dve, VJ, r, "exs")
                exb = exs[:, :, 0:H]
                done(nc.vector.tensor_copy(exv[:, :, :].rearrange("p g (h k) -> p g h k", h=H),
                                           exb.unsqueeze(3).to_broadcast([P, G, H, per_v])))
                done(tt(msg[:, b, :, 0:C0].rearrange("p g (h k) -> p g h k", h=H),
                        out_s.rearrange("p g (h k) -> p g h k", h=H),
                        exb.unsqueeze(3).to_broadcast([P, G, H, per_s]), ALU.mult))
                src = e.ea4[:, bass.ds(r * G, G), 1:4] if L1 else y3[:, bass.ds(r * G, G), :]
                vec_out(done, VJ, r, t3, src.unsqueeze(3).to_broadcast([P, G, 3, C1]))
                done(tt(comps(msg[:, b, :, C0:W]), t3[:, :, :, :],
                        exv[:, :, :].unsqueeze(2).to_broadcast([P, G, 3, C1]), ALU.mult))
                done(nc.vector.tensor_copy(msg[:, b, :, W:MW], exb))

            def bends(r, b, n):
                wait(dve, AM, r, "bend")
                if not early(r, 1):
                    wait(dve, PM, r - 1, "at")
                stt(out=bend[:, :], in0=soft[:, :], scalar=4.0 if L1 else 1.5, in1=ps_l[0:C0, :],
                    op0=ALU.mult if L1 else ALU.add, op1=ALU.add if L1 else ALU.mult).then_inc(VM.sem, 1)

            def second(r, b, n):
                done = steps_of(VM)
                wait(dve, PM, r, "v")
                if not last(r):
                    wait(dve, VP, r + 1, "o0b")
                vec_out(done, VM, r, t1, y_of(b, 0, 3, C1))
                wait(dve, AM, r, "gh")
                done(ts(gate[:, :, :], gh[:, :, :], 0.5, 0.5, ALU.mult, ALU.add))
                if not early(r, 1):
                    wait(dve, PZ, r - 1, "x3")
                done(ts(z23[:, :, 0:C0], sh[:, :, :], 0.5, 0.5, ALU.mult, ALU.add))
                wait(dve, VM, r, "gate")
                gb_ = gate[:, :, :].unsqueeze(2)
                done(tt(v5[:, :, 0:3, :], t1[:, :, :, :], gb_.to_broadcast([P, G, 3, C1]), ALU.mult))
                done(tt(v5[:, :, 3:5, :], t1[:, :, 0:2, :], gb_.to_broadcast([P, G, 2, C1]), ALU.mult))
                wait(dve, VM, r, "v5b")
                y0 = e.ea4[:, bass.ds(r * G, G), 0:1]
                done(tt(dot[:, :, :, :], v5[:, :, 0:3], y_of(b, 0, 3, C1), ALU.mult))
                done(tt(t1[:, :, :, :], v5[:, :, 1:4], y_of(b, 2, 3, C1), ALU.mult))
                done(tt(t2[:, :, :, :], v5[:, :, 2:5], y_of(b, 1, 3, C1), ALU.mult))
                done(tt(z1[:, :, 0:C0], z23[:, :, 0:C0], y0.to_broadcast([P, G, C0]), ALU.mult))
                done(tt(vectors(z23, 0), v5[:, :, 0:3], y0.unsqueeze(3).to_broadcast([P, G, 3, C1]), ALU.mult))
                wait(dve, VM, r, "dot")
                done(tt(dot[:, :, 0, :], dot[:, :, 0, :], dot[:, :, 1, :], ALU.add))
                wait(dve, VM, r, "t2")
                done(tt(vectors(z23, 1), t1[:, :, :, :], t2[:, :, :, :], ALU.subtract))
                wait(dve, VM, r, "dot1")
                done(tt(z1[:, :, 64:96], dot[:, :, 0, :], dot[:, :, 2, :], ALU.add))

            def shifts(r, b, n):
                done = steps_of(VM)
                wait(dve, PM, r, "at")
                dve.wait_ge(pen_in[b], 16 * (n + 1))
                done(nc.vector.tensor_tensor_scan(shf[:, b, :], pen[:, b, 0:SB], ps_l[0:H, :],
                                                  shf[:, 1 - b, SB - 1:SB], ALU.min, ALU.max))
                wait(dve, VM, r, "fwd")
                if not early(r, 1):
                    wait(dve, AE, r - 1, "sh2")
                done(nc.vector.tensor_tensor_scan(shb[:, ::-1], pen[:, b, SB:0:-1], shf[:, b, ::-1],
                                                  -BIG, ALU.min, ALU.max))
                wait(dve, VM, r, "bwd")
                done(tt(arg[:, :], ps_l[0:H, :], shb[:, :], ALU.subtract))

            rounds(dve, [(product_a, LP), (product_b, LP), (joint, LJ), (bends, LT), (second, LT), (shifts, LT)]
                   if L1 else
                   [(scaled(0), 1), (scaled(1), 3), (product_a, LP), (joint, LJ), (bends, LT), (product_b, LP),
                    (hidden(0), 1), (hidden(1), 3), (variance(0), 0), (variance(1), 2), (shifts, LT)], S)


def block_loads(big, cols, ws, wv):
    c = cols
    return [(big[0:64, 0, c:c + 64], ws), (big[64:96, 0, c + 64:c + 96], wv),
            (big[96:128, 0, c + 96:c + 128], wv), (big[0:32, 1, c + 128:c + 160], wv)]


def col_loads(col, j, s, v):
    s, v = s.rearrange("(p a) -> p a", a=1), v.rearrange("(p a) -> p a", a=1)
    return [(col[0:64, 0, j:j + 1], s), (col[64:96, 0, j:j + 1], v), (col[96:128, 0, j:j + 1], v),
            (col[0:32, 1, j:j + 1], v)]


def node_phase(nc, e, d, layer):
    prev = layer - 1
    tag = f"node{layer}_"
    join, opens = prev >= 0, layer < LAYERS
    H = {1: 4, 3: 8}.get(prev, 0)
    per_s, per_v = {1: (16, 8), 3: (8, 4)}.get(prev, (1, 1))
    DW = 384 if prev == 0 else W + 2 * H
    inner = layer in (1, 3)
    TW = 384 if layer == 2 else W
    OW = 0 if not opens else TW + W
    ffn = prev == 3
    parts = [(i, min(HW, DW - HW * i)) for i in range(-(-DW // HW))]
    nfetch = len(parts) + 1
    with ExitStack() as loc:
        def tmp(name, shape, dt=F32):
            return loc.enter_context(nc.sbuf_tensor(tag + name, shape, dt))

        sems = []

        def sem(name):
            sems.append(loc.enter_context(nc.semaphore(tag + name)))
            return sems[-1]

        def ps(name, shape):
            return loc.enter_context(nc.psum_tensor(tag + name, shape, F32))

        loadw, zeroed, prepped, biased, ready = (sem("weights_loaded"), sem("weights_zeroed"), sem("weights_ready"),
                                                 sem("bias_rows"), sem("bias_ready"))
        wload, wprep, wbias = [], [], []
        nz = 0
        if join:
            idx = tmp("idx", [P, 2, 2], I32)
            r_last = tmp("r_last", [P, 2, DW])
            r_carry = tmp("r_carry", [P, 2, DW])
            tot = tmp("tot", [P, DW])
            tot_t = tmp("tot_t", [P, 512])
            ps_t = ps("ps_t", [P, 512])
            ps_j = ps("ps_j", [P, 512])
            fj = tmp("fj", [P, 8])
            den = tmp("den", [P, 8])
            if prev == 0:
                wj = tmp("w_join", [96, 96])
            else:
                wj = tmp("w_join", [P, 2, W])
            if ffn:
                hrow = tmp("hrow", [P, 2, W])
                xp = tmp("xp", [P, W])
                st2 = tmp("st2", [P, 6])
                mv2 = tmp("mv2", [P, 2])
                ve2 = tmp("ve2", [P, 2])
                rs2 = tmp("rs2", [P, 2])
                sq2 = tmp("sq2", [P, 96])
                n2 = tmp("n2", [P, W])
                n2_t = tmp("n2_t", [P, 256])
                wf1 = tmp("w_f1", [P, 2, 384])
                bf1 = tmp("b_f1", [1, 384])
                bfj = tmp("b_j", [1, W])
                bf2 = tmp("b_f2", [1, W])
                wf2s = tmp("w_f2s", [P, 64])
                wf2v = tmp("w_f2v", [P, 2, 64])
                gcol2 = tmp("gcol2", [P, 2, 2])
                f1 = tmp("f1", [P, 384])
                th = tmp("th", [P, 192])
                f1_t = tmp("f1_t", [P, 3, P])
                ps_f = ps("ps_f", [P, 512])
                ps_g = ps("ps_g", [P, 512])
                oo = tmp("oo", [P, 2, W])
        if opens:
            st = tmp("st", [P, 6])
            mv = tmp("mv", [P, 2])
            ve = tmp("ve", [P, 1])
            rs = tmp("rs", [P, 1])
            h = tmp("h", [P, 2, W])
            h_t = tmp("h_t", [P, 2, 2 * P])
            tab = tmp("tab", [P, 2, OW])
            wo = tmp("w_open", [P, 2, OW])
            ps_h = ps("ps_h", [P, 512])
            ps_o = ps("ps_o", [P, 2, 512])
            if inner:
                sti = tmp("sti", [P, 6])
                mvi = tmp("mvi", [P, 2])
                vei = tmp("vei", [P, 2])
                rsi = tmp("rsi", [P, 2])
                sqi = tmp("sqi", [P, 96])
                hn = tmp("hn", [P, W])
                gcol = tmp("gcol", [P, 2, 2])
                brow = tmp("brow", [1, 2 * W])
        if join:
            J = Steps(sem("vec_join"),
                      {0: ["tot", "y", "x"], 2: ["tot", "x"]}.get(prev, None) or
                      ["d", "dm", "cs", "cv", "cd", "tot", "den", "rden", "ns", "nv"] +
                      (["x"] if not ffn else
                       ["xp", "st", "mv", "ve", "sq", "s", "v", "f1", "th", "sc", "fv", "o1", "oo"]))
            PJ = Steps(sem("pe_join"), ["t", "j"] + (["t2", "f1", "t3", "f2"] if ffn else []))
            AJ = Steps(sem("act_join"), (["exp"] if H else []) + ["t"] + (["t2", "tanh", "t3"] if ffn else []))
            KJ = Steps(sem("pool_join"), ["idx", "idx2"] + (["rs"] if ffn else []))
            joined_in = [e.pool_dma_sem(tag + f"joined_in{b}") for b in range(2)]
            h_in = [sem(f"h_in{b}") for b in range(2)]
            oo_sent = [sem(f"oo_sent{b}") for b in range(2)]
        if opens:
            O = Steps(sem("vec_open"), ["st", "mv", "ve", "c", "h"] +
                      (["sti", "mvi", "vei", "sq", "ns", "nv"] if inner else []) + ["tab", "x"])
            PO = Steps(sem("pe_open"), ["t", "o"])
            AO = Steps(sem("act_open"), ["t1", "t2"])
            KO = Steps(sem("pool_open"), ["rs"] + (["rsi"] if inner else []))
            tab_sent = [sem(f"tab_sent{b}") for b in range(2)]
            h_sent = [sem(f"h_sent{b}") for b in range(2)]
            ntab = {0: 1, 1: 2, 2: 1, 3: 2}[layer]

        zero = []
        c3 = lambda ap: ap.rearrange("(a b) -> a b", a=1)
        if join and prev == 0:
            wload += [(wj[0:64, 0:64], d["L0_gnn_W_l2_00"]), (wj[64:96, 0:64], d["L0_gnn_W_l2_10"]),
                      (wj[0:64, 64:96], d["L0_gnn_W_l2_01"]), (wj[64:96, 64:96], d["L0_gnn_W_l2_11"])]
            k0 = 0.25 * 0.5 / float(np.sqrt(96.0))
            wprep += [(wj[:, :], k0), (wj[64:96, 0:64], 1.0 / float(np.sqrt(3.0)))]
        elif join:
            zero += [wj[:, :, :]]
            if prev == 1:
                wload += block_loads(wj, 0, d["L1_gnn_Wps"], d["L1_gnn_Wpv"])
            elif prev == 2:
                wload += block_loads(wj, 0, d["L2_gnn_L_s"], d["L2_gnn_L_v"])
                wprep += [(wj[:, :, 0:64], 0.125), (wj[:, :, 64:160], 1.0 / float(np.sqrt(32.0)))]
            else:
                wload += block_loads(wj, 0, d["L3_gnn_proj_ws"], d["L3_gnn_proj_wv"])
                zero += [wf1[:, :, :], bf1[:, :], bfj[:, :], bf2[:, :], wf2v[:, :, :]]
                f1v, f2v = d["L3_gnn_f1_wv"], d["L3_gnn_f2_wv"]
                wload += [(wf1[0:64, 0, 0:192], d["L3_gnn_f1_ws"]), (wf1[64:96, 0, 192:256], f1v),
                          (wf1[96:128, 0, 256:320], f1v), (wf1[0:32, 1, 320:384], f1v),
                          (bf1[:, 0:192], c3(d["L3_gnn_f1_bs"])), (bfj[:, 0:64], c3(d["L3_gnn_proj_bs"])),
                          (bf2[:, 0:64], c3(d["L3_gnn_f2_bs"])), (wf2s[:, :], d["L3_gnn_f2_ws"]),
                          (wf2v[0:64, 0, 0:32], f2v), (wf2v[64:128, 0, 32:64], f2v), (wf2v[0:64, 1, 0:32], f2v)]
                wload += col_loads(gcol2, 0, d["L3_gnn_ln2_w0"], d["L3_gnn_ln2_w1"])
                zero += [gcol2[:, :, :]]
                wload += [(gcol2[0:64, 0, 1:2], d["L3_gnn_ln2_b0"].rearrange("(p a) -> p a", a=1))]
                wbias += [(gcol2, wf1, bf1, 384)]
        if opens:
            zero += [wo[:, :, :]]
            if layer == 0:
                wload += block_loads(wo, 0, d["L0_gnn_W_l1_0"], d["L0_gnn_W_l1_1"])
                wload += block_loads(wo, W, d["L0_gnn_W_si0"], d["L0_gnn_W_si1"])
                for c in (0, W):
                    wprep += [(wo[:, :, c:c + 64], 0.125), (wo[:, :, c + 64:c + 160], 1.0 / float(np.sqrt(32.0)))]
            elif layer == 1:
                wload += block_loads(wo, 0, d["L1_gnn_Ws_src"], d["L1_gnn_Wv_src"])
                wload += block_loads(wo, W, d["L1_gnn_Ws_dst"], d["L1_gnn_Wv_dst"])
                wload += col_loads(gcol, 0, d["L1_gnn_gamma_s"], d["L1_gnn_gamma_v"])
                wload += [(gcol[0:64, 0, 1:2], d["L1_gnn_beta_s"].rearrange("(p a) -> p a", a=1))]
            elif layer == 2:
                vv, sv, vs = d["L2_gnn_W_vv"], d["L2_gnn_W_sv"], d["L2_gnn_W_vs"]
                rows = [(0, 64, 96), (0, 96, 128), (1, 0, 32)]
                wload += [(wo[0:64, 0, 0:64], d["L2_gnn_W_ss"]), (wo[0:64, 0, 256:288], sv)]
                for i, (k, a, b) in enumerate(rows):
                    wload += [(wo[a:b, k, 64 + 64 * i:128 + 64 * i], vv),
                              (wo[a:b, k, 288 + 32 * i:320 + 32 * i], vs)]
                wload += block_loads(wo, 384, d["L2_gnn_L_s"], d["L2_gnn_L_v"])
                i2, i3 = 1.0 / float(np.sqrt(2.0)), 1.0 / float(np.sqrt(3.0))
                r32 = 1.0 / float(np.sqrt(32.0))
                wprep += [(wo[:, :, 0:64], 0.125 * i2), (wo[:, :, 64:256], i3 * r32 * i2),
                          (wo[:, :, 256:288], i3 * 0.125 * i2), (wo[:, :, 288:384], i3 * r32 * i2),
                          (wo[:, :, 384:448], 0.125), (wo[:, :, 448:544], r32)]
            else:
                wload += block_loads(wo, 0, d["L3_gnn_msrc_ws"], d["L3_gnn_msrc_wv"])
                wload += block_loads(wo, W, d["L3_gnn_mdst_ws"], d["L3_gnn_mdst_wv"])
                wload += col_loads(gcol, 0, d["L3_gnn_ln1_w0"], d["L3_gnn_ln1_w1"])
                wload += [(gcol[0:64, 0, 1:2], d["L3_gnn_ln1_b0"].rearrange("(p a) -> p a", a=1)),
                          (brow[:, W:W + 64], c3(d["L3_gnn_mdst_bs"]))]
            if inner:
                zero += [gcol[:, :, :], brow[:, :]]
                wbias += [(gcol, wo, brow, 2 * W)]
        nprep = len(wprep) + 3 * len(wbias)
        loc.callback(clear, nc, sems)
        block = loc.enter_context(nc.Block())

        @block.sync
        def _(sp):
            sp.wait_ge(zeroed, len(zero)) if zero else None
            load_blocks(sp, loadw, wload)

            def fetch_h(r, b, n):
                if not early(r):
                    wait(sp, J, r - 2, "xp")
                sp.dma_start(hrow[:, b], e.h3[bass.ds(r * P, P), :]).then_inc(h_in[b], 16)

            def store_out(r, b, n):
                wait(sp, J, r, "oo")
                sp.dma_start(d["out"][bass.ds(r * P, P), :], oo[:, b]).then_inc(oo_sent[b], 16)

            def store_tab(r, b, n):
                wait(sp, O, r, "tab")
                sp.dma_start(e.tsrc[layer][bass.ds(r * P, P), :], tab[:, b, 0:TW]).then_inc(tab_sent[b], 16)
                if inner:
                    sp.dma_start(e.tdst[bass.ds(r * P, P), :], tab[:, b, W:2 * W]).then_inc(tab_sent[b], 16)
                if layer == 3:
                    sp.dma_start(e.h3[bass.ds(r * P, P), :], h[:, b]).then_inc(h_sent[b], 16)

            if ffn:
                rounds(sp, [(fetch_h, 0), (store_out, 2)], NT)
                for b in range(2):
                    sp.wait_ge(oo_sent[b], 16 * (NT // 2))
            else:
                rounds(sp, [(store_tab, 2)], NT)
                for b in range(2):
                    sp.wait_ge(tab_sent[b], 16 * ntab * (NT // 2))
                    if layer == 3:
                        sp.wait_ge(h_sent[b], 16 * (NT // 2))

        @block.gpsimd
        def _(pool):
            for z in zero:
                pool.memset(z, 0.0).then_inc(zeroed, 1)

            def fetch(r, b, n):
                if not early(r):
                    wait(pool, J, r - 2, "tot")
                    pool.wait_ge(joined_in[b], 16 * nfetch * n)
                    pool.nop(nofuse=True)
                nc.gpsimd.tensor_copy(idx[:, b, 0:1], e.last[:, bass.ds(r, 1)]).then_inc(KJ.sem, 1)
                nc.gpsimd.tensor_copy(idx[:, b, 1:2], e.carry[:, bass.ds(r, 1)]).then_inc(KJ.sem, 1)
                wait(pool, KJ, r, "idx2")
                pool.nop(nofuse=True)
                for i, w in parts:
                    pool.indirect_dma_start(r_last[:, b, HW * i:HW * i + w], None, e.rows[prev][i],
                                            bass.IndirectOffsetOnAxis(ap=idx[:, b, 0:1], axis=0))\
                        .then_inc(joined_in[b], 16)
                pool.indirect_dma_start(r_carry[:, b, :], None, e.carries[prev],
                                        bass.IndirectOffsetOnAxis(ap=idx[:, b, 1:2], axis=0))\
                        .then_inc(joined_in[b], 16)

            def power(r, b, n):
                wait(pool, O, r, "ve")
                nc.gpsimd.tensor_tensor(rs[:, :], ve[:, :], e.mhalf[:, 0:1], ALU.pow).then_inc(KO.sem, 1)
                if inner:
                    wait(pool, O, r, "sq")
                    nc.gpsimd.tensor_tensor(rsi[:, :], vei[:, :], e.mhalf[:, 0:2], ALU.pow).then_inc(KO.sem, 1)

            def power2(r, b, n):
                wait(pool, J, r, "sq")
                nc.gpsimd.tensor_tensor(rs2[:, :], ve2[:, :], e.mhalf[:, 0:2], ALU.pow).then_inc(KJ.sem, 1)

            rounds(pool, ([(fetch, 0)] if join else []) + ([(power, 1 if join else 0)] if opens else []) +
                   ([(power2, 0)] if ffn else []), NT)

        @block.tensor
        def _(pe):
            for k, (g, w, row, n) in enumerate(wbias):
                pe.wait_ge(loadw, 16 * len(wload))
                if k == 0 and wprep:
                    pe.wait_ge(prepped, len(wprep))
                t = ps_f if ffn else ps_h
                nc.tensor.matmul(t[0:1, 0:n], g[:, 0, 1:2], w[:, 0, 0:n], start=True, stop=False)
                nc.tensor.matmul(t[0:1, 0:n], g[0:32, 1, 1:2], w[0:32, 1, 0:n], start=False, stop=True)\
                    .then_inc(biased, 1)
            pe.wait_ge(prepped, nprep)

            def joins(r, b, n):
                wait(pe, J, r, "tot" if not H else "nv")
                if not early(r, 1):
                    wait(pe, AJ, r - 1, "t")
                if prev == 0:
                    for k in range(4):
                        mm = nc.tensor.transpose(ps_t[0:96, k * P:(k + 1) * P], tot[:, 96 * k:96 * k + 96],
                                                 e.ident[:, :])
                else:
                    nc.tensor.transpose(ps_t[:, 0:P], tot[:, 0:P], e.ident[:, :])
                    mm = nc.tensor.transpose(ps_t[0:32, P:2 * P], tot[:, P:W], e.ident[:, :])
                mm.then_inc(PJ.sem, 1)
                wait(pe, AJ, r, "t")
                if not early(r, 1):
                    wait(pe, J, r - 1, "xp" if ffn else "x" if prev else "y")
                if prev == 0:
                    for k in range(4):
                        o = ps_j[:, 0:64] if k == 0 else ps_j[:, 32 + 32 * k:64 + 32 * k]
                        mm = nc.tensor.matmul(o, tot_t[0:96, k * P:(k + 1) * P],
                                              wj[:, 0:64] if k == 0 else wj[:, 64:96], start=True, stop=True)
                else:
                    nc.tensor.matmul(ps_j[:, 0:W], tot_t[:, 0:P], wj[:, 0, :], start=True, stop=False)
                    mm = nc.tensor.matmul(ps_j[:, 0:W], tot_t[0:32, P:2 * P], wj[0:32, 1, :], start=False,
                                          stop=not ffn)
                    if ffn:
                        mm = nc.tensor.matmul(ps_j[:, 0:W], e.ones[0:1, :], bfj[:, :], start=False, stop=True)
                mm.then_inc(PJ.sem, 1)
                if ffn:
                    wait(pe, J, r, "v")
                    nc.tensor.transpose(ps_t[:, 0:P], n2[:, 0:P], e.ident[:, :])
                    nc.tensor.transpose(ps_t[0:32, P:2 * P], n2[:, P:W], e.ident[:, :]).then_inc(PJ.sem, 1)
                    wait(pe, AJ, r, "t2")
                    nc.tensor.matmul(ps_f[:, 0:384], n2_t[:, 0:P], wf1[:, 0, :], start=True, stop=False)
                    nc.tensor.matmul(ps_f[:, 0:384], n2_t[0:32, P:2 * P], wf1[0:32, 1, :], start=False, stop=False)
                    nc.tensor.matmul(ps_f[:, 0:384], e.ones[0:1, :], bf1[:, :], start=False, stop=True)\
                        .then_inc(PJ.sem, 1)
                    wait(pe, J, r, "fv")
                    nc.tensor.transpose(ps_t[:, 0:P], f1[:, 0:P], e.ident[:, :])
                    nc.tensor.transpose(ps_t[:, P:2 * P], f1[:, 192:320], e.ident[:, :])
                    nc.tensor.transpose(ps_t[0:64, 2 * P:3 * P], f1[:, 320:384], e.ident[:, :]).then_inc(PJ.sem, 1)
                    wait(pe, AJ, r, "t3")
                    nc.tensor.matmul(ps_g[:, 0:64], f1_t[:, 0, :], wf2s[:, :], start=True, stop=False)
                    nc.tensor.matmul(ps_g[:, 0:64], e.ones[0:1, :], bf2[:, 0:64], start=False, stop=True)
                    nc.tensor.matmul(ps_g[:, 64:128], f1_t[:, 1, :], wf2v[:, 0, :], start=True, stop=True)
                    nc.tensor.matmul(ps_g[:, 128:160], f1_t[0:64, 2, :], wf2v[0:64, 1, 0:32], start=True, stop=True)\
                        .then_inc(PJ.sem, 1)

            def opening(r, b, n):
                wait(pe, O, r, "nv" if inner else "h")
                src = hn[:, :] if inner else h[:, b]
                if not early(r, 1):
                    wait(pe, AO, r - 1, "t2")
                nc.tensor.transpose(ps_h[:, 0:P], src[:, 0:P], e.ident[:, :])
                nc.tensor.transpose(ps_h[0:32, P:2 * P], src[:, P:W], e.ident[:, :]).then_inc(PO.sem, 1)
                wait(pe, AO, r, "t2")
                if not early(r, 1):
                    wait(pe, O, r - 1, "x")
                for o, c0, cw in ((0, 0, TW), (1, TW, W)):
                    nc.tensor.matmul(ps_o[:, o, 0:cw], h_t[:, b, 0:P], wo[:, 0, c0:c0 + cw], start=True, stop=False)
                    mm = nc.tensor.matmul(ps_o[:, o, 0:cw], h_t[0:32, b, P:2 * P], wo[0:32, 1, c0:c0 + cw],
                                          start=False, stop=not inner)
                    if inner:
                        mm = nc.tensor.matmul(ps_o[:, o, 0:cw], e.ones[0:1, :], brow[:, c0:c0 + cw],
                                              start=False, stop=True)
                mm.then_inc(PO.sem, 1)

            rounds(pe, ([(joins, 0)] if join else []) + ([(opening, 1 if join else 0)] if opens else []), NT)

        @block.scalar
        def _(act):
            def joins(r, b, n):
                if H:
                    wait(act, J, r, "dm")
                    nc.scalar.activation(fj[:, 0:H], fj[:, 0:H], ACT.Exp).then_inc(AJ.sem, 1)
                wait(act, PJ, r, "t")
                if not early(r, 1):
                    wait(act, PJ, r - 1, "j")
                if prev == 0:
                    nc.scalar.copy(tot_t[0:96, :], ps_t[0:96, :]).then_inc(AJ.sem, 1)
                else:
                    nc.scalar.copy(tot_t[:, 0:P], ps_t[:, 0:P]).then_inc(ready, 1)
                    nc.scalar.copy(tot_t[0:32, P:2 * P], ps_t[0:32, P:2 * P]).then_inc(AJ.sem, 1)
                if ffn:
                    wait(act, PJ, r, "t2")
                    nc.scalar.copy(n2_t[:, 0:P], ps_t[:, 0:P]).then_inc(ready, 1)
                    nc.scalar.copy(n2_t[0:32, P:2 * P], ps_t[0:32, P:2 * P]).then_inc(AJ.sem, 1)
                    wait(act, J, r, "f1")
                    nc.scalar.activation(th[:, :], f1[:, 0:192], ACT.Tanh, scale=0.5).then_inc(AJ.sem, 1)
                    wait(act, PJ, r, "t3")
                    nc.scalar.copy(f1_t[:, 0:2, :], ps_t[:, 0:2 * P].rearrange("p (a b) -> p a b", a=2))\
                        .then_inc(ready, 1)
                    nc.scalar.copy(f1_t[0:64, 2, :], ps_t[0:64, 2 * P:3 * P]).then_inc(AJ.sem, 1)

            def opening(r, b, n):
                wait(act, PO, r, "t")
                if not early(r):
                    wait(act, PO, r - 2, "o")
                nc.scalar.copy(h_t[:, b, 0:P], ps_h[:, 0:P]).then_inc(AO.sem, 1)
                nc.scalar.copy(h_t[0:32, b, P:2 * P], ps_h[0:32, P:2 * P]).then_inc(AO.sem, 1)

            rounds(act, ([(joins, 0)] if join else []) + ([(opening, 1 if join else 0)] if opens else []), NT)

        @block.vector
        def _(dve):
            tt, ts = nc.vector.tensor_tensor, nc.vector.tensor_scalar
            dve.wait_ge(loadw, 16 * len(wload))
            for k, (ap, c) in enumerate(wprep):
                dve.wait_ge(prepped, k) if k else None
                ts(ap, ap, c, None, ALU.mult).then_inc(prepped, 1)
            m = len(wprep)
            for k, (g, w, row, n) in enumerate(wbias):
                dve.wait_ge(biased, k + 1)
                t = ps_f if ffn else ps_h
                tt(row[0:1, 0:n], row[0:1, 0:n], t[0:1, 0:n], ALU.add).then_inc(prepped, 1)
                ts(w[:, 0, 0:n], w[:, 0, 0:n], g[:, 0, 0:1], None, ALU.mult).then_inc(prepped, 1)
                ts(w[0:32, 1, 0:n], w[0:32, 1, 0:n], g[0:32, 1, 0:1], None, ALU.mult).then_inc(prepped, 1)
                m += 3

            def xs(r):
                return e.x[:, bass.ds(r, 1), :].rearrange("p a w -> p (a w)")

            def attr(r, n):
                return e.attr[:, bass.ds(r, 1)].to_broadcast([P, n])

            def heads(ap, f):
                return ((ap[:, 0:C0].rearrange("p (h k) -> p h k", h=H),
                         f[:, 0:H].unsqueeze(2).to_broadcast([P, H, per_s])),
                        (ap[:, C0:W].rearrange("p (c h k) -> p c h k", c=3, h=H),
                         f[:, 0:H].unsqueeze(1).unsqueeze(3).to_broadcast([P, 3, H, per_v])))

            def joins(r, b, n):
                def done(ins):
                    ins.then_inc(J.sem, 1)

                dve.wait_ge(joined_in[b], 16 * nfetch * (n + 1))
                if not early(r, 1):
                    wait(dve, J, r - 1, J.names[-1])
                D, C = r_last[:, b], r_carry[:, b]
                if not early(r, 1):
                    wait(dve, PJ, r - 1, "t")
                if H:
                    done(tt(fj[:, 0:H], C[:, W + H:W + 2 * H], D[:, W + H:W + 2 * H], ALU.subtract))
                    wait(dve, J, r, "d")
                    done(ts(fj[:, 0:H], fj[:, 0:H], 0.0, None, ALU.min))
                    wait(dve, AJ, r, "exp")
                    for v, f in heads(C, fj):
                        done(tt(v, v, f, ALU.mult))
                    done(tt(C[:, W:W + H], C[:, W:W + H], fj[:, 0:H], ALU.mult))
                    wait(dve, J, r, "cd")
                    done(tt(tot[:, 0:W + H], D[:, 0:W + H], C[:, 0:W + H], ALU.add))
                    wait(dve, J, r, "tot")
                    done(ts(den[:, 0:H], tot[:, W:W + H], 1e-16 if prev == 1 else 1e-12, None, ALU.add))
                    wait(dve, J, r, "den")
                    done(nc.vector.reciprocal(den[:, 0:H], den[:, 0:H]))
                    wait(dve, J, r, "rden")
                    for v, f in heads(tot, den):
                        done(tt(v, v, f, ALU.mult))
                else:
                    done(tt(tot[:, :], D, C, ALU.add))
                wait(dve, PJ, r, "j")
                if prev == 0:
                    done(tt(tot[:, 0:W], ps_j[:, 0:W], attr(r, W), ALU.mult))
                    wait(dve, J, r, "y")
                    done(tt(xs(r), xs(r), tot[:, 0:W], ALU.add))
                elif not ffn:
                    done(tt(xs(r), xs(r), ps_j[:, 0:W], ALU.add))
                else:
                    dve.wait_ge(h_in[b], 16 * (n + 1))
                    done(tt(xp[:, :], hrow[:, b], ps_j[:, 0:W], ALU.add))
                    wait(dve, J, r, "xp")
                    done(nc.vector.bn_stats(st2[:, :], xp[:, 0:C0]))
                    wait(dve, J, r, "st")
                    dve.nop(nofuse=True)
                    done(nc.vector.bn_aggr(mv2[:, :], st2[:, :]))
                    wait(dve, J, r, "mv")
                    done(ts(ve2[:, 0:1], mv2[:, 1:2], EPS, None, ALU.add))
                    done(nc.vector.tensor_tensor_reduce(out=sq2[:, :], in0=xp[:, C0:W], in1=xp[:, C0:W],
                                                        scale=1.0 / 96, scalar=EPS, op0=ALU.mult, op1=ALU.add,
                                                        accum_out=ve2[:, 1:2]))
                    wait(dve, KJ, r, "rs")
                    done(ts(n2[:, 0:C0], xp[:, 0:C0], mv2[:, 0:1], rs2[:, 0:1], ALU.subtract, ALU.mult))
                    done(ts(n2[:, C0:W], xp[:, C0:W], rs2[:, 1:2], None, ALU.mult))
                    wait(dve, PJ, r, "f1")
                    done(tt(f1[:, :], ps_f[:, 0:384], attr(r, 384), ALU.mult))
                    wait(dve, AJ, r, "tanh")
                    done(ts(th[:, :], th[:, :], 0.5, 0.5, ALU.mult, ALU.add))
                    wait(dve, J, r, "th")
                    done(tt(f1[:, 0:128], f1[:, 0:128], th[:, 0:128], ALU.mult))
                    fv = f1[:, 192:384].rearrange("p (c k) -> p c k", c=3)
                    done(tt(fv, fv, th[:, 128:192].unsqueeze(1).to_broadcast([P, 3, 64]), ALU.mult))
                    wait(dve, PJ, r, "f2")
                    if not early(r):
                        dve.wait_ge(oo_sent[b], 16 * n)
                    done(tt(oo[:, b], ps_g[:, 0:W], attr(r, W), ALU.mult))
                    dve.wait_ge(J.sem, J.at(r, "o1"))
                    tt(oo[:, b], oo[:, b], xp[:, :], ALU.add).then_inc(zeroed, 1)
                    dve.wait_ge(zeroed, len(zero) + r + 1)
                    done(tt(oo[:, b], oo[:, b], xs(r), ALU.add))

            def opening(r, b, n):
                def done(ins):
                    ins.then_inc(O.sem, 1)

                if join:
                    wait(dve, J, r, J.names[-1])
                if not early(r, 1):
                    wait(dve, O, r - 1, O.names[-1])
                dve.nop(nofuse=True)
                done(nc.vector.bn_stats(st[:, :], xs(r)))
                wait(dve, O, r, "st")
                dve.nop(nofuse=True)
                done(nc.vector.bn_aggr(mv[:, :], st[:, :]))
                wait(dve, O, r, "mv")
                done(ts(ve[:, :], mv[:, 1:2], EPS, None, ALU.add))
                wait(dve, KO, r, "rs")
                if not early(r):
                    wait(dve, PO, r - 2, "t")
                    if layer == 3:
                        dve.wait_ge(h_sent[b], 16 * n)
                done(ts(h[:, b], xs(r), mv[:, 0:1], rs[:, 0:1], ALU.subtract, ALU.mult))
                wait(dve, O, r, "c")
                done(ts(h[:, b], h[:, b], 0.0, None, ALU.max))
                if inner:
                    wait(dve, O, r, "h")
                    done(nc.vector.bn_stats(sti[:, :], h[:, b, 0:C0]))
                    wait(dve, O, r, "sti")
                    dve.nop(nofuse=True)
                    done(nc.vector.bn_aggr(mvi[:, :], sti[:, :]))
                    wait(dve, O, r, "mvi")
                    done(ts(vei[:, 0:1], mvi[:, 1:2], EPS, None, ALU.add))
                    done(nc.vector.tensor_tensor_reduce(out=sqi[:, :], in0=h[:, b, C0:W], in1=h[:, b, C0:W],
                                                        scale=1.0 / (32 if layer == 1 else 96), scalar=EPS,
                                                        op0=ALU.mult, op1=ALU.add, accum_out=vei[:, 1:2]))
                    wait(dve, KO, r, "rsi")
                    if not early(r, 1):
                        wait(dve, PO, r - 1, "t")
                    done(ts(hn[:, 0:C0], h[:, b, 0:C0], mvi[:, 0:1], rsi[:, 0:1], ALU.subtract, ALU.mult))
                    done(ts(hn[:, C0:W], h[:, b, C0:W], rsi[:, 1:2], None, ALU.mult))
                wait(dve, PO, r, "o")
                if not early(r):
                    dve.wait_ge(tab_sent[b], 16 * ntab * n)
                if layer == 0:
                    done(tt(tab[:, b, 0:W], ps_o[:, 0, 0:W], attr(r, W), ALU.mult))
                    tt(tab[:, b, W:2 * W], ps_o[:, 1, 0:W], attr(r, W), ALU.mult).then_inc(zeroed, 1)
                    dve.wait_ge(zeroed, len(zero) + r + 1)
                    done(tt(xs(r), xs(r), tab[:, b, W:2 * W], ALU.add))
                elif layer == 2:
                    done(nc.vector.tensor_copy(tab[:, b, 0:TW], ps_o[:, 0, 0:TW]))
                    done(tt(xs(r), xs(r), ps_o[:, 1, 0:W], ALU.add))
                else:
                    done(nc.vector.tensor_copy(tab[:, b, 0:2 * W].rearrange("p (a w) -> p a w", a=2),
                                               ps_o[:, :, 0:W]))
                    done(tt(xs(r), xs(r), h[:, b], ALU.add) if layer == 1 else
                         nc.vector.memset(sqi[:, 0:1], 0.0))

            rounds(dve, ([(joins, 0)] if join else []) + ([(opening, 1 if join else 0)] if opens else []), NT)


def build(nc, d):
    with ExitStack() as ctx:
        ctx.enter_context(nc.allow_non_contiguous_dma(reason="columns of a few words, read once"))
        e = setup(nc, ctx, d)
        for layer in range(LAYERS + 1):
            node_phase(nc, e, d, layer)
            if layer == LAYERS:
                break
            if layer in (0, 2):
                edge_conv(nc, e, d, layer)
                carry_phase(nc, e, layer, 384 if layer == 0 else W)
            else:
                edge_attention(nc, e, d, layer)
                H = 4 if layer == 1 else 8
                carry_phase(nc, e, layer, W + 2 * H, H, C0 // H, C1 // H)


def kernel(**inputs):
    import concourse.bacc as _bacc
    from concourse.bass_utils import run_bass_kernel_spmd as _run

    a = {k: np.asarray(v) for k, v in inputs.items()}

    def pad(v, rows, fill=0):
        out = np.full((rows,) + v.shape[1:], fill, v.dtype)
        out[:len(v)] = v
        return out

    def cols(v):
        return np.ascontiguousarray(np.swapaxes(v.reshape(T, P, *v.shape[1:]), 0, 1))

    def comp_major(v):
        tail = v[..., C0:].reshape(*v.shape[:-1], C1, 3)
        return np.concatenate([v[..., :C0], np.swapaxes(tail, -1, -2).reshape(*v.shape[:-1], 3 * C1)], -1)

    def with_ones(v):
        return np.concatenate([v, np.ones((1,) + v.shape[1:], v.dtype)], 0)

    dst = pad(a["dst"], EP, N)
    arrays = {
        "x": np.ascontiguousarray(np.swapaxes(pad(comp_major(a["x"]), NP).reshape(NT, P, W), 0, 1)),
        "attr": np.ascontiguousarray(pad(a["node_vec1"][:, 0], NP).reshape(NT, P).T),
        "src_cols": cols(pad(a["src"], EP)),
        "dst_cols": cols(dst),
        "dst_rows": dst.reshape(1, EP),
        "dst_run": np.concatenate([np.array([-1], dst.dtype), dst, np.full(EP // P, -1, dst.dtype)]),
        "ea4_cols": cols(pad(a["edge_attr_4"], EP)),
        "ea3_cols": cols(pad(a["edge_attr_3"], EP, 1)),
        "ea10_rows": np.ascontiguousarray(pad(a["edge_attr_10"], EP).T),
        "ea16_rows": with_ones(pad(a["edge_attr_16"], EP).T),
        "ea64_rows": with_ones(pad(a["edge_attr_64"], EP).T),
    }
    arrays["L2_rad"] = comp_major(np.concatenate([a["L2_gnn_W_rad"].T, a["L2_gnn_b_rad"][None]]))
    for k, v in a.items():
        if "_gnn_" in k:
            arrays[k] = v
    arrays = {k: np.ascontiguousarray(v) for k, v in arrays.items()}
    nc = _bacc.Bacc("TRN2", target_bir_lowering=False, num_devices=1)
    d = {k: nc.dram_tensor(f"in_{k}", v.shape, mybir.dt.from_np(v.dtype), kind="ExternalInput").ap()
         for k, v in arrays.items()}
    d["out"] = nc.dram_tensor("out_nodes", (NP, W), F32, kind="ExternalOutput").ap()
    build(nc, d)
    r = _run(nc, [{f"in_{k}": v for k, v in arrays.items()}], core_ids=[0])
    got = np.asarray(r.results[0]["out_nodes"])[:N]
    tail = np.swapaxes(got[:, C0:].reshape(N, 3, C1), 1, 2).reshape(N, 3 * C1)
    return np.concatenate([got[:, :C0], tail], 1)
```

```python
from contextlib import ExitStack

import numpy as np

import concourse.bass as bass
from concourse import mybir

F32 = mybir.dt.float32
BF16 = mybir.dt.bfloat16
I32 = mybir.dt.int32
ALU = mybir.AluOpType
ACT = mybir.ActivationFunctionType
AX = mybir.AxisListType

P = 128
N = 12500
NT = -(-N // P)
NP = NT * P
E = 200000
G = 4
SB = G * P
S = -(-E // (2 * SB)) * 2
T = S * G
EP = T * P
C0, C1 = 64, 32
W = C0 + 3 * C1
EPS = 1e-5
BIG = 1e30
LAYERS = 4

HW = 192
HEADS = (0, 4, 0, 8)
ROW_W = (384, W + 2 * 4, W, W + 2 * 8)
ZERO_ROW = EP
ZERO_CARRY = T + 1


class Steps:

    def __init__(self, sem, names):
        self.sem, self.names, self.n = sem, names, len(names)

    def at(self, r, name):
        return r * self.n + (self.names.index(name) + 1)




def wait(eng, steps, r, name):
    eng.wait_ge(steps.sem, steps.at(r, name))


def rounds(eng, stages, total):
    lag = max(l for _, l in stages)

    def turn(i, par, k):
        for fn, l in stages:
            if not isinstance(i, int) or 0 <= i - l < total:
                fn(i - l, (par - l) % 2, k + (par - l) // 2)

    head = lag + 2
    head += head % 2
    tail = total - (total - head) % 2
    for i in range(head):
        turn(i, i % 2, i // 2)
    with eng.Fori(head // 2, tail // 2) as k:
        turn(2 * k, 0, k)
        turn(2 * k + 1, 1, k)
    for i in range(tail, total + lag):
        turn(i, i % 2, i // 2)


def early(r, n=2):
    return isinstance(r, int) and r < n


class Env:
    pass


def clear(nc, sems):
    with nc.Block() as block:
        @block.gpsimd
        def _(pool):
            for s in sems:
                pool.sem_clear(s)


def load_blocks(sp, sem, pairs):
    for out, src in pairs:
        sp.dma_start(out, src).then_inc(sem, 16)
    return 16 * len(pairs)


def setup(nc, ctx, d):
    e = Env()

    def pool_dma_sem(name):
        return ctx.enter_context(nc.semaphore(name))

    e.pool_dma_sem = pool_dma_sem
    tag = "setup_"

    def sb(name, shape, dt=F32):
        return ctx.enter_context(nc.sbuf_tensor(tag + name, shape, dt))

    e.x = sb("x_nodes", [P, NT, W])
    e.src = sb("src_cols", [P, T], I32)
    e.dst = sb("dst_cols", [P, T], I32)
    e.ea4 = sb("ea4_cols", [P, T, 4])
    e.chain = sb("chain", [P, T])
    e.last = sb("last_row", [P, NT], I32)
    e.carry = sb("carry_row", [P, NT], I32)
    e.ident = sb("ident", [P, P])
    e.ones = sb("ones", [P, P])
    e.mhalf = sb("minus_half", [P, 8])
    e.attr = sb("node_attr", [P, NT])
    e.rows, e.carries, e.tsrc = [], [], []
    for layer, w in enumerate(ROW_W):
        e.rows.append([nc.dram_tensor(f"edge_rows{layer}_{i}", [EP + 1, min(w, HW)], F32, kind="Internal").ap()
                       for i in range(-(-w // HW))])
        e.carries.append(nc.dram_tensor(f"carry_rows{layer}", [T + 2, w], F32, kind="Internal").ap())
        e.tsrc.append(nc.dram_tensor(f"table_src{layer}", [NP, 384 if layer == 2 else W], F32,
                                     kind="Internal").ap())
    e.tdst = nc.dram_tensor("table_dst", [NP, W], F32, kind="Internal").ap()
    e.pens = nc.dram_tensor("resets", [EP + P], F32, kind="Internal").ap()
    e.h3 = nc.dram_tensor("h_last", [NP, W], F32, kind="Internal").ap()

    with ExitStack() as loc:
        def tmp(name, shape, dt=F32):
            return loc.enter_context(nc.sbuf_tensor(tag + name, shape, dt))

        sems = []

        def sem(name):
            sems.append(loc.enter_context(nc.semaphore(tag + name)))
            return sems[-1]

        RW = EP // P
        iota = tmp("iota", [P, P])
        hi_i = tmp("hi_i", [P, T], I32)
        hi = tmp("hi", [P, T])
        lo = tmp("lo", [P, T])
        is_lo = tmp("is_lo", [P, 2, G, P], BF16)
        is_hi = tmp("is_hi", [P, 2, G, NT], BF16)
        ends = tmp("ends", [P, T + 1], I32)
        run = tmp("run", [P, RW + 1], I32)
        pen = tmp("pen", [P, RW])
        tri = tmp("tri", [P, P])
        cnt = tmp("cnt", [P, NT])
        tot = tmp("tot", [P, NT])
        offs = tmp("offs", [P, NT + 1])
        end = tmp("end", [P, NT])
        beg = tmp("beg", [P, NT])
        has = tmp("has", [P, NT])
        w0 = tmp("w0", [P, NT])
        w1 = tmp("w1", [P, NT])
        til = tmp("til", [P, NT])
        til_i = tmp("til_i", [P, NT], I32)
        zrow = tmp("zrow", [P, 3 * P])
        counts = loc.enter_context(nc.psum_tensor("counts", [P, 512], F32))
        sums = loc.enter_context(nc.psum_tensor("sums", [P, 512], F32))
        loaded, stored = sem("loaded"), sem("stored")
        consts, ready = sem("consts"), sem("ready")
        hot, counted, summed, vec = sem("one_hots"), sem("counted"), sem("summed"), sem("vec")
        loc.callback(clear, nc, sems)
        block = loc.enter_context(nc.Block())

        @block.sync
        def _(sp):
            load_blocks(sp, loaded, [
                (e.dst[:, :], d["dst_cols"]), (e.src[:, :], d["src_cols"]),
                (ends[:, 1:T + 1], d["dst_cols"][P - 1:P, :].to_broadcast([P, T])),
                (ends[:, 0:1], d["dst_run"][0:1].rearrange("(a b) -> a b", a=1).to_broadcast([P, 1])),
                (run[:, 0:RW], d["dst_run"][0:EP].rearrange("(p f) -> p f", p=P)),
                (run[:, RW:RW + 1], d["dst_run"][RW:RW + EP].rearrange("(p f) -> p f", p=P)[:, 0:1]),
                (e.ea4[:, :, :], d["ea4_cols"]), (e.x[:, :, :], d["x"]), (e.attr[:, :], d["attr"])])
            sp.wait_ge(ready, 1)
            sp.dma_start(e.pens[0:EP].rearrange("(p f) -> p f", p=P), pen[:, :]).then_inc(stored, 16)
            sp.wait_ge(ready, 2)
            n = 2
            for rows, carries, w in zip(e.rows, e.carries, ROW_W):
                for part in rows:
                    sp.dma_start(part[EP:EP + 1, :], zrow[0:1, 0:min(w, HW)]).then_inc(stored, 16)
                    n += 1
                for k in (0, ZERO_CARRY):
                    sp.dma_start(carries[k:k + 1, :], zrow[0:1, 0:w]).then_inc(stored, 16)
                    n += 1
            sp.wait_ge(ready, 3)
            sp.dma_start(e.pens[EP:EP + P].rearrange("(a f) -> a f", a=1), tri[0:1, :]).then_inc(stored, 16)
            sp.wait_ge(stored, 16 * n)

        @block.gpsimd
        def _(pool):
            pool.iota(iota[:, :], [[1, P]], base=0, channel_multiplier=0,
                      allow_small_or_imprecise_dtypes=True).then_inc(consts, 1)
            pool.memset(e.ident[:, :], 0.0).then_inc(consts, 1)
            pool.memset(e.ones[:, :], 1.0).then_inc(consts, 1)
            pool.memset(e.mhalf[:, :], -0.5).then_inc(consts, 1)
            pool.wait_ge(consts, 4)
            pool.affine_select(out=e.ident[:, :], in_=e.ident[:, :], compare_op=ALU.not_equal, fill=1.0,
                               base=0, pattern=[[-1, P]], channel_multiplier=1).then_inc(consts, 1)
            pool.affine_select(out=tri[:, :], in_=e.ones[:, :], compare_op=ALU.is_ge, fill=0.0,
                               base=0, pattern=[[1, P]], channel_multiplier=-1).then_inc(consts, 1)

        @block.vector
        def _(dve):
            dve.wait_ge(loaded, 9 * 16)
            dve.wait_ge(consts, 6)
            nc.vector.tensor_scalar(hi_i[:, :], e.dst[:, :], 7, None, ALU.logical_shift_right).then_inc(vec, 1)
            dve.wait_ge(vec, 1)
            nc.vector.tensor_copy(hi[:, :], hi_i[:, :]).then_inc(vec, 1)
            dve.wait_ge(vec, 2)
            nc.vector.scalar_tensor_tensor(out=lo[:, :], in0=hi[:, :], scalar=-float(P), in1=e.dst[:, :],
                                           op0=ALU.mult, op1=ALU.add).then_inc(vec, 1)
            nc.vector.tensor_tensor(e.chain[:, :], ends[:, 1:T + 1], ends[:, 0:T], ALU.is_equal).then_inc(vec, 1)
            nc.vector.tensor_tensor(pen[:, :], run[:, 1:RW + 1], run[:, 0:RW], ALU.is_equal).then_inc(vec, 1)
            dve.wait_ge(vec, 5)
            nc.vector.tensor_scalar(pen[:, :], pen[:, :], 2 * BIG, -BIG, ALU.mult, ALU.add).then_inc(ready, 1)
            nc.vector.memset(zrow[:, :], 0.0).then_inc(ready, 1)

            def hots(r, b, n):
                if not early(r):
                    dve.wait_ge(counted, r - 1)
                nc.vector.tensor_tensor(is_lo[:, b], iota[:, :].unsqueeze(1).to_broadcast([P, G, P]),
                                        lo[:, bass.ds(r * G, G)].unsqueeze(2).to_broadcast([P, G, P]),
                                        ALU.is_equal).then_inc(hot, 1)
                nc.vector.tensor_tensor(is_hi[:, b], iota[:, 0:NT].unsqueeze(1).to_broadcast([P, G, NT]),
                                        hi[:, bass.ds(r * G, G)].unsqueeze(2).to_broadcast([P, G, NT]),
                                        ALU.is_equal).then_inc(hot, 1)

            rounds(dve, [(hots, 0)], S)
            dve.wait_ge(counted, S)
            nc.vector.tensor_copy(cnt[:, :], counts[:, 0:NT]).then_inc(vec, 1)
            dve.wait_ge(summed, 1)
            nc.vector.tensor_copy(tot[:, :], sums[:, 0:NT]).then_inc(vec, 1)
            nc.vector.memset(offs[:, 0:1], 0.0).then_inc(vec, 1)
            dve.wait_ge(vec, 8)
            nc.vector.tensor_tensor_scan(offs[:, 1:NT + 1], e.ones[:, 0:NT], tot[:, :], 0.0,
                                         ALU.mult, ALU.add).then_inc(vec, 1)
            dve.wait_ge(vec, 9)
            nc.vector.tensor_tensor(end[:, :], sums[:, P:P + NT], offs[:, 0:NT], ALU.add).then_inc(vec, 1)
            nc.vector.tensor_scalar(has[:, :], cnt[:, :], 0.0, None, ALU.is_gt).then_inc(vec, 1)
            dve.wait_ge(vec, 11)
            nc.vector.tensor_tensor(beg[:, :], end[:, :], cnt[:, :], ALU.subtract).then_inc(vec, 1)
            nc.vector.tensor_scalar(w0[:, :], end[:, :], float(-1 - ZERO_ROW), None, ALU.add).then_inc(vec, 1)
            dve.wait_ge(vec, 13)
            nc.vector.tensor_tensor(w0[:, :], w0[:, :], has[:, :], ALU.mult).then_inc(vec, 1)
            dve.wait_ge(vec, 14)
            nc.vector.tensor_scalar(e.last[:, :], w0[:, :], float(ZERO_ROW), None, ALU.add).then_inc(vec, 1)
            dve.wait_ge(vec, 15)
            nc.vector.tensor_scalar(til_i[:, :], e.last[:, :], 7, None, ALU.logical_shift_right).then_inc(vec, 1)
            dve.wait_ge(vec, 16)
            nc.vector.tensor_copy(til[:, :], til_i[:, :]).then_inc(vec, 1)
            dve.wait_ge(vec, 17)
            nc.vector.scalar_tensor_tensor(out=w1[:, :], in0=til[:, :], scalar=float(P), in1=beg[:, :],
                                           op0=ALU.mult, op1=ALU.is_gt).then_inc(vec, 1)
            dve.wait_ge(vec, 18)
            nc.vector.tensor_tensor(w1[:, :], w1[:, :], has[:, :], ALU.mult).then_inc(vec, 1)
            dve.wait_ge(vec, 19)
            nc.vector.scalar_tensor_tensor(out=w0[:, :], in0=til[:, :], scalar=float(-ZERO_CARRY), in1=w1[:, :],
                                           op0=ALU.add, op1=ALU.mult).then_inc(vec, 1)
            dve.wait_ge(vec, 20)
            nc.vector.tensor_scalar(e.carry[:, :], w0[:, :], float(ZERO_CARRY), None, ALU.add).then_inc(vec, 1)
            dve.wait_ge(vec, 21)
            nc.vector.memset(tri[0:1, :], -BIG).then_inc(ready, 1)

        @block.tensor
        def _(pe):
            def count(r, b, n):
                pe.wait_ge(hot, 2 * r + 2)
                for g in range(G):
                    first = isinstance(r, int) and r == 0 and g == 0
                    final = isinstance(r, int) and r == S - 1 and g == G - 1
                    mm = nc.tensor.matmul(counts[:, 0:NT], is_lo[:, b, g], is_hi[:, b, g],
                                          start=first, stop=final)
                mm.then_inc(counted, 1)

            rounds(pe, [(count, 1)], S)
            pe.wait_ge(vec, 6)
            nc.tensor.matmul(sums[:, 0:NT], e.ones[:, :], cnt[:, :], start=True, stop=True)
            nc.tensor.matmul(sums[:, P:P + NT], tri[:, :], cnt[:, :], start=True, stop=True).then_inc(summed, 1)
    return e


def carry_phase(nc, e, layer, width, heads=0, per_s=0, per_v=0):
    tag = f"carry{layer}_"
    chunks = [(c, min(P, width - c)) for c in range(0, width, P)]
    TG = -(-T // P)
    with ExitStack() as loc:
        def tmp(name, shape, dt=F32):
            return loc.enter_context(nc.sbuf_tensor(tag + name, shape, dt))

        sems = []

        def sem(name):
            sems.append(loc.enter_context(nc.semaphore(tag + name)))
            return sems[-1]

        H = heads
        scanned = width - H if H else width
        lasts = tmp("lasts", [P, TG, width])
        state = tmp("state", [P, TG, width])
        fin = tmp("feat_in", [P, T])
        fout = tmp("feat_out", [P, T])
        ps = loc.enter_context(nc.psum_tensor(tag + "ps", [P, 4, 512], F32))
        loaded, stored = sem("loaded"), sem("stored")
        turned, copied, scans, back, final = sem("turned"), sem("copied"), sem("scans"), sem("back"), sem("final")
        if H:
            shifts = tmp("shifts", [H, T + 1])
            decay = tmp("decay", [H, T])
            wide = tmp("wide", [P, T])
            expand = tmp("expand", [H, 2 * P])
            sh_in, sh_out, dec, spread, widened = (sem("shift_turned"), sem("shift_copied"), sem("decayed"),
                                                   sem("spread"), sem("widened"))
            exped, zeroed, loadw = sem("exped"), sem("zeroed"), sem("loadw")
        loc.callback(clear, nc, sems)
        block = loc.enter_context(nc.Block())
        parts = [(i, min(HW, width - HW * i)) for i in range(-(-width // HW))]
        rows = [part[0:EP, :].rearrange("(t p) w -> t p w", p=P)[:, P - 1, :] for part in e.rows[layer]]
        full = T // P
        part = T - full * P
        tiles = [(k, P if k < full else part) for k in range(TG)]
        NQ = -(-T // 512)

        @block.sync
        def _(sp):
            for k, m in tiles:
                for i, w in parts:
                    sp.dma_start(lasts[0:m, k, HW * i:HW * i + w], rows[i][k * P:k * P + m, 0:w])\
                        .then_inc(loaded, 16)
            sp.wait_ge(final, len(chunks) * TG + (1 if H else 0))
            for k, m in tiles:
                sp.dma_start(e.carries[layer][1 + k * P:1 + k * P + m, :], state[0:m, k, :]).then_inc(stored, 16)
            sp.wait_ge(stored, 16 * TG)

        if H:
            @block.gpsimd
            def _(pool):
                pool.memset(expand[:, :], 1.0).then_inc(zeroed, 1)
                n = 1
                for a, b, per in ((0, C0, per_s), *((C0 + C1 * i, C0 + C1 * i + C1, per_v) for i in range(3)),
                                  (W, W + H, 1)):
                    v = expand[:, a:b]
                    pool.wait_ge(zeroed, n)
                    pool.affine_select(out=v, in_=v, compare_op=ALU.is_ge, fill=0.0, base=0,
                                       pattern=[[1, b - a]], channel_multiplier=-per).then_inc(zeroed, 1)
                    pool.wait_ge(zeroed, n + 1)
                    pool.affine_select(out=v, in_=v, compare_op=ALU.is_ge, fill=0.0, base=per - 1,
                                       pattern=[[-1, b - a]], channel_multiplier=per).then_inc(zeroed, 1)
                    n += 2

        @block.tensor
        def _(pe):
            pe.wait_ge(loaded, 16 * TG * len(parts))
            if H:
                for k, m in tiles:
                    mm = nc.tensor.transpose(ps[0:H, k // 4, (k % 4) * P:(k % 4) * P + m],
                                             lasts[0:m, k, width - H:width], e.ident[0:m, 0:m])
                mm.then_inc(sh_in, 1)
                pe.wait_ge(sh_out, 1)
            for c, (c0, cw) in enumerate(chunks):
                if H:
                    pe.wait_ge(zeroed, 11)
                    pe.wait_ge(exped, 2)
                    cs = min(cw, scanned - c0)
                    if c:
                        pe.wait_ge(final, c * TG)
                    for q in range(NQ):
                        n = min(512, T - 512 * q)
                        mm = nc.tensor.matmul(ps[0:cs, q, 0:n], expand[:, c0:c0 + cs],
                                              decay[:, 512 * q:512 * q + n], start=True, stop=True)
                    mm.then_inc(spread, 1)
                    pe.wait_ge(widened, c + 1)
                elif c:
                    pe.wait_ge(final, c * TG)
                for k, m in tiles:
                    mm = nc.tensor.transpose(ps[0:cw, k // 4, (k % 4) * P:(k % 4) * P + m],
                                             lasts[0:m, k, c0:c0 + cw], e.ident[0:m, 0:m])
                mm.then_inc(turned, 1)
                pe.wait_ge(scans, c + 1)
                for k, m in tiles:
                    if k >= 4:
                        pe.wait_ge(final, c * TG + k - 3)
                    else:
                        pe.wait_ge(copied, c + 1)
                    nc.tensor.transpose(ps[0:m, k % 4, 0:cw], fout[0:cw, k * P:k * P + m],
                                        e.ident[0:cw, 0:cw]).then_inc(back, 1)

        @block.scalar
        def _(act):
            if H:
                act.wait_ge(dec, 2)
                nc.scalar.activation(decay[:, :], decay[:, :], ACT.Exp).then_inc(exped, 1)

        @block.vector
        def _(dve):
            n = 0
            if H:
                nc.vector.memset(shifts[:, 0:1], 0.0).then_inc(dec, 1)
                dve.wait_ge(sh_in, 1)
                nc.vector.tensor_copy(shifts[:, 1:T + 1],
                                      ps[0:H, :, :].rearrange("p a b -> p (a b)")[:, 0:T]).then_inc(sh_out, 1)
                dve.wait_ge(sh_out, 1)
                dve.wait_ge(dec, 1)
                nc.vector.tensor_tensor(decay[:, :], shifts[:, 0:T], shifts[:, 1:T + 1], ALU.subtract)\
                    .then_inc(loadw, 1)
                dve.wait_ge(loadw, 1)
                nc.vector.tensor_scalar(decay[:, :], decay[:, :], 0.0, None, ALU.min).then_inc(dec, 1)
                dve.wait_ge(exped, 1)
                nc.vector.tensor_tensor(decay[:, :], decay[:, :], e.chain[0:H, :], ALU.mult).then_inc(exped, 1)
            for c, (c0, cw) in enumerate(chunks):
                cs = min(cw, scanned - c0)
                if H:
                    dve.wait_ge(spread, c + 1)
                    nc.vector.tensor_copy(wide[0:cs, :], ps[0:cs, :, :].rearrange("p a b -> p (a b)")[:, 0:T])\
                        .then_inc(widened, 1)
                dve.wait_ge(turned, c + 1)
                if c:
                    dve.wait_ge(back, c * TG)
                nc.vector.tensor_copy(fin[0:cw, :], ps[0:cw, :, :].rearrange("p a b -> p (a b)")[:, 0:T])\
                    .then_inc(copied, 1)
                dve.wait_ge(copied, c + 1)
                if H:
                    dve.wait_ge(widened, c + 1)
                    if cs < cw:
                        nc.vector.tensor_copy(fout[0:cw, :], fin[0:cw, :]).then_inc(loadw, 1)
                        dve.wait_ge(loadw, 2)
                    nc.vector.tensor_tensor_scan(fout[0:cs, :], wide[0:cs, :], fin[0:cs, :], 0.0,
                                                 ALU.mult, ALU.add).then_inc(scans, 1)
                else:
                    nc.vector.tensor_tensor_scan(fout[0:cs, :], e.chain[0:cs, :], fin[0:cs, :], 0.0,
                                                 ALU.mult, ALU.add).then_inc(scans, 1)
                for k, m in tiles:
                    dve.wait_ge(back, c * TG + k + 1)
                    nc.vector.tensor_copy(state[0:m, k, c0:c0 + cw], ps[0:m, k % 4, 0:cw]).then_inc(final, 1)
            if H:
                nc.vector.memset(shifts[:, 0:1], 0.0).then_inc(final, 1)


def dst_same(nc, dve, e, same, dst_b, r, b):
    return nc.vector.tensor_tensor(same[:, b], dst_b[:, b].rearrange("p (g i) -> p g i", g=G),
                                   e.dst[:, bass.ds(r * G, G)].unsqueeze(2).to_broadcast([P, G, P]),
                                   ALU.is_equal)


def edge_conv(nc, e, d, layer):
    L0 = layer == 0
    tag = f"edge{layer}_"
    TW = W if L0 else 384
    MW = 384 if L0 else W
    KE = 10 if L0 else 17
    parts = [(i, min(HW, MW - HW * i)) for i in range(-(-MW // HW))]
    with ExitStack() as loc:
        def tmp(name, shape, dt=F32):
            return loc.enter_context(nc.sbuf_tensor(tag + name, shape, dt))

        sems = []

        def sem(name):
            sems.append(loc.enter_context(nc.semaphore(tag + name)))
            return sems[-1]

        def ps(name, shape):
            return loc.enter_context(nc.psum_tensor(tag + name, shape, F32))

        idx = tmp("idx", [P, 2, G], I32)
        row = tmp("row", [P, 2, G, TW])
        feat = tmp("feat", [KE, 2, SB])
        dst_b = tmp("dst_b", [P, 2, SB], I32)
        same = tmp("same", [P, 2, G, P])
        msg = tmp("msg", [P, 2, G, MW])
        out = tmp("out", [P, 2, G, MW])
        if L0:
            w_a = tmp("w_fc1", [10, 100])
            w_b = tmp("w_fc2", [100, 192])
            hid = tmp("hid", [100, 2, SB])
            wy = tmp("wy", [P, G, 2, C0])
            we = tmp("we", [P, G, C1])
            dot = tmp("dot", [P, G, 3, C1])
            ps_h = ps("ps_h", [P, 512])
        else:
            w_a = tmp("w_rad", [17, W])
            sig = tmp("sig", [P, 2, G, W])
            u = tmp("u", [P, G, 4, C0])
            q = tmp("q", [P, G, 3, C1])
            r_ = tmp("r_", [P, G, 3, C1])
        ps_w = ps("ps_w", [P, 2, G, 256])
        ps_a = ps("ps_a", [P, 2, 512])
        loadw, scaled = sem("weights_loaded"), sem("weights_scaled")
        picked = sem("indices_copied")
        rows_in = [e.pool_dma_sem(tag + f"rows_in{b}") for b in range(2)]
        feat_in = [sem(f"feat_in{b}") for b in range(2)]
        dst_in = [sem(f"dst_in{b}") for b in range(2)]
        out_sent = [sem(f"out_sent{b}") for b in range(2)]
        if L0:
            V = Steps(sem("vec_msg"), ["same", "wy", "we", "dot", "m0", "m1", "m2", "dot1", "dot2", "m3"])
        else:
            V = Steps(sem("vec_msg"), ["same", "u", "q", "r", "u2", "v", "us", "ms", "mv"])
        PA = Steps(sem("pe_weights"), ["hid", "w"] if L0 else ["w"])
        PB = Steps(sem("pe_sums"), ["lo", "hi"])
        A = Steps(sem("act_weights"), ["hid"] if L0 else ["sig"])
        B = Steps(sem("act_sums"), ["lo", "hi"])
        first = "hid" if L0 else "sig"
        lastv = V.names[-1]
        readers_row = V.names[-1]
        loc.callback(clear, nc, sems)
        block = loc.enter_context(nc.Block())

        @block.sync
        def _(sp):
            if L0:
                load_blocks(sp, loadw, [(w_a[:, :], d["L0_gnn_W_fc1"]), (w_b[:, :], d["L0_gnn_W_fc2"])])
            else:
                load_blocks(sp, loadw, [(w_a[:, :], d["L2_rad"])])

            def load(r, b, n):
                if not early(r):
                    wait(sp, PA, r - 2, PA.names[0])
                sp.dma_start(feat[:, b], (d["ea10_rows"] if L0 else d["ea16_rows"])[0:KE, bass.ds(r * SB, SB)])\
                    .then_inc(feat_in[b], 16)
                if not early(r):
                    wait(sp, V, r - 2, "same")
                sp.dma_start(dst_b[:, b], d["dst_rows"][0:1, bass.ds(r * SB, SB)].to_broadcast([P, SB]))\
                    .then_inc(dst_in[b], 16)

            def store(r, b, n):
                wait(sp, B, r, "hi")
                for i, w in parts:
                    sp.dma_start(e.rows[layer][i][bass.ds(r * SB, SB), :].rearrange("(g p) w -> p g w", p=P),
                                 out[:, b, :, HW * i:HW * i + w]).then_inc(out_sent[b], 16)

            rounds(sp, [(load, 0), (store, 3)], S)
            for b in range(2):
                sp.wait_ge(out_sent[b], 16 * len(parts) * (S // 2))

        @block.gpsimd
        def _(pool):
            def fetch(r, b, n):
                if not early(r):
                    wait(pool, V, r - 2, readers_row)
                    pool.wait_ge(rows_in[b], 16 * G * n)
                    pool.nop(nofuse=True)
                nc.gpsimd.tensor_copy(idx[:, b, :], e.src[:, bass.ds(r * G, G)]).then_inc(picked, 1)
                pool.wait_ge(picked, r + 1)
                pool.nop(nofuse=True)
                for g in range(G):
                    pool.indirect_dma_start(row[:, b, g, :], None, e.tsrc[layer],
                                            bass.IndirectOffsetOnAxis(ap=idx[:, b, g:g + 1], axis=0))\
                        .then_inc(rows_in[b], 16)

            rounds(pool, [(fetch, 0)], S)

        @block.tensor
        def _(pe):
            pe.wait_ge(loadw, 32 if L0 else 16)
            if L0:
                pe.wait_ge(scaled, 1)

            def hidden(r, b, n):
                pe.wait_ge(feat_in[b], 16 * (n + 1))
                if not early(r, 1):
                    wait(pe, A, r - 1, "hid")
                nc.tensor.matmul(ps_h[0:100, :], w_a[:, :], feat[:, b], start=True, stop=True)\
                    .then_inc(PA.sem, 1)

            def weights(r, b, n):
                if L0:
                    wait(pe, A, r, "hid")
                else:
                    pe.wait_ge(feat_in[b], 16 * (n + 1))
                if not early(r):
                    if L0:
                        wait(pe, V, r - 2, "m3")
                    else:
                        wait(pe, A, r - 2, "sig")
                for g in range(G):
                    lhs = hid[:, b, g * P:(g + 1) * P] if L0 else feat[:, b, g * P:(g + 1) * P]
                    mm = nc.tensor.matmul(ps_w[:, b, g, 0:(192 if L0 else W)], lhs, w_b[:, :] if L0 else w_a[:, :],
                                          start=True, stop=True)
                mm.then_inc(PA.sem, 1)

            def sums(h):
                def fn(r, b, n):
                    wait(pe, V, r, lastv)
                    if h:
                        wait(pe, B, r, "lo")
                    elif not early(r, 1):
                        wait(pe, B, r - 1, "hi")
                    for g in range(2):
                        mm = nc.tensor.matmul(ps_a[:, g, 0:MW], same[:, b, 2 * h + g], msg[:, b, 2 * h + g],
                                              start=True, stop=True)
                    mm.then_inc(PB.sem, 1)
                return fn

            rounds(pe, ([(hidden, 0)] if L0 else []) + [(sums(0), 2), (weights, 0), (sums(1), 2)], S)

        @block.scalar
        def _(act):
            def weights(r, b, n):
                wait(act, PA, r, "hid" if L0 else "w")
                if L0:
                    if not early(r):
                        wait(act, PA, r - 2, "w")
                    nc.scalar.activation(hid[:, b], ps_h[0:100, :], ACT.Relu, scale=1.0 / np.sqrt(10.0))\
                        .then_inc(A.sem, 1)
                else:
                    if not early(r):
                        wait(act, V, r - 2, "mv")
                    nc.scalar.activation(sig[:, b], ps_w[:, b, :, 0:W], ACT.Sigmoid).then_inc(A.sem, 1)

            def sums(r, b, n):
                if not early(r):
                    act.wait_ge(out_sent[b], 16 * len(parts) * n)
                for h, name in enumerate(("lo", "hi")):
                    wait(act, PB, r, name)
                    nc.scalar.copy(out[:, b, 2 * h:2 * h + 2], ps_a[:, :, 0:MW]).then_inc(B.sem, 1)

            rounds(act, [(weights, 0), (sums, 2)], S)

        @block.vector
        def _(dve):
            if L0:
                dve.wait_ge(loadw, 32)
                nc.vector.tensor_scalar(w_b[:, :], w_b[:, :], float(np.sqrt(2.0) / 10.0), None, ALU.mult)\
                    .then_inc(scaled, 1)

            def att(r, i0, i1):
                return e.ea4[:, bass.ds(r * G, G), i0:i1]

            def done(ins):
                ins.then_inc(V.sem, 1)

            def messages0(r, b, n):
                tt = nc.vector.tensor_tensor
                if not early(r, 1):
                    wait(dve, V, r - 1, V.names[-1])
                dve.wait_ge(dst_in[b], 16 * (n + 1))
                if not early(r):
                    wait(dve, PB, r - 2, "hi")
                done(dst_same(nc, dve, e, same, dst_b, r, b))
                wait(dve, PA, r, "w")
                dve.wait_ge(rows_in[b], 16 * G * (n + 1))
                y = row[:, b]
                yv = y[:, :, C0:W].rearrange("p g (d c) -> p g d c", d=3)
                done(tt(wy[:, :, :, :], ps_w[:, b, :, 0:128].rearrange("p g (a c) -> p g a c", a=2),
                        y[:, :, 0:C0].unsqueeze(2).to_broadcast([P, G, 2, C0]), ALU.mult))
                done(tt(we[:, :, :], ps_w[:, b, :, 128:160], att(r, 0, 1).to_broadcast([P, G, C1]), ALU.mult))
                done(tt(dot[:, :, :, :], yv, att(r, 1, 4).unsqueeze(3).to_broadcast([P, G, 3, C1]), ALU.mult))
                wait(dve, V, r, "wy")
                done(tt(msg[:, b, :, 0:C0], wy[:, :, 0, :], att(r, 0, 1).to_broadcast([P, G, C0]), ALU.mult))
                m = msg[:, b, :, 96:384].rearrange("p g (d c) -> p g d c", d=3)
                done(tt(m[:, :, :, 0:C0], wy[:, :, 1, :].unsqueeze(2).to_broadcast([P, G, 3, C0]),
                        att(r, 1, 4).unsqueeze(3).to_broadcast([P, G, 3, C0]), ALU.mult))
                wait(dve, V, r, "dot")
                done(tt(m[:, :, :, C0:96], we[:, :, :].unsqueeze(2).to_broadcast([P, G, 3, C1]), yv, ALU.mult))
                done(tt(dot[:, :, 0, :], dot[:, :, 0, :], dot[:, :, 1, :], ALU.add))
                wait(dve, V, r, "dot1")
                done(tt(dot[:, :, 0, :], dot[:, :, 0, :], dot[:, :, 2, :], ALU.add))
                wait(dve, V, r, "dot2")
                done(tt(msg[:, b, :, C0:96], dot[:, :, 0, :], ps_w[:, b, :, 160:192], ALU.mult))

            def messages2(r, b, n):
                tt = nc.vector.tensor_tensor
                if not early(r, 1):
                    wait(dve, V, r - 1, V.names[-1])
                dve.wait_ge(dst_in[b], 16 * (n + 1))
                if not early(r):
                    wait(dve, PB, r - 2, "hi")
                done(dst_same(nc, dve, e, same, dst_b, r, b))
                dve.wait_ge(rows_in[b], 16 * G * (n + 1))
                y = row[:, b]
                done(tt(u[:, :, :, :], y[:, :, 0:256].rearrange("p g (k c) -> p g k c", k=4),
                        att(r, 0, 4).unsqueeze(3).to_broadcast([P, G, 4, C0]), ALU.mult))
                done(tt(q[:, :, :, :], y[:, :, 256:288].unsqueeze(2).to_broadcast([P, G, 3, C1]),
                        att(r, 1, 4).unsqueeze(3).to_broadcast([P, G, 3, C1]), ALU.mult))
                done(tt(r_[:, :, :, :].rearrange("p g d c -> p g (d c)"), y[:, :, 288:384],
                        att(r, 0, 1).to_broadcast([P, G, 96]), ALU.mult))
                wait(dve, V, r, "u")
                done(tt(u[:, :, 0:2, :], u[:, :, 0:2, :], u[:, :, 2:4, :], ALU.add))
                wait(dve, V, r, "r")
                done(tt(q[:, :, :, :], q[:, :, :, :], r_[:, :, :, :], ALU.add))
                wait(dve, V, r, "u2")
                done(tt(u[:, :, 0, :], u[:, :, 0, :], u[:, :, 1, :], ALU.add))
                wait(dve, A, r, "sig")
                wait(dve, V, r, "us")
                done(tt(msg[:, b, :, 0:C0], u[:, :, 0, :], sig[:, b, :, 0:C0], ALU.mult))
                done(tt(msg[:, b, :, C0:W], q[:, :, :, :].rearrange("p g d c -> p g (d c)"),
                        sig[:, b, :, C0:W], ALU.mult))

            rounds(dve, [(messages0 if L0 else messages2, 1)], S)


def edge_attention(nc, e, d, layer):
    L1 = layer == 1
    tag = f"edge{layer}_"
    H = HEADS[layer]
    per_s, per_v = C0 // H, C1 // H
    MW = W + H
    RW = W + 2 * H
    KE = 16 if L1 else 65
    KB = 96 if L1 else 97
    LW, LP, LT, LE, LJ = (1, 2, 3, 4, 5) if L1 else (4, 4, 5, 6, 6)
    r2, r3 = 1.0 / float(np.sqrt(2.0)), 1.0 / float(np.sqrt(3.0))
    with ExitStack() as loc:
        def tmp(name, shape, dt=F32):
            return loc.enter_context(nc.sbuf_tensor(tag + name, shape, dt))

        sems = []

        def sem(name):
            sems.append(loc.enter_context(nc.semaphore(tag + name)))
            return sems[-1]

        def ps(name, shape):
            return loc.enter_context(nc.psum_tensor(tag + name, shape, F32))

        idx = tmp("idx", [P, 2, 2, G], I32)
        row = tmp("row", [P, 2, 2, G, W])
        feat = tmp("feat", [KE, 2, SB])
        dst_b = tmp("dst_b", [P, 2, SB], I32)
        pen = tmp("pen", [H, 2, SB + 1])
        m = tmp("m", [P, 2, G, C0 + 5 * C1])
        y5 = tmp("y5", [P, 2, G, 5])
        t1 = tmp("t1", [P, G, 3, C1])
        t2 = tmp("t2", [P, G, 3, C1])
        t3 = tmp("t3", [P, G, 3, C1])
        dot = tmp("dot", [P, G, 3, C1])
        x1 = tmp("x1", [P, G, 96])
        x23 = tmp("x23", [P, G, 256])
        x1t = tmp("x1t", [KB, SB])
        x2t = tmp("x2t", [P, SB])
        x3t = tmp("x3t", [P, SB])
        bend = tmp("bend", [C0, SB])
        soft = tmp("soft", [C0, SB])
        shf = tmp("shf", [H, 2, SB])
        shb = tmp("shb", [H, SB])
        arg = tmp("arg", [H, SB])
        es = tmp("es", [32 + H, SB])
        exs = tmp("exs", [P, G, 32 + H])
        exv = tmp("exv", [P, G, C1])
        same = tmp("same", [P, 2, G, P])
        msg = tmp("msg", [P, 2, G, MW])
        out = tmp("out", [P, 2, G, RW])
        w_rad = tmp("w_rad", [KE, 224])
        w_al = tmp("w_al", [KB, C0])
        w_ad = tmp("w_ad", [C0, H])
        w_s = tmp("w_s", [KB, C0])
        w_v = tmp("w_v", [P, 2, C0])
        ps_w = ps("ps_w", [P, G, 256])
        ps_n = ps("ps_n", [P, 512])
        ring = [ps(f"ring{i}", [P, 512]) for i in range(2)]
        ps_l = ps("ps_l", [P, 512])
        ps_v = ps("ps_v", [P, G, 128])
        ps_s = ps("ps_s", [P, 512])
        val = ps_n[:, 0:384].rearrange("p (g c) -> p g c", g=G)
        out_s = ps_s[:, 0:256].rearrange("p (g c) -> p g c", g=G)
        ex_p = ps_s[:, 256:256 + G * (32 + H)].rearrange("p (g c) -> p g c", g=G)
        if L1:
            wy = tmp("wy", [P, G, 96])
            gate = tmp("gate", [P, G, C1])
            sh = tmp("sh", [P, G, 96])
            v5 = tmp("v5", [P, G, 5, C1])
            z1 = tmp("z1", [P, G, 96])
            z23 = tmp("z23", [P, G, 256])
            z1t = tmp("z1t", [96, SB])
            z2t = tmp("z2t", [P, SB])
            z3t = tmp("z3t", [P, SB])
            half = tmp("half", [P, 2])
            w_g = tmp("w_g", [C0, C1])
            w_st = tmp("w_st", [C0, 96])
            w_sg = tmp("w_sg", [96, 96])
            w_s2 = tmp("w_s2", [96, C0])
            w_v2 = tmp("w_v2", [P, 2, C0])
            c_s2 = tmp("c_s2", [96, 1])
            c_v2 = tmp("c_v2", [P, 2, 1])
        else:
            ea4_flat = e.ea4[:, :, :].rearrange("p t k -> p (t k)")
            y3 = ea4_flat[:, 0:3 * T].rearrange("p (t k) -> p t k", k=3)
            len2 = ea4_flat[:, 3 * T:4 * T]
            square = m[:, :, :, :].rearrange("p b g c -> p (b g c)")[:, 0:T]
            inv = tmp("inv", [P, 2, G])
            w1 = tmp("w1", [65, C0])
            w2 = tmp("w2", [65, C0])
            w3 = tmp("w3", [65, 224])
            mean = tmp("mean", [65, 2])
            gb = tmp("gb", [C0, 4])
            gbh = tmp("gbh", [C0, 4])
            sq = tmp("sq", [P, 2, G, C0])
            ve = tmp("ve", [P, 2, G])
            rs = tmp("rs", [P, 2, G])
            zn = tmp("zn", [P, 2, G, C0])
            hu = tmp("hu", [C0, 2, SB])
            th = tmp("th", [C0, 2, SB])
            h1t = tmp("h1t", [65, SB])
            h2t = tmp("h2t", [65, 2, SB])

        loadw, zeroed, prepped, chained = (sem("weights_loaded"), sem("zeroed"), sem("weights_ready"),
                                           sem("prep_chain"))
        folding = sem("pe_folding")
        picked = sem("indices_copied")
        rows_in = [e.pool_dma_sem(tag + f"rows_in{b}") for b in range(2)]
        feat_in = [sem(f"feat_in{b}") for b in range(2)]
        dst_in = [sem(f"dst_in{b}") for b in range(2)]
        pen_in = [sem(f"pen_in{b}") for b in range(2)]
        out_sent = [sem(f"out_sent{b}") for b in range(2)]
        VP = Steps(sem("vec_product"), ([] if L1 else ["yn"]) + ["y5", "y5b"] + (["wy"] if L1 else []) +
                   ["dot", "t1", "t2", "s", "q", "vs", "dot1", "t12", "dot2", "cross", "o0b"])
        VM = Steps(sem("vec_maps"), ["soft"] + (["zy", "bc", "v5", "v5b", "dot", "t1", "t2", "s", "vs",
                                                 "dot1", "cross", "o0b"] if L1 else []) +
                   ["fwd", "bwd", "arg"])
        VJ = Steps(sem("vec_joint"), ["same", "exs", "exv", "s", "zy", "bc", "v", "w"])
        PW = Steps(sem("pe_weights"), ["w"])
        PX = Steps(sem("pe_turn"), ["x1", "x2", "x3"])
        PM = Steps(sem("pe_maps"), ["al", "s", "v", "at"] if L1 else ["al", "at", "s", "v"])
        PE_ = Steps(sem("pe_ex"), ["ex"])
        PJ = Steps(sem("pe_joint"), ["lo", "hi"])
        AT = Steps(sem("act_turn"), ["x1", "x2", "x3"])
        KM = Steps(sem("pool_rows_added"), ["m"])
        AW = Steps(sem("act_wrap"), ["m5"])
        AM = Steps(sem("act_maps"), ["bend"] + (["sh", "gate", "z"] if L1 else []))
        AE = Steps(sem("act_ex"), ["ex", "sh2"])
        AJ = Steps(sem("act_joint"), ["shift", "lo", "hi"])
        if L1:
            PZ = Steps(sem("pe_turn2"), ["x1", "x2", "x3", "v"])
            AZ = Steps(sem("act_turn2"), ["x1", "x2", "x3"])
        else:
            VZ = [Steps(sem(f"vec_z{k}"), ["ss", "ve"]) for k in (1, 2)]
            VN = [Steps(sem(f"vec_zn{k}"), ["zn"]) for k in (1, 2)]
            VH = [Steps(sem(f"vec_h{k}"), ["h"]) for k in (1, 2)]
            PZ_ = [Steps(sem(f"pe_z{k}"), ["z"]) for k in (1, 2)]
            PT = [Steps(sem(f"pe_zt{k}"), ["zt"]) for k in (1, 2)]
            AQ = [Steps(sem(f"act_sq{k}"), ["sq"]) for k in (1, 2)]
            AH = [Steps(sem(f"act_h{k}"), ["hu", "th"]) for k in (1, 2)]
            KL = Steps(sem("pool_lengths"), ["inv"])
            KN = [Steps(sem(f"pool_rs{k}"), ["rs"]) for k in (1, 2)]

        def last(r, n=1):
            return isinstance(r, int) and r + n >= S

        def c1(ap):
            return ap.rearrange("(p a) -> p a", a=1)

        def maps_loads(w_v, wv):
            return [(w_v[0:64, 0, 0:32], wv[0:64, :]), (w_v[64:128, 0, 32:64], wv[64:128, :]),
                    (w_v[0:64, 1, 0:32], wv[64:128, :]), (w_v[64:128, 1, 32:64], wv[64:128, :])]

        def rad_loads(w, src, k):
            return [(w[0:k, 0:64], src[:, 0:64]), (w[0:k, 64:96], src[:, 128:160]), (w[0:k, 96:160], src[:, 64:128]),
                    (w[0:k, 160:224], src[:, 160:224])]

        wload = []
        if L1:
            wload += rad_loads(w_rad, d["L1_gnn_W_rbf"], 16)
            wload += [(w_al[:, :], d["L1_gnn_W_alpha"]), (w_s[:, :], d["L1_gnn_Ws_val"]), (w_g[:, :], d["L1_gnn_Wg"]),
                      (w_s2[:, :], d["L1_gnn_Ws_vlin"])]
            wload += maps_loads(w_v, d["L1_gnn_Wv_val"]) + maps_loads(w_v2, d["L1_gnn_Wv_vlin"])
            wload += [(c_s2[0:64, :], c1(d["L1_gnn_w2_ss"])), (c_s2[64:96, :], c1(d["L1_gnn_w2_vv0"])),
                      (c_v2[0:64, 0, :], c1(d["L1_gnn_w2_sv"]))]
            for p0, k in ((64, 0), (0, 1), (64, 1)):
                wload += [(c_v2[p0:p0 + 32, k, :], c1(d["L1_gnn_w2_vs"])),
                          (c_v2[p0 + 32:p0 + 64, k, :], c1(d["L1_gnn_w2_vv1"]))]
            adot = d["L1_gnn_alpha_dot"]
        else:
            wload += rad_loads(w3, d["L3_gnn_rw3"], 64)
            roff = d["L3_gnn_roff"].rearrange("(a b) -> a b", a=1)
            wload += rad_loads(w3[64:65, :], roff, 1)
            c = lambda n: d["L3_gnn_" + n].rearrange("(a b) -> a b", a=1)
            wload += [(w1[0:64, :], d["L3_gnn_rw1"]), (w1[64:65, :], c("rb1")),
                      (w2[0:64, :], d["L3_gnn_rw2"]), (w2[64:65, :], c("rb2")),
                      (w_al[0:96, :], d["L3_gnn_lin_ws"][:, 0:64]), (w_al[96:97, :], c("lin_bs")[:, 0:64]),
                      (w_s[0:96, :], d["L3_gnn_lin_ws"][:, 64:128]), (w_s[96:97, :], c("lin_bs")[:, 64:128]),
                      (y3[:, :, :], d["ea3_cols"])]
            wload += maps_loads(w_v, d["L3_gnn_lin_wv"])
            wload += [(gb[:, i:i + 1], c1(d["L3_gnn_" + n])) for i, n in enumerate(("rg1", "rbe1", "rg2", "rbe2"))]
            adot = d["L3_gnn_alpha_dot"]
        for h in range(H):
            wload += [(w_ad[per_s * h:per_s * h + per_s, h:h + 1],
                       adot[(0, h) if len(adot.shape) == 3 else h].rearrange("(p a) -> p a", a=1))]
        zero = [w_v[:, :, :], w_ad[:, :], es[:, :]] + ([w_v2[:, :, :]] if L1 else [])
        loc.callback(clear, nc, sems)
        block = loc.enter_context(nc.Block())

        @block.sync
        def _(sp):
            sp.wait_ge(zeroed, len(zero))
            load_blocks(sp, loadw, wload)

            def load_feat(r, b, n):
                if not early(r):
                    wait(sp, PW if L1 else PZ_[0], r - 2, "w" if L1 else "z")
                sp.dma_start(feat[:, b], d["ea16_rows" if L1 else "ea64_rows"][0:KE, bass.ds(r * SB, SB)])\
                    .then_inc(feat_in[b], 16)

            def load_pen(r, b, n):
                if not early(r):
                    wait(sp, VM, r - 2, "bwd")
                sp.dma_start(pen[:, b], e.pens[bass.ds(r * SB, SB + 1)].rearrange("(a f) -> a f", a=1)
                             .to_broadcast([H, SB + 1])).then_inc(pen_in[b], 16)

            def load_dst(r, b, n):
                if not early(r):
                    wait(sp, VJ, r - 2, "same")
                sp.dma_start(dst_b[:, b], d["dst_rows"][0:1, bass.ds(r * SB, SB)].to_broadcast([P, SB]))\
                    .then_inc(dst_in[b], 16)

            def store(r, b, n):
                wait(sp, AJ, r, "hi")
                sp.dma_start(e.rows[layer][0][bass.ds(r * SB, SB), :].rearrange("(g p) w -> p g w", p=P),
                             out[:, b]).then_inc(out_sent[b], 16)

            rounds(sp, [(load_feat, 0), (load_pen, LT - 1), (load_dst, LJ - 1), (store, LJ + 1)], S)
            for b in range(2):
                sp.wait_ge(out_sent[b], 16 * (S // 2))

        @block.gpsimd
        def _(pool):
            for z in zero:
                pool.memset(z, 0.0).then_inc(zeroed, 1)
            def fetch(r, b, n):
                if not early(r):
                    wait(pool, KM, r - 2, "m")
                    pool.wait_ge(rows_in[b], 32 * G * n)
                    pool.nop(nofuse=True)
                for k, cols in enumerate((e.src, e.dst)):
                    nc.gpsimd.tensor_copy(idx[:, b, k, :], cols[:, bass.ds(r * G, G)]).then_inc(picked, 1)
                pool.wait_ge(picked, 2 * r + 2)
                pool.nop(nofuse=True)
                for k, table in enumerate((e.tsrc[layer], e.tdst)):
                    for g in range(G):
                        pool.indirect_dma_start(row[:, b, k, g, :], None, table,
                                                bass.IndirectOffsetOnAxis(ap=idx[:, b, k, g:g + 1], axis=0))\
                            .then_inc(rows_in[b], 16)

            def add_rows(r, b, n):
                pool.wait_ge(rows_in[b], 32 * G * (n + 1))
                if not early(r):
                    wait(pool, VP, r - 2, "vs")
                pool.nop(nofuse=True)
                nc.gpsimd.tensor_tensor(m[:, b, :, 0:W], row[:, b, 0], row[:, b, 1], ALU.add).then_inc(KM.sem, 1)

            def lengths(r, b, n):
                if not early(r):
                    wait(pool, VP, r - 2, "yn")
                else:
                    pool.wait_ge(prepped, 1)
                pool.nop(nofuse=True)
                nc.gpsimd.tensor_tensor(inv[:, b, :], len2[:, bass.ds(r * G, G)], e.mhalf[:, 0:G], ALU.pow)\
                    .then_inc(KL.sem, 1)

            def power(k):
                def fn(r, b, n):
                    wait(pool, VZ[k], r, "ve")
                    nc.gpsimd.tensor_tensor(rs[:, k, :], ve[:, k, :], e.mhalf[:, 0:G], ALU.pow).then_inc(KN[k].sem, 1)
                return fn

            rounds(pool, [(fetch, LP - 2), (add_rows, LP - 1)] if L1 else
                   [(lengths, LP - 1), (fetch, LP - 2), (add_rows, LP - 1), (power(0), 0), (power(1), 2)], S)

        @block.tensor
        def _(pe):
            mm, tp = nc.tensor.matmul, nc.tensor.transpose
            pe.wait_ge(loadw, 16 * len(wload))
            if L1:
                tp(ring[0][0:C0, 0:96], w_s[0:96, :], e.ident[0:96, 0:96]).then_inc(folding, 1)
                pe.wait_ge(chained, 1)
                pe.nop(nofuse=True)
                mm(ring[1][0:96, 0:C1], w_st[:, :], w_g[:, :], start=True, stop=True).then_inc(folding, 1)
            pe.wait_ge(prepped, 1)

            def turn_x(steps, a, a2, first, second, third, r):
                for k, (i, waits) in enumerate((first, second, third)):
                    for w in waits:
                        wait(pe, *w)
                    if waits:
                        pe.nop(nofuse=True)
                    for g in range(G):
                        if k == 0:
                            t = tp(ring[i][0:96, g * P:(g + 1) * P], a[:, g, :], e.ident[:, :])
                        else:
                            t = tp(ring[i][:, g * P:(g + 1) * P], a2[:, g, P * (k - 1):P * k], e.ident[:, :])
                    t.then_inc(steps.sem, 1)

            def z(k):
                def fn(r, b, n):
                    if k == 0:
                        pe.wait_ge(feat_in[b], 16 * (n + 1))
                    else:
                        wait(pe, VH[0], r, "h")
                    if not early(r, 1):
                        wait(pe, VN[k], r - 1, "zn")
                    if k == 0 and not early(r, 3):
                        wait(pe, VN[1], r - 3, "zn")
                    if k == 1 and not last(r):
                        wait(pe, VN[0], r + 1, "zn")
                    pe.nop(nofuse=True)
                    for g in range(G):
                        lhs = feat[:, b, g * P:(g + 1) * P] if k == 0 else h1t[:, g * P:(g + 1) * P]
                        t = mm(ps_n[:, 256 * k + C0 * g:256 * k + C0 * (g + 1)], lhs, (w2 if k else w1)[:, :],
                               start=True, stop=True)
                    t.then_inc(PZ_[k].sem, 1)
                return fn

            def zt(k):
                def fn(r, b, n):
                    lag = 4 if k == 0 else 2
                    if not early(r, lag):
                        wait(pe, AT, r - lag, "x3" if k else "x2")
                    elif r > 0:
                        wait(pe, AH[k], r - 1, "th")
                    wait(pe, VN[k], r, "zn")
                    pe.nop(nofuse=True)
                    for g in range(G):
                        t = tp(ring[1 - k][0:C0, P * g:P * (g + 1)], zn[:, k, g, :], e.ident[:, :])
                    t.then_inc(PT[k].sem, 1)
                return fn

            def weights(r, b, n):
                if L1:
                    pe.wait_ge(feat_in[b], 16 * (n + 1))
                else:
                    wait(pe, VH[1], r, "h")
                if not early(r, 1):
                    wait(pe, VP, r - 1, "o0b")
                for g in range(G):
                    lhs = feat[:, b, g * P:(g + 1) * P] if L1 else h2t[:, b, g * P:(g + 1) * P]
                    t = mm(ps_w[:, g, 0:224], lhs, (w_rad if L1 else w3)[:, :], start=True, stop=True)
                t.then_inc(PW.sem, 1)

            def turn(r, b, n):
                wait(pe, VP, r, "o0b")
                if L1:
                    if not early(r, 3):
                        free = [(AJ, r - 3, "hi")]
                    elif r:
                        free = [(AZ, r - 2, "x3") if r == 2 else (AT, r - 1, "x3")]
                    else:
                        free = []
                    uses = (0, free), (1, []), (0, [(AT, r, "x1")])
                else:
                    uses = (0, [(AH[1], r + 1, "th")] if early(r) else [(AJ, r - 2, "hi")]), (1, []), \
                           (0, [(AT, r, "x1")])
                turn_x(PX, x1, x23, *uses, r)

            def turn2(r, b, n):
                wait(pe, VM, r, "o0b")
                turn_x(PZ, z1, z23, (1, [(AJ, r - 2, "hi")] if last(r) else [(AT, r + 1, "x2")]),
                       (0, [] if last(r) else [(AT, r + 1, "x3")]), (1, [(AZ, r, "x1")]), r)

            def ex(r, b, n):
                wait(pe, AE, r, "sh2")
                if not early(r, 1):
                    wait(pe, VJ, r - 1, "w")
                pe.nop(nofuse=True)
                for g in range(G):
                    t = tp(ex_p[:, g, :], es[:, g * P:(g + 1) * P], e.ident[0:32 + H, 0:32 + H])
                t.then_inc(PE_.sem, 1)

            def sums(r, b, n):
                wait(pe, VJ, r, "w")
                for k, name in enumerate(("lo", "hi")):
                    if L1:
                        wait(pe, *((AJ, r - 1, "hi") if last(r) else (AZ, r + 1, "x3" if k else "x2")))
                    elif not last(r, 3 if k else 5):
                        wait(pe, AH[k], r + (3 if k else 5), "th")
                    elif not last(r):
                        wait(pe, AT, r + 1, "x3" if k else "x2")
                    else:
                        wait(pe, AJ, r - 1, name)
                    bank = ring[k if L1 else 1 - k]
                    for g in range(2):
                        t = mm(bank[:, 256 * g:256 * g + MW], same[:, b, 2 * k + g], msg[:, b, 2 * k + g],
                               start=True, stop=True)
                    t.then_inc(PJ.sem, 1)

            def out_maps(to, xt, ws):
                for g in range(G):
                    t = mm(to[:, g, :], xt[:, g * P:(g + 1) * P], ws[:, :], start=True, stop=True)
                return t

            def vec_maps(xt, yt, wv):
                for g in range(G):
                    mm(ps_v[:, g, 0:64], xt[:, g * P:(g + 1) * P], wv[:, 0, :], start=True, stop=True)
                    t = mm(ps_v[:, g, 64:128], yt[:, g * P:(g + 1) * P], wv[:, 1, :], start=True, stop=True)
                return t

            def maps_al(r, b, n):
                wait(pe, AT, r, "x1")
                if not early(r, 1):
                    wait(pe, VM, r - 1, "arg")
                mm(ps_l[0:C0, :], w_al[:, :], x1t[:, :], start=True, stop=True).then_inc(PM.sem, 1)

            def maps_sv(r, b, n):
                wait(pe, AT, r, "x3")
                if L1:
                    if not early(r, 1):
                        wait(pe, AM, r - 1, "sh")
                    out_maps(val, x1t[0:96, :], w_sg).then_inc(PM.sem, 1)
                    if not early(r):
                        wait(pe, VJ, r - 2, "w")
                else:
                    if not early(r, 1):
                        wait(pe, VJ, r - 1, "w")
                    out_maps(out_s, x1t, w_s).then_inc(PM.sem, 1)
                vec_maps(x2t, x3t, w_v).then_inc(PM.sem, 1)

            def maps_at(r, b, n):
                wait(pe, VM, r, "soft")
                pe.nop(nofuse=True)
                mm(ps_l[0:H, :], w_ad[:, :], bend[:, :], start=True, stop=True).then_inc(PM.sem, 1)

            def maps2(r, b, n):
                wait(pe, AZ, r, "x3")
                if not early(r, 1):
                    wait(pe, VJ, r - 1, "w")
                wait(pe, VM, *((r, "arg") if last(r) else (r + 1, "bc")))
                out_maps(out_s, z1t, w_s2)
                vec_maps(z2t, z3t, w_v2).then_inc(PZ.sem, 1)

            rounds(pe, [(turn, LT), (maps_al, LT), (maps_sv, LT), (maps_at, LT), (turn2, LE), (sums, LJ),
                        (weights, LW), (maps2, LE), (ex, LE)] if L1 else
                   [(weights, LW), (ex, LE), (turn, LT), (maps_al, LT), (zt(0), 1), (zt(1), 3), (maps_at, LT),
                    (z(0), 0), (z(1), 2), (maps_sv, LT), (sums, LJ)], S)

        @block.scalar
        def _(act):
            copy, af = nc.scalar.copy, nc.scalar.activation
            act.wait_ge(prepped, 1)

            def squares(k):
                def fn(r, b, n):
                    wait(act, PZ_[k], r, "z")
                    if k == 0 and not early(r):
                        wait(act, PZ_[1], r - 2, "z")
                    if not early(r, 1):
                        wait(act, VZ[k], r - 1, "ss")
                    af(sq[:, k, :, :].rearrange("p g c -> p (g c)"), ps_n[:, 256 * k:256 * k + 256], ACT.Square)\
                        .then_inc(AQ[k].sem, 1)
                return fn

            def silu(k):
                def fn(r, b, n):
                    wait(act, PT[k], r, "zt")
                    if not early(r, 1):
                        wait(act, VH[k], r - 1, "h")
                    af(hu[:, k], ring[1 - k][0:C0, :], ACT.Identity, scale=gb[:, 2 * k:2 * k + 1],
                       bias=gb[:, 2 * k + 1:2 * k + 2]).then_inc(AH[k].sem, 1)
                    af(th[:, k], ring[1 - k][0:C0, :], ACT.Tanh, scale=gbh[:, 2 * k:2 * k + 1],
                       bias=gbh[:, 2 * k + 1:2 * k + 2]).then_inc(AH[k].sem, 1)
                return fn

            def copy_x(psteps, steps, r, outs, bank):
                for k, dst in enumerate(outs):
                    rows = 96 if k == 0 else P
                    wait(act, psteps, r, f"x{k + 1}")
                    copy(dst[0:rows, :], ring[(bank + k) % 2][0:rows, :]).then_inc(steps.sem, 1)

            def wrap(r, b, n):
                wait(act, KM, r, "m")
                copy(m[:, b, :, W:W + 64], m[:, b, :, 64:128]).then_inc(AW.sem, 1)

            def turn(r, b, n):
                if not early(r, 1):
                    wait(act, PM, r - 1, "v")
                copy_x(PX, AT, r, (x1t, x2t, x3t), 0)

            def turn2(r, b, n):
                if not early(r, 1):
                    wait(act, PZ, r - 1, "v")
                copy_x(PZ, AZ, r, (z1t, z2t, z3t), 1)

            def exps(r, b, n):
                wait(act, VM, r, "arg")
                if not early(r, 1):
                    wait(act, PE_, r - 1, "ex")
                af(es[0:H, :], arg[:, :], ACT.Exp).then_inc(AE.sem, 1)
                copy(es[32:32 + H, :], shb[:, :]).then_inc(AE.sem, 1)

            def joint(r, b, n):
                wait(act, VJ, r, "exs")
                if not early(r):
                    act.wait_ge(out_sent[b], 16 * n)
                copy(out[:, b, :, MW:RW], exs[:, :, 32:32 + H]).then_inc(AJ.sem, 1)
                for k, name in enumerate(("lo", "hi")):
                    bank = ring[k if L1 else 1 - k]
                    wait(act, PJ, r, name)
                    copy(out[:, b, 2 * k:2 * k + 2, 0:MW], bank[:, :].rearrange("p (g c) -> p g c", g=2)[:, :, 0:MW])\
                        .then_inc(AJ.sem, 1)

            def bends(r, b, n):
                wait(act, PM, r, "al")
                if not early(r, 1):
                    wait(act, VM, r - 1, "soft")
                if L1:
                    af(soft[:, :], ps_l[0:C0, :], ACT.Relu).then_inc(AM.sem, 1)
                else:
                    af(soft[:, :], ps_l[0:C0, :], ACT.Tanh, scale=0.5).then_inc(AM.sem, 1)

            def gates(r, b, n):
                wait(act, PM, r, "s")
                if not early(r, 1):
                    wait(act, VM, r - 1, "o0b")
                af(sh[:, :, :], val, ACT.Tanh, scale=0.5).then_inc(AM.sem, 1)
                wait(act, AM, r, "sh")
                act.nop(nofuse=True)
                af(gate[:, :, :], sh[:, :, C0:96], ACT.Identity, scale=half[:, 0:1], bias=half[:, 1:2])\
                    .then_inc(AM.sem, 1)

            def halves(r, b, n):
                if not early(r, 1):
                    wait(act, PZ, r - 1, "x3")
                act.nop(nofuse=True)
                af(z23[:, :, 0:C0], sh[:, :, 0:C0], ACT.Identity, scale=half[:, 0:1], bias=half[:, 1:2])\
                    .then_inc(AM.sem, 1)

            rounds(act, [(turn, LT), (wrap, LP), (bends, LT), (gates, LT), (exps, LE), (turn2, LE),
                         (halves, LT), (joint, LJ)] if L1 else
                   [(exps, LE), (wrap, LP), (turn, LT), (bends, LT), (silu(0), 1), (silu(1), 3), (squares(0), 0),
                    (squares(1), 2), (joint, LJ)], S)

        @block.vector
        def _(dve):
            tt, ts, stt = nc.vector.tensor_tensor, nc.vector.tensor_scalar, nc.vector.scalar_tensor_tensor
            dve.wait_ge(loadw, 16 * len(wload))
            n_ch = [0]

            def link(ins):
                ins.then_inc(chained, 1)
                n_ch[0] += 1
                dve.wait_ge(chained, n_ch[0])

            if L1:
                dve.wait_ge(folding, 1)
                link(nc.vector.tensor_copy(w_st[:, :], ring[0][0:C0, 0:96]))
                dve.wait_ge(folding, 2)
                link(nc.vector.tensor_copy(w_sg[:, C0:96], ring[1][0:96, 0:C1]))
                link(nc.vector.tensor_copy(w_sg[:, 0:C0], w_s[0:96, :]))
                link(nc.vector.memset(half[:, :], 0.5))
            if not L1:
                link(tt(len2[:, :], y3[:, :, 0], y3[:, :, 0], ALU.mult))
                link(tt(square, y3[:, :, 1], y3[:, :, 1], ALU.mult))
                link(tt(len2[:, :], len2[:, :], square, ALU.add))
                link(tt(square, y3[:, :, 2], y3[:, :, 2], ALU.mult))
                link(stt(out=len2[:, :], in0=square, scalar=1e-12, in1=len2[:, :], op0=ALU.add, op1=ALU.add))
                link(ts(ea4_flat[:, 0:3 * T], ea4_flat[:, 0:3 * T], float(np.sqrt(3.0)), None, ALU.mult))
                link(ts(w2[0:64, :], w2[0:64, :], 0.5, None, ALU.mult))
                link(ts(w3[0:64, :], w3[0:64, :], 0.5, None, ALU.mult))
                for k, w in enumerate((w1, w2)):
                    link(nc.vector.tensor_reduce(mean[:, k:k + 1], w[:, :], AX.X, ALU.add))
                    link(ts(mean[:, k:k + 1], mean[:, k:k + 1], 1.0 / C0, None, ALU.mult))
                    link(ts(w[:, :], w[:, :], mean[:, k:k + 1], None, ALU.subtract))
                link(ts(gbh[:, :], gb[:, :], 0.5, None, ALU.mult))
                link(nc.vector.memset(h1t[64:65, :], 1.0))
                link(nc.vector.memset(h2t[64:65, :, :], 1.0))
                link(nc.vector.memset(x1t[96:97, :], 1.0))
            wr = w_rad if L1 else w3
            link(ts(wr[:, 160:192], wr[:, 160:192], r3, None, ALU.mult))
            link(ts(wr[:, 192:224], wr[:, 192:224], r2, None, ALU.mult))
            link(ts(w_ad[:, :], w_ad[:, :], 0.2 if L1 else 0.4, None, ALU.mult))
            if L1:
                link(ts(w_s2[:, :], w_s2[:, :], c_s2[:, :], None, ALU.mult))
                link(ts(w_s2[64:96, :], w_s2[64:96, :], r3, None, ALU.mult))
                for k in range(2):
                    link(ts(w_v2[:, k, :], w_v2[:, k, :], c_v2[:, k, :], None, ALU.mult))
                for p0, k in ((96, 0), (32, 1), (96, 1)):
                    link(ts(w_v2[p0:p0 + 32, k, :], w_v2[p0:p0 + 32, k, :], r2, None, ALU.mult))
            nc.vector.memset(shf[:, 1, SB - 1:SB], -BIG).then_inc(prepped, 1)

            def y_of(b, k, n, width):
                return y5[:, b, :, k:k + n].unsqueeze(3).to_broadcast([P, G, n, width])

            def comps(ap):
                return ap.rearrange("p g (d c) -> p g d c", c=C1)

            def steps_of(steps):
                def done(ins):
                    ins.then_inc(steps.sem, 1)
                return done

            def variance(k):
                def fn(r, b, n):
                    done = steps_of(VZ[k])
                    wait(dve, AQ[k], r, "sq")
                    if not early(r, 1):
                        wait(dve, KN[k], r - 1, "rs")
                        wait(dve, VN[k], r - 1, "zn")
                    done(nc.vector.tensor_reduce(ve[:, k, :], sq[:, k, :, :], AX.X, ALU.add))
                    wait(dve, VZ[k], r, "ss")
                    done(ts(ve[:, k, :], ve[:, k, :], 1.0 / C0, EPS, ALU.mult, ALU.add))
                return fn

            def scaled(k):
                def fn(r, b, n):
                    wait(dve, KN[k], r, "rs")
                    if not early(r, 1):
                        wait(dve, PT[k], r - 1, "zt")
                    tt(zn[:, k, :, :], ps_n[:, 256 * k:256 * k + 256].rearrange("p (g c) -> p g c", g=G),
                       rs[:, k, :].unsqueeze(2).to_broadcast([P, G, C0]), ALU.mult).then_inc(VN[k].sem, 1)
                return fn

            def hidden(k):
                def fn(r, b, n):
                    wait(dve, AH[k], r, "th")
                    if k == 0 and not early(r, 1):
                        wait(dve, PZ_[1], r - 1, "z")
                    if k == 1 and not early(r):
                        wait(dve, PW, r - 2, "w")
                    stt(out=h2t[0:C0, b] if k else h1t[0:C0, :], in0=th[:, k], scalar=1.0, in1=hu[:, k],
                        op0=ALU.add, op1=ALU.mult).then_inc(VH[k].sem, 1)
                return fn

            def product_a(r, b, n):
                done = steps_of(VP)
                if not early(r, 1):
                    wait(dve, VP, r - 1, "o0b")
                if L1 and not early(r):
                    wait(dve, VM, r - 2, "arg")
                if not L1:
                    wait(dve, KL, r, "inv")
                    done(tt(y3[:, bass.ds(r * G, G), :], y3[:, bass.ds(r * G, G), :],
                            inv[:, b, :].unsqueeze(2).to_broadcast([P, G, 3]), ALU.mult))
                    wait(dve, VP, r, "yn")
                    dve.nop(nofuse=True)
                yr = e.ea4[:, bass.ds(r * G, G), 1:4] if L1 else y3[:, bass.ds(r * G, G), :]
                yr2 = e.ea4[:, bass.ds(r * G, G), 1:3] if L1 else y3[:, bass.ds(r * G, G), 0:2]
                done(nc.vector.tensor_copy(y5[:, b, :, 0:3], yr))
                done(nc.vector.tensor_copy(y5[:, b, :, 3:5], yr2))
                if L1:
                    wait(dve, PW, r, "w")
                    done(tt(wy[:, :, :], ps_w[:, :, 0:96],
                            e.ea4[:, bass.ds(r * G, G), 0:1].to_broadcast([P, G, 96]), ALU.mult))
                wait(dve, VP, r, "y5b")
                wait(dve, KM, r, "m")
                v = comps(m[:, b, :, 64:224])
                done(tt(dot[:, :, :, :], v[:, :, 0:3], y_of(b, 0, 3, C1), ALU.mult))
                wait(dve, AW, r, "m5")
                done(tt(t1[:, :, :, :], v[:, :, 1:4], y_of(b, 2, 3, C1), ALU.mult))
                done(tt(t2[:, :, :, :], v[:, :, 2:5], y_of(b, 1, 3, C1), ALU.mult))

            def product_b(r, b, n):
                done = steps_of(VP)
                v = comps(m[:, b, :, 64:224])
                if not L1:
                    wait(dve, PW, r, "w")
                if not early(r, 1):
                    wait(dve, PX, r - 1, "x3")
                if L1:
                    wait(dve, VP, r, "wy")
                ws = wy if L1 else ps_w
                done(tt(x1[:, :, 0:C0], m[:, b, :, 0:C0], ws[:, :, 0:C0], ALU.mult))
                done(tt(x23[:, :, 0:C0], m[:, b, :, 0:C0], ps_w[:, :, 96:160], ALU.mult))
                done(tt(vectors(x23, 0), v[:, :, 0:3], ws[:, :, 64:96].unsqueeze(2).to_broadcast([P, G, 3, C1]),
                        ALU.mult))
                wait(dve, VP, r, "dot")
                done(tt(dot[:, :, 0, :], dot[:, :, 0, :], dot[:, :, 1, :], ALU.add))
                wait(dve, VP, r, "t2")
                done(tt(t1[:, :, :, :], t1[:, :, :, :], t2[:, :, :, :], ALU.subtract))
                wait(dve, VP, r, "dot1")
                done(tt(dot[:, :, 0, :], dot[:, :, 0, :], dot[:, :, 2, :], ALU.add))
                wait(dve, VP, r, "t12")
                done(tt(vectors(x23, 1), t1[:, :, :, :],
                        ps_w[:, :, 192:224].unsqueeze(2).to_broadcast([P, G, 3, C1]), ALU.mult))
                wait(dve, VP, r, "dot2")
                done(tt(x1[:, :, 64:96], dot[:, :, 0, :], ps_w[:, :, 160:192], ALU.mult))

            def vectors(ap, k):
                return ap[:, :, 64:256].rearrange("p g (d k c) -> p g d k c", d=3, k=2)[:, :, :, k, :]

            def vec_out(done, steps, r, to, y):
                done(tt(to[:, :, :, :], ps_v[:, :, 0:32].unsqueeze(2).to_broadcast([P, G, 3, C1]), y, ALU.mult))
                wait(dve, steps, r, "zy")
                done(tt(to[:, :, :, :], to[:, :, :, :], comps(ps_v[:, :, 32:128]), ALU.add))
                wait(dve, steps, r, "bc")

            def joint(r, b, n):
                done = steps_of(VJ)
                dve.wait_ge(dst_in[b], 16 * (n + 1))
                if not early(r):
                    wait(dve, PJ, r - 2, "hi")
                done(dst_same(nc, dve, e, same, dst_b, r, b))
                wait(dve, PE_, r, "ex")
                wait(dve, *((PZ, r, "v") if L1 else (PM, r, "v")))
                if not early(r, 1):
                    wait(dve, AJ, r - 1, "shift")
                    wait(dve, VJ, r - 1, "w")
                done(nc.vector.tensor_copy(exs[:, :, :], ex_p))
                wait(dve, VJ, r, "exs")
                exb = exs[:, :, 0:H]
                done(nc.vector.tensor_copy(exv[:, :, :].rearrange("p g (h k) -> p g h k", h=H),
                                           exb.unsqueeze(3).to_broadcast([P, G, H, per_v])))
                done(tt(msg[:, b, :, 0:C0].rearrange("p g (h k) -> p g h k", h=H),
                        out_s.rearrange("p g (h k) -> p g h k", h=H),
                        exb.unsqueeze(3).to_broadcast([P, G, H, per_s]), ALU.mult))
                src = e.ea4[:, bass.ds(r * G, G), 1:4] if L1 else y3[:, bass.ds(r * G, G), :]
                vec_out(done, VJ, r, t3, src.unsqueeze(3).to_broadcast([P, G, 3, C1]))
                done(tt(comps(msg[:, b, :, C0:W]), t3[:, :, :, :],
                        exv[:, :, :].unsqueeze(2).to_broadcast([P, G, 3, C1]), ALU.mult))
                done(nc.vector.tensor_copy(msg[:, b, :, W:MW], exb))

            def bends(r, b, n):
                wait(dve, AM, r, "bend")
                if not early(r, 1):
                    wait(dve, PM, r - 1, "at")
                stt(out=bend[:, :], in0=soft[:, :], scalar=4.0 if L1 else 1.5, in1=ps_l[0:C0, :],
                    op0=ALU.mult if L1 else ALU.add, op1=ALU.add if L1 else ALU.mult).then_inc(VM.sem, 1)

            def second(r, b, n):
                done = steps_of(VM)
                wait(dve, PM, r, "v")
                if not last(r):
                    wait(dve, VP, r + 1, "o0b")
                vec_out(done, VM, r, t1, y_of(b, 0, 3, C1))
                wait(dve, AM, r, "gate")
                if not early(r, 1):
                    wait(dve, PZ, r - 1, "x3")
                gb_ = gate[:, :, :].unsqueeze(2)
                done(tt(v5[:, :, 0:3, :], t1[:, :, :, :], gb_.to_broadcast([P, G, 3, C1]), ALU.mult))
                done(tt(v5[:, :, 3:5, :], t1[:, :, 0:2, :], gb_.to_broadcast([P, G, 2, C1]), ALU.mult))
                wait(dve, VM, r, "v5b")
                y0 = e.ea4[:, bass.ds(r * G, G), 0:1]
                done(tt(dot[:, :, :, :], v5[:, :, 0:3], y_of(b, 0, 3, C1), ALU.mult))
                done(tt(t1[:, :, :, :], v5[:, :, 1:4], y_of(b, 2, 3, C1), ALU.mult))
                done(tt(t2[:, :, :, :], v5[:, :, 2:5], y_of(b, 1, 3, C1), ALU.mult))
                wait(dve, AM, r, "z")
                done(tt(z1[:, :, 0:C0], z23[:, :, 0:C0], y0.to_broadcast([P, G, C0]), ALU.mult))
                done(tt(vectors(z23, 0), v5[:, :, 0:3], y0.unsqueeze(3).to_broadcast([P, G, 3, C1]), ALU.mult))
                wait(dve, VM, r, "dot")
                done(tt(dot[:, :, 0, :], dot[:, :, 0, :], dot[:, :, 1, :], ALU.add))
                wait(dve, VM, r, "t2")
                done(tt(vectors(z23, 1), t1[:, :, :, :], t2[:, :, :, :], ALU.subtract))
                wait(dve, VM, r, "dot1")
                done(tt(z1[:, :, 64:96], dot[:, :, 0, :], dot[:, :, 2, :], ALU.add))

            def shifts(r, b, n):
                done = steps_of(VM)
                wait(dve, PM, r, "at")
                dve.wait_ge(pen_in[b], 16 * (n + 1))
                done(nc.vector.tensor_tensor_scan(shf[:, b, :], pen[:, b, 0:SB], ps_l[0:H, :],
                                                  shf[:, 1 - b, SB - 1:SB], ALU.min, ALU.max))
                wait(dve, VM, r, "fwd")
                if not early(r, 1):
                    wait(dve, AE, r - 1, "sh2")
                done(nc.vector.tensor_tensor_scan(shb[:, ::-1], pen[:, b, SB:0:-1], shf[:, b, ::-1],
                                                  -BIG, ALU.min, ALU.max))
                wait(dve, VM, r, "bwd")
                done(tt(arg[:, :], ps_l[0:H, :], shb[:, :], ALU.subtract))

            rounds(dve, [(joint, LJ), (product_a, LP), (bends, LT), (product_b, LP), (second, LT), (shifts, LT)]
                   if L1 else
                   [(scaled(0), 1), (scaled(1), 3), (product_a, LP), (joint, LJ), (bends, LT), (product_b, LP),
                    (hidden(0), 1), (hidden(1), 3), (variance(0), 0), (variance(1), 2), (shifts, LT)], S)


def block_loads(big, cols, ws, wv):
    c = cols
    return [(big[0:64, 0, c:c + 64], ws), (big[64:96, 0, c + 64:c + 96], wv),
            (big[96:128, 0, c + 96:c + 128], wv), (big[0:32, 1, c + 128:c + 160], wv)]


def col_loads(col, j, s, v):
    s, v = s.rearrange("(p a) -> p a", a=1), v.rearrange("(p a) -> p a", a=1)
    return [(col[0:64, 0, j:j + 1], s), (col[64:96, 0, j:j + 1], v), (col[96:128, 0, j:j + 1], v),
            (col[0:32, 1, j:j + 1], v)]


def node_phase(nc, e, d, layer):
    prev = layer - 1
    tag = f"node{layer}_"
    join, opens = prev >= 0, layer < LAYERS
    H = {1: 4, 3: 8}.get(prev, 0)
    per_s, per_v = {1: (16, 8), 3: (8, 4)}.get(prev, (1, 1))
    DW = 384 if prev == 0 else W + 2 * H
    inner = layer in (1, 3)
    TW = 384 if layer == 2 else W
    OW = 0 if not opens else TW + W
    ffn = prev == 3
    parts = [(i, min(HW, DW - HW * i)) for i in range(-(-DW // HW))]
    nfetch = len(parts) + 1
    with ExitStack() as loc:
        def tmp(name, shape, dt=F32):
            return loc.enter_context(nc.sbuf_tensor(tag + name, shape, dt))

        sems = []

        def sem(name):
            sems.append(loc.enter_context(nc.semaphore(tag + name)))
            return sems[-1]

        def ps(name, shape):
            return loc.enter_context(nc.psum_tensor(tag + name, shape, F32))

        loadw, zeroed, prepped, biased = (sem("weights_loaded"), sem("weights_zeroed"), sem("weights_ready"),
                                                 sem("bias_rows"))
        wload, wprep, wbias = [], [], []
        nz = 0
        if join:
            idx = tmp("idx", [P, 2, 2], I32)
            r_last = tmp("r_last", [P, 2, DW])
            r_carry = tmp("r_carry", [P, 2, DW])
            tot = tmp("tot", [P, DW])
            joined = tmp("joined", [P, W])
            tot_t = tmp("tot_t", [P, 512])
            ps_t = ps("ps_t", [P, 512])
            ps_j = ps("ps_j", [P, 512])
            fj = tmp("fj", [P, 8])
            den = tmp("den", [P, 8])
            if prev == 0:
                wj = tmp("w_join", [96, 96])
            else:
                wj = tmp("w_join", [P, 2, W])
            if ffn:
                hrow = tmp("hrow", [P, 2, W])
                xp = tmp("xp", [P, 2, W])
                st2 = tmp("st2", [P, 6])
                mv2 = tmp("mv2", [P, 2])
                ve2 = tmp("ve2", [P, 2])
                rs2 = tmp("rs2", [P, 2])
                sq2 = tmp("sq2", [P, 96])
                n2 = tmp("n2", [P, W])
                n2_t = tmp("n2_t", [P, 256])
                wf1 = tmp("w_f1", [P, 2, 384])
                bf1 = tmp("b_f1", [1, 384])
                bfj = tmp("b_j", [1, W])
                bf2 = tmp("b_f2", [1, W])
                wf2s = tmp("w_f2s", [P, 64])
                wf2v = tmp("w_f2v", [P, 2, 64])
                gcol2 = tmp("gcol2", [P, 2, 2])
                f1 = tmp("f1", [P, 2, 384])
                th = tmp("th", [P, 2, 192])
                ps_t2 = ps("ps_t2", [P, 512])
                ps_t3 = ps("ps_t3", [P, 512])
                f1_t = tmp("f1_t", [P, 3, P])
                ps_f = ps("ps_f", [P, 512])
                ps_g = ps("ps_g", [P, 512])
                oo = tmp("oo", [P, 2, W])
        if opens:
            st = tmp("st", [P, 6])
            mv = tmp("mv", [P, 2])
            ve = tmp("ve", [P, 1])
            rs = tmp("rs", [P, 1])
            h = tmp("h", [P, 2, W])
            h_t = tmp("h_t", [P, 2, 2 * P])
            tab = tmp("tab", [P, 2, OW])
            wo = tmp("w_open", [P, 2, OW])
            ps_h = ps("ps_h", [P, 512])
            ps_o = ps("ps_o", [P, 2, 512])
            if inner:
                sti = tmp("sti", [P, 6])
                mvi = tmp("mvi", [P, 2])
                vei = tmp("vei", [P, 2])
                rsi = tmp("rsi", [P, 2])
                sqi = tmp("sqi", [P, 96])
                hn = tmp("hn", [P, W])
                gcol = tmp("gcol", [P, 2, 2])
                brow = tmp("brow", [1, 2 * W])
        if join:
            JA = Steps(sem("vec_factors"), ["d", "dm"])
            J = Steps(sem("vec_sums"), ["cs", "cv", "cd", "tot", "den", "rden", "ns", "nv"] if H else ["tot"])
            X = Steps(sem("vec_join"), {0: ["y", "x"]}.get(prev, ["x"]) if not ffn else
                      ["xp", "x", "st", "mv", "ve", "sq"])
            PT, PJ = Steps(sem("pe_tot_turned"), ["t"]), Steps(sem("pe_joined"), ["j"])
            AF, AT = Steps(sem("act_factors"), ["exp"]), Steps(sem("act_tot_turned"), ["t1", "t2"][0:1 if prev == 0 else 2])
            KJ = Steps(sem("pool_join"), ["idx", "idx2"])
            if ffn:
                F = [Steps(sem(f"vec_ffn{i}"), names) for i, names in
                     enumerate((["s", "v"], ["f1"], ["th", "sc", "fv"], ["o1", "oo"]))]
                PF = [Steps(sem(f"pe_ffn{i}"), ["m"]) for i in range(4)]
                AF_ = [Steps(sem(f"act_ffn{i}"), names) for i, names in enumerate((["t1", "t2"], ["tanh"], ["t1", "t2"]))]
                KF = Steps(sem("pool_ffn"), ["rs"])
            joined_in = [e.pool_dma_sem(tag + f"joined_in{b}") for b in range(2)]
            h_in = [sem(f"h_in{b}") for b in range(2)]
            oo_sent = [sem(f"oo_sent{b}") for b in range(2)]
        if opens:
            OA = Steps(sem("vec_open_a"), ["st", "mv", "ve"])
            OB = Steps(sem("vec_open_b"), ["c", "h"] + (["sti", "mvi", "vei", "sq"] if inner else []))
            OC = Steps(sem("vec_open_c"), ["ns", "nv"] + (["xh"] if layer == 1 else []))
            OT = Steps(sem("vec_tables"), ["tab"] + (["si", "x"] if layer == 0 else ["x"] if layer == 2 else []))
            PH, PO = Steps(sem("pe_h_turned"), ["t"]), Steps(sem("pe_tables"), ["o"])
            AO = Steps(sem("act_h_turned"), ["t1", "t2"])
            KO, KI = Steps(sem("pool_open"), ["rs"]), Steps(sem("pool_inner"), ["rsi"])
            tab_sent = [sem(f"tab_sent{b}") for b in range(2)]
            h_sent = [sem(f"h_sent{b}") for b in range(2)]
            ntab = {0: 1, 1: 2, 2: 1, 3: 2}[layer]

        lag_f = 1
        lag_s = lag_f + 1 if H else 1
        lag_x = lag_s + 1 if join else 0
        lag_h = lag_x + 1
        lag_t = lag_h + 1 if inner else lag_h

        zero = []
        c3 = lambda ap: ap.rearrange("(a b) -> a b", a=1)
        if join and prev == 0:
            wload += [(wj[0:64, 0:64], d["L0_gnn_W_l2_00"]), (wj[64:96, 0:64], d["L0_gnn_W_l2_10"]),
                      (wj[0:64, 64:96], d["L0_gnn_W_l2_01"]), (wj[64:96, 64:96], d["L0_gnn_W_l2_11"])]
            k0 = 0.25 * 0.5 / float(np.sqrt(96.0))
            wprep += [(wj[:, :], k0), (wj[64:96, 0:64], 1.0 / float(np.sqrt(3.0)))]
        elif join:
            zero += [wj[:, :, :]]
            if prev == 1:
                wload += block_loads(wj, 0, d["L1_gnn_Wps"], d["L1_gnn_Wpv"])
            elif prev == 2:
                wload += block_loads(wj, 0, d["L2_gnn_L_s"], d["L2_gnn_L_v"])
                wprep += [(wj[:, :, 0:64], 0.125), (wj[:, :, 64:160], 1.0 / float(np.sqrt(32.0)))]
            else:
                wload += block_loads(wj, 0, d["L3_gnn_proj_ws"], d["L3_gnn_proj_wv"])
                zero += [wf1[:, :, :], bf1[:, :], bfj[:, :], bf2[:, :], wf2v[:, :, :]]
                f1v, f2v = d["L3_gnn_f1_wv"], d["L3_gnn_f2_wv"]
                wload += [(wf1[0:64, 0, 0:192], d["L3_gnn_f1_ws"]), (wf1[64:96, 0, 192:256], f1v),
                          (wf1[96:128, 0, 256:320], f1v), (wf1[0:32, 1, 320:384], f1v),
                          (bf1[:, 0:192], c3(d["L3_gnn_f1_bs"])), (bfj[:, 0:64], c3(d["L3_gnn_proj_bs"])),
                          (bf2[:, 0:64], c3(d["L3_gnn_f2_bs"])), (wf2s[:, :], d["L3_gnn_f2_ws"]),
                          (wf2v[0:64, 0, 0:32], f2v), (wf2v[64:128, 0, 32:64], f2v), (wf2v[0:64, 1, 0:32], f2v)]
                wload += col_loads(gcol2, 0, d["L3_gnn_ln2_w0"], d["L3_gnn_ln2_w1"])
                zero += [gcol2[:, :, :]]
                wload += [(gcol2[0:64, 0, 1:2], d["L3_gnn_ln2_b0"].rearrange("(p a) -> p a", a=1))]
                wbias += [(gcol2, wf1, bf1, 384)]
        if opens:
            zero += [wo[:, :, :]]
            if layer == 0:
                wload += block_loads(wo, 0, d["L0_gnn_W_l1_0"], d["L0_gnn_W_l1_1"])
                wload += block_loads(wo, W, d["L0_gnn_W_si0"], d["L0_gnn_W_si1"])
                for c in (0, W):
                    wprep += [(wo[:, :, c:c + 64], 0.125), (wo[:, :, c + 64:c + 160], 1.0 / float(np.sqrt(32.0)))]
            elif layer == 1:
                wload += block_loads(wo, 0, d["L1_gnn_Ws_src"], d["L1_gnn_Wv_src"])
                wload += block_loads(wo, W, d["L1_gnn_Ws_dst"], d["L1_gnn_Wv_dst"])
                wload += col_loads(gcol, 0, d["L1_gnn_gamma_s"], d["L1_gnn_gamma_v"])
                wload += [(gcol[0:64, 0, 1:2], d["L1_gnn_beta_s"].rearrange("(p a) -> p a", a=1))]
            elif layer == 2:
                vv, sv, vs = d["L2_gnn_W_vv"], d["L2_gnn_W_sv"], d["L2_gnn_W_vs"]
                rows = [(0, 64, 96), (0, 96, 128), (1, 0, 32)]
                wload += [(wo[0:64, 0, 0:64], d["L2_gnn_W_ss"]), (wo[0:64, 0, 256:288], sv)]
                for i, (k, a, b) in enumerate(rows):
                    wload += [(wo[a:b, k, 64 + 64 * i:128 + 64 * i], vv),
                              (wo[a:b, k, 288 + 32 * i:320 + 32 * i], vs)]
                wload += block_loads(wo, 384, d["L2_gnn_L_s"], d["L2_gnn_L_v"])
                i2, i3 = 1.0 / float(np.sqrt(2.0)), 1.0 / float(np.sqrt(3.0))
                r32 = 1.0 / float(np.sqrt(32.0))
                wprep += [(wo[:, :, 0:64], 0.125 * i2), (wo[:, :, 64:256], i3 * r32 * i2),
                          (wo[:, :, 256:288], i3 * 0.125 * i2), (wo[:, :, 288:384], i3 * r32 * i2),
                          (wo[:, :, 384:448], 0.125), (wo[:, :, 448:544], r32)]
            else:
                wload += block_loads(wo, 0, d["L3_gnn_msrc_ws"], d["L3_gnn_msrc_wv"])
                wload += block_loads(wo, W, d["L3_gnn_mdst_ws"], d["L3_gnn_mdst_wv"])
                wload += col_loads(gcol, 0, d["L3_gnn_ln1_w0"], d["L3_gnn_ln1_w1"])
                wload += [(gcol[0:64, 0, 1:2], d["L3_gnn_ln1_b0"].rearrange("(p a) -> p a", a=1)),
                          (brow[:, W:W + 64], c3(d["L3_gnn_mdst_bs"]))]
            if inner:
                zero += [gcol[:, :, :], brow[:, :]]
                wbias += [(gcol, wo, brow, 2 * W)]
        nprep = len(wprep) + 3 * len(wbias)
        loc.callback(clear, nc, sems)
        block = loc.enter_context(nc.Block())

        @block.sync
        def _(sp):
            sp.wait_ge(zeroed, len(zero)) if zero else None
            load_blocks(sp, loadw, wload)

            def fetch_h(r, b, n):
                if not early(r):
                    wait(sp, X, r - 2, "xp")
                sp.dma_start(hrow[:, b], e.h3[bass.ds(r * P, P), :]).then_inc(h_in[b], 16)

            def store_out(r, b, n):
                wait(sp, F[3], r, "oo")
                sp.dma_start(d["out"][bass.ds(r * P, P), :], oo[:, b]).then_inc(oo_sent[b], 16)

            def store_h(r, b, n):
                wait(sp, OB, r, "h")
                sp.dma_start(e.h3[bass.ds(r * P, P), :], h[:, b]).then_inc(h_sent[b], 16)

            def store_tab(r, b, n):
                wait(sp, OT, r, "tab")
                sp.dma_start(e.tsrc[layer][bass.ds(r * P, P), :], tab[:, b, 0:TW]).then_inc(tab_sent[b], 16)
                if inner:
                    sp.dma_start(e.tdst[bass.ds(r * P, P), :], tab[:, b, W:2 * W]).then_inc(tab_sent[b], 16)

            if ffn:
                rounds(sp, [(fetch_h, lag_x - 1), (store_out, lag_x + 5)], NT)
                for b in range(2):
                    sp.wait_ge(oo_sent[b], 16 * (NT // 2))
            else:
                rounds(sp, ([(store_h, lag_h + 1)] if layer == 3 else []) + [(store_tab, lag_t + 2)], NT)
                for b in range(2):
                    sp.wait_ge(tab_sent[b], 16 * ntab * (NT // 2))
                    if layer == 3:
                        sp.wait_ge(h_sent[b], 16 * (NT // 2))

        @block.gpsimd
        def _(pool):
            for z in zero:
                pool.memset(z, 0.0).then_inc(zeroed, 1)

            def fetch(r, b, n):
                if not early(r):
                    wait(pool, J, r - 2, "tot")
                    pool.wait_ge(joined_in[b], 16 * nfetch * n)
                    pool.nop(nofuse=True)
                nc.gpsimd.tensor_copy(idx[:, b, 0:1], e.last[:, bass.ds(r, 1)]).then_inc(KJ.sem, 1)
                nc.gpsimd.tensor_copy(idx[:, b, 1:2], e.carry[:, bass.ds(r, 1)]).then_inc(KJ.sem, 1)
                wait(pool, KJ, r, "idx2")
                pool.nop(nofuse=True)
                for i, w in parts:
                    pool.indirect_dma_start(r_last[:, b, HW * i:HW * i + w], None, e.rows[prev][i],
                                            bass.IndirectOffsetOnAxis(ap=idx[:, b, 0:1], axis=0))\
                        .then_inc(joined_in[b], 16)
                pool.indirect_dma_start(r_carry[:, b, :], None, e.carries[prev],
                                        bass.IndirectOffsetOnAxis(ap=idx[:, b, 1:2], axis=0))\
                        .then_inc(joined_in[b], 16)

            def power(r, b, n):
                wait(pool, OA, r, "ve")
                nc.gpsimd.tensor_tensor(rs[:, :], ve[:, :], e.mhalf[:, 0:1], ALU.pow).then_inc(KO.sem, 1)

            def power_inner(r, b, n):
                wait(pool, OB, r, "sq")
                nc.gpsimd.tensor_tensor(rsi[:, :], vei[:, :], e.mhalf[:, 0:2], ALU.pow).then_inc(KI.sem, 1)

            def power_ffn(r, b, n):
                wait(pool, X, r, "sq")
                nc.gpsimd.tensor_tensor(rs2[:, :], ve2[:, :], e.mhalf[:, 0:2], ALU.pow).then_inc(KF.sem, 1)

            rounds(pool, ([(fetch, 0)] if join else []) + ([(power_inner, lag_h)] if inner else []) +
                   ([(power, lag_x)] if opens else []) + ([(power_ffn, lag_x)] if ffn else []), NT)

        @block.tensor
        def _(pe):
            for k, (g, w, row, n) in enumerate(wbias):
                pe.wait_ge(loadw, 16 * len(wload))
                if k == 0 and wprep:
                    pe.wait_ge(prepped, len(wprep))
                t = ps_f if ffn else ps_h
                nc.tensor.matmul(t[0:1, 0:n], g[:, 0, 1:2], w[:, 0, 0:n], start=True, stop=False)
                nc.tensor.matmul(t[0:1, 0:n], g[0:32, 1, 1:2], w[0:32, 1, 0:n], start=False, stop=True)\
                    .then_inc(biased, 1)
            pe.wait_ge(prepped, nprep)

            def turn_tot(r, b, n):
                wait(pe, J, r, J.names[-1])
                if not early(r, 1):
                    wait(pe, AT, r - 1, AT.names[-1])
                if prev == 0:
                    for k in range(4):
                        mm = nc.tensor.transpose(ps_t[0:96, k * P:(k + 1) * P], tot[:, 96 * k:96 * k + 96],
                                                 e.ident[:, :])
                else:
                    nc.tensor.transpose(ps_t[:, 0:P], tot[:, 0:P], e.ident[:, :])
                    mm = nc.tensor.transpose(ps_t[0:32, P:2 * P], tot[:, P:W], e.ident[:, :])
                mm.then_inc(PT.sem, 1)

            def join_maps(r, b, n):
                wait(pe, AT, r, AT.names[-1])
                if not early(r, 1):
                    wait(pe, X, r - 1, X.names[0])
                if prev == 0:
                    for k in range(4):
                        o = ps_j[:, 0:64] if k == 0 else ps_j[:, 32 + 32 * k:64 + 32 * k]
                        mm = nc.tensor.matmul(o, tot_t[0:96, k * P:(k + 1) * P],
                                              wj[:, 0:64] if k == 0 else wj[:, 64:96], start=True, stop=True)
                else:
                    nc.tensor.matmul(ps_j[:, 0:W], tot_t[:, 0:P], wj[:, 0, :], start=True, stop=False)
                    mm = nc.tensor.matmul(ps_j[:, 0:W], tot_t[0:32, P:2 * P], wj[0:32, 1, :], start=False,
                                          stop=not ffn)
                    if ffn:
                        mm = nc.tensor.matmul(ps_j[:, 0:W], e.ones[0:1, :], bfj[:, :], start=False, stop=True)
                mm.then_inc(PJ.sem, 1)

            def turn_n2(r, b, n):
                wait(pe, F[0], r, "v")
                if not early(r, 1):
                    wait(pe, AF_[0], r - 1, "t2")
                nc.tensor.transpose(ps_t2[:, 0:P], n2[:, 0:P], e.ident[:, :])
                nc.tensor.transpose(ps_t2[0:32, P:2 * P], n2[:, P:W], e.ident[:, :]).then_inc(PF[0].sem, 1)

            def ffn1(r, b, n):
                wait(pe, AF_[0], r, "t2")
                if not early(r, 1):
                    wait(pe, F[1], r - 1, "f1")
                nc.tensor.matmul(ps_f[:, 0:384], n2_t[:, 0:P], wf1[:, 0, :], start=True, stop=False)
                nc.tensor.matmul(ps_f[:, 0:384], n2_t[0:32, P:2 * P], wf1[0:32, 1, :], start=False, stop=False)
                nc.tensor.matmul(ps_f[:, 0:384], e.ones[0:1, :], bf1[:, :], start=False, stop=True)\
                    .then_inc(PF[1].sem, 1)

            def turn_f1(r, b, n):
                wait(pe, F[2], r, "fv")
                if not early(r, 1):
                    wait(pe, AF_[2], r - 1, "t2")
                nc.tensor.transpose(ps_t3[:, 0:P], f1[:, b, 0:P], e.ident[:, :])
                nc.tensor.transpose(ps_t3[:, P:2 * P], f1[:, b, 192:320], e.ident[:, :])
                nc.tensor.transpose(ps_t3[0:64, 2 * P:3 * P], f1[:, b, 320:384], e.ident[:, :]).then_inc(PF[2].sem, 1)

            def ffn2(r, b, n):
                wait(pe, AF_[2], r, "t2")
                if not early(r, 1):
                    wait(pe, F[3], r - 1, "o1")
                nc.tensor.matmul(ps_g[:, 0:64], f1_t[:, 0, :], wf2s[:, :], start=True, stop=False)
                nc.tensor.matmul(ps_g[:, 0:64], e.ones[0:1, :], bf2[:, 0:64], start=False, stop=True)
                nc.tensor.matmul(ps_g[:, 64:128], f1_t[:, 1, :], wf2v[:, 0, :], start=True, stop=True)
                nc.tensor.matmul(ps_g[:, 128:160], f1_t[0:64, 2, :], wf2v[0:64, 1, 0:32], start=True, stop=True)\
                    .then_inc(PF[3].sem, 1)

            def turn_h(r, b, n):
                wait(pe, *((OC, r, "nv") if inner else (OB, r, "h")))
                src = hn[:, :] if inner else h[:, b]
                if not early(r, 1):
                    wait(pe, AO, r - 1, "t2")
                nc.tensor.transpose(ps_h[:, 0:P], src[:, 0:P], e.ident[:, :])
                nc.tensor.transpose(ps_h[0:32, P:2 * P], src[:, P:W], e.ident[:, :]).then_inc(PH.sem, 1)

            def tables(r, b, n):
                wait(pe, AO, r, "t2")
                if not early(r, 1):
                    wait(pe, OT, r - 1, OT.names[-1])
                for o, c0, cw in ((0, 0, TW), (1, TW, W)):
                    nc.tensor.matmul(ps_o[:, o, 0:cw], h_t[:, b, 0:P], wo[:, 0, c0:c0 + cw], start=True, stop=False)
                    mm = nc.tensor.matmul(ps_o[:, o, 0:cw], h_t[0:32, b, P:2 * P], wo[0:32, 1, c0:c0 + cw],
                                          start=False, stop=not inner)
                    if inner:
                        mm = nc.tensor.matmul(ps_o[:, o, 0:cw], e.ones[0:1, :], brow[:, c0:c0 + cw],
                                              start=False, stop=True)
                mm.then_inc(PO.sem, 1)

            rounds(pe, ([(join_maps, lag_x)] if join else []) + ([(tables, lag_t + 1)] if opens else []) +
                   ([(ffn2, lag_x + 4), (ffn1, lag_x + 2)] if ffn else []) +
                   ([(turn_tot, lag_s)] if join else []) + ([(turn_h, lag_t)] if opens else []) +
                   ([(turn_f1, lag_x + 3), (turn_n2, lag_x + 1)] if ffn else []), NT)

        @block.scalar
        def _(act):
            def factors(r, b, n):
                wait(act, JA, r, "dm")
                nc.scalar.activation(fj[:, 0:H], fj[:, 0:H], ACT.Exp).then_inc(AF.sem, 1)

            def turned_tot(r, b, n):
                wait(act, PT, r, "t")
                if not early(r, 1):
                    wait(act, PJ, r - 1, "j")
                if prev == 0:
                    nc.scalar.copy(tot_t[0:96, :], ps_t[0:96, :]).then_inc(AT.sem, 1)
                else:
                    nc.scalar.copy(tot_t[:, 0:P], ps_t[:, 0:P]).then_inc(AT.sem, 1)
                    nc.scalar.copy(tot_t[0:32, P:2 * P], ps_t[0:32, P:2 * P]).then_inc(AT.sem, 1)

            def turned_n2(r, b, n):
                wait(act, PF[0], r, "m")
                if not early(r, 1):
                    wait(act, PF[1], r - 1, "m")
                nc.scalar.copy(n2_t[:, 0:P], ps_t2[:, 0:P]).then_inc(AF_[0].sem, 1)
                nc.scalar.copy(n2_t[0:32, P:2 * P], ps_t2[0:32, P:2 * P]).then_inc(AF_[0].sem, 1)

            def gates(r, b, n):
                wait(act, F[1], r, "f1")
                if not early(r):
                    wait(act, F[2], r - 2, "fv")
                nc.scalar.activation(th[:, b], f1[:, b, 0:192], ACT.Tanh, scale=0.5).then_inc(AF_[1].sem, 1)

            def turned_f1(r, b, n):
                wait(act, PF[2], r, "m")
                if not early(r, 1):
                    wait(act, PF[3], r - 1, "m")
                nc.scalar.copy(f1_t[:, 0:2, :], ps_t3[:, 0:2 * P].rearrange("p (a b) -> p a b", a=2))\
                    .then_inc(AF_[2].sem, 1)
                nc.scalar.copy(f1_t[0:64, 2, :], ps_t3[0:64, 2 * P:3 * P]).then_inc(AF_[2].sem, 1)

            def turned_h(r, b, n):
                wait(act, PH, r, "t")
                if not early(r):
                    wait(act, PO, r - 2, "o")
                nc.scalar.copy(h_t[:, b, 0:P], ps_h[:, 0:P]).then_inc(AO.sem, 1)
                nc.scalar.copy(h_t[0:32, b, P:2 * P], ps_h[0:32, P:2 * P]).then_inc(AO.sem, 1)

            rounds(act, ([(turned_tot, lag_s)] if join else []) + ([(factors, lag_f)] if join and H else []) +
                   ([(turned_h, lag_t)] if opens else []) +
                   ([(turned_f1, lag_x + 3), (turned_n2, lag_x + 1), (gates, lag_x + 2)] if ffn else []), NT)

        @block.vector
        def _(dve):
            tt, ts = nc.vector.tensor_tensor, nc.vector.tensor_scalar
            dve.wait_ge(loadw, 16 * len(wload))
            for k, (ap, c) in enumerate(wprep):
                dve.wait_ge(prepped, k) if k else None
                ts(ap, ap, c, None, ALU.mult).then_inc(prepped, 1)
            m = len(wprep)
            for k, (g, w, row, n) in enumerate(wbias):
                dve.wait_ge(biased, k + 1)
                t = ps_f if ffn else ps_h
                tt(row[0:1, 0:n], row[0:1, 0:n], t[0:1, 0:n], ALU.add).then_inc(prepped, 1)
                ts(w[:, 0, 0:n], w[:, 0, 0:n], g[:, 0, 0:1], None, ALU.mult).then_inc(prepped, 1)
                ts(w[0:32, 1, 0:n], w[0:32, 1, 0:n], g[0:32, 1, 0:1], None, ALU.mult).then_inc(prepped, 1)
                m += 3

            def xs(r):
                return e.x[:, bass.ds(r, 1), :].rearrange("p a w -> p (a w)")

            def attr(r, n):
                return e.attr[:, bass.ds(r, 1)].to_broadcast([P, n])

            def heads(ap, f):
                return ((ap[:, 0:C0].rearrange("p (h k) -> p h k", h=H),
                         f[:, 0:H].unsqueeze(2).to_broadcast([P, H, per_s])),
                        (ap[:, C0:W].rearrange("p (c h k) -> p c h k", c=3, h=H),
                         f[:, 0:H].unsqueeze(1).unsqueeze(3).to_broadcast([P, 3, H, per_v])))

            def counted(steps):
                def done(ins):
                    ins.then_inc(steps.sem, 1)
                return done

            def factors(r, b, n):
                done = counted(JA)
                dve.wait_ge(joined_in[b], 16 * nfetch * (n + 1))
                if not early(r, 1):
                    wait(dve, J, r - 1, "cd")
                done(tt(fj[:, 0:H], r_carry[:, b, W + H:W + 2 * H], r_last[:, b, W + H:W + 2 * H], ALU.subtract))
                wait(dve, JA, r, "d")
                done(ts(fj[:, 0:H], fj[:, 0:H], 0.0, None, ALU.min))

            def totals(r, b, n):
                done = counted(J)
                D, C = r_last[:, b], r_carry[:, b]
                if not early(r, 1):
                    wait(dve, PT, r - 1, "t")
                if H:
                    wait(dve, AF, r, "exp")
                    for v, f in heads(C, fj):
                        done(tt(v, v, f, ALU.mult))
                    done(tt(C[:, W:W + H], C[:, W:W + H], fj[:, 0:H], ALU.mult))
                    wait(dve, J, r, "cd")
                    done(tt(tot[:, 0:W + H], D[:, 0:W + H], C[:, 0:W + H], ALU.add))
                    wait(dve, J, r, "tot")
                    done(ts(den[:, 0:H], tot[:, W:W + H], 1e-16 if prev == 1 else 1e-12, None, ALU.add))
                    wait(dve, J, r, "den")
                    done(nc.vector.reciprocal(den[:, 0:H], den[:, 0:H]))
                    wait(dve, J, r, "rden")
                    for v, f in heads(tot, den):
                        done(tt(v, v, f, ALU.mult))
                else:
                    dve.wait_ge(joined_in[b], 16 * nfetch * (n + 1))
                    done(tt(tot[:, :], D, C, ALU.add))

            def join_x(r, b, n):
                done = counted(X)
                wait(dve, PJ, r, "j")
                if not early(r, 1):
                    wait(dve, X, r - 1, X.names[-1])
                if prev == 0:
                    done(tt(joined[:, :], ps_j[:, 0:W], attr(r, W), ALU.mult))
                    wait(dve, X, r, "y")
                    done(tt(xs(r), xs(r), joined[:, :], ALU.add))
                elif not ffn:
                    done(tt(xs(r), xs(r), ps_j[:, 0:W], ALU.add))
                else:
                    dve.wait_ge(h_in[b], 16 * (n + 1))
                    if not early(r):
                        wait(dve, F[0], r - 2, "v")
                    if not early(r, 1):
                        wait(dve, F[0], r - 1, "v")
                    done(tt(xp[:, b], hrow[:, b], ps_j[:, 0:W], ALU.add))
                    wait(dve, X, r, "xp")
                    done(tt(xs(r), xs(r), xp[:, b], ALU.add))
                    dve.nop(nofuse=True)
                    done(nc.vector.bn_stats(st2[:, :], xp[:, b, 0:C0]))
                    wait(dve, X, r, "st")
                    dve.nop(nofuse=True)
                    done(nc.vector.bn_aggr(mv2[:, :], st2[:, :]))
                    wait(dve, X, r, "mv")
                    done(ts(ve2[:, 0:1], mv2[:, 1:2], EPS, None, ALU.add))
                    done(nc.vector.tensor_tensor_reduce(out=sq2[:, :], in0=xp[:, b, C0:W], in1=xp[:, b, C0:W],
                                                        scale=1.0 / 96, scalar=EPS, op0=ALU.mult, op1=ALU.add,
                                                        accum_out=ve2[:, 1:2]))

            def ffn_norm(r, b, n):
                done = counted(F[0])
                wait(dve, KF, r, "rs")
                if not early(r, 1):
                    wait(dve, PF[0], r - 1, "m")
                done(ts(n2[:, 0:C0], xp[:, b, 0:C0], mv2[:, 0:1], rs2[:, 0:1], ALU.subtract, ALU.mult))
                done(ts(n2[:, C0:W], xp[:, b, C0:W], rs2[:, 1:2], None, ALU.mult))

            def ffn_f1(r, b, n):
                done = counted(F[1])
                wait(dve, PF[1], r, "m")
                if not early(r):
                    wait(dve, PF[2], r - 2, "m")
                done(tt(f1[:, b], ps_f[:, 0:384], attr(r, 384), ALU.mult))

            def ffn_gate(r, b, n):
                done = counted(F[2])
                wait(dve, AF_[1], r, "tanh")
                done(ts(th[:, b], th[:, b], 0.5, 0.5, ALU.mult, ALU.add))
                wait(dve, F[2], r, "th")
                done(tt(f1[:, b, 0:128], f1[:, b, 0:128], th[:, b, 0:128], ALU.mult))
                fv = f1[:, b, 192:384].rearrange("p (c k) -> p c k", c=3)
                done(tt(fv, fv, th[:, b, 128:192].unsqueeze(1).to_broadcast([P, 3, 64]), ALU.mult))

            def ffn_out(r, b, n):
                done = counted(F[3])
                wait(dve, PF[3], r, "m")
                if not early(r):
                    dve.wait_ge(oo_sent[b], 16 * n)
                done(tt(oo[:, b], ps_g[:, 0:W], attr(r, W), ALU.mult))
                wait(dve, F[3], r, "o1")
                done(tt(oo[:, b], oo[:, b], xs(r), ALU.add))

            def stats(r, b, n):
                done = counted(OA)
                if join:
                    wait(dve, X, r, "x")
                if not early(r, 1):
                    wait(dve, OB, r - 1, "h")
                dve.nop(nofuse=True)
                done(nc.vector.bn_stats(st[:, :], xs(r)))
                wait(dve, OA, r, "st")
                dve.nop(nofuse=True)
                done(nc.vector.bn_aggr(mv[:, :], st[:, :]))
                wait(dve, OA, r, "mv")
                done(ts(ve[:, :], mv[:, 1:2], EPS, None, ALU.add))

            def hidden(r, b, n):
                done = counted(OB)
                wait(dve, KO, r, "rs")
                if not early(r):
                    wait(dve, PH, r - 2, "t")
                    if layer == 3:
                        dve.wait_ge(h_sent[b], 16 * n)
                if inner and not early(r, 1):
                    wait(dve, OC, r - 1, OC.names[-1])
                done(ts(h[:, b], xs(r), mv[:, 0:1], rs[:, 0:1], ALU.subtract, ALU.mult))
                wait(dve, OB, r, "c")
                done(ts(h[:, b], h[:, b], 0.0, None, ALU.max))
                if inner:
                    wait(dve, OB, r, "h")
                    done(nc.vector.bn_stats(sti[:, :], h[:, b, 0:C0]))
                    wait(dve, OB, r, "sti")
                    dve.nop(nofuse=True)
                    done(nc.vector.bn_aggr(mvi[:, :], sti[:, :]))
                    wait(dve, OB, r, "mvi")
                    done(ts(vei[:, 0:1], mvi[:, 1:2], EPS, None, ALU.add))
                    done(nc.vector.tensor_tensor_reduce(out=sqi[:, :], in0=h[:, b, C0:W], in1=h[:, b, C0:W],
                                                        scale=1.0 / (32 if layer == 1 else 96), scalar=EPS,
                                                        op0=ALU.mult, op1=ALU.add, accum_out=vei[:, 1:2]))

            def inner_norm(r, b, n):
                done = counted(OC)
                wait(dve, KI, r, "rsi")
                if not early(r, 1):
                    wait(dve, PH, r - 1, "t")
                done(ts(hn[:, 0:C0], h[:, b, 0:C0], mvi[:, 0:1], rsi[:, 0:1], ALU.subtract, ALU.mult))
                done(ts(hn[:, C0:W], h[:, b, C0:W], rsi[:, 1:2], None, ALU.mult))
                if layer == 1:
                    done(tt(xs(r), xs(r), h[:, b], ALU.add))

            def store_tables(r, b, n):
                done = counted(OT)
                wait(dve, PO, r, "o")
                if not early(r):
                    dve.wait_ge(tab_sent[b], 16 * ntab * n)
                if layer == 0:
                    done(tt(tab[:, b, 0:W], ps_o[:, 0, 0:W], attr(r, W), ALU.mult))
                    done(tt(tab[:, b, W:2 * W], ps_o[:, 1, 0:W], attr(r, W), ALU.mult))
                    wait(dve, OT, r, "si")
                    done(tt(xs(r), xs(r), tab[:, b, W:2 * W], ALU.add))
                elif layer == 2:
                    done(nc.vector.tensor_copy(tab[:, b, 0:TW], ps_o[:, 0, 0:TW]))
                    done(tt(xs(r), xs(r), ps_o[:, 1, 0:W], ALU.add))
                else:
                    done(nc.vector.tensor_copy(tab[:, b, 0:2 * W].rearrange("p (a w) -> p a w", a=2),
                                               ps_o[:, :, 0:W]))

            rounds(dve, ([(totals, lag_s)] if join else []) + ([(factors, lag_f)] if join and H else []) +
                   ([(ffn_norm, lag_x + 1), (join_x, lag_x), (ffn_gate, lag_x + 3), (ffn_f1, lag_x + 2),
                     (ffn_out, lag_x + 4)] if ffn else
                    ([(inner_norm, lag_t)] if inner else []) + [(hidden, lag_h)] +
                    ([(join_x, lag_x)] if join else []) + [(stats, lag_x), (store_tables, lag_t + 1)]), NT)


def build(nc, d):
    with ExitStack() as ctx:
        ctx.enter_context(nc.allow_non_contiguous_dma(reason="columns of a few words, read once"))
        e = setup(nc, ctx, d)
        for layer in range(LAYERS + 1):
            node_phase(nc, e, d, layer)
            if layer == LAYERS:
                break
            if layer in (0, 2):
                edge_conv(nc, e, d, layer)
                carry_phase(nc, e, layer, 384 if layer == 0 else W)
            else:
                edge_attention(nc, e, d, layer)
                H = 4 if layer == 1 else 8
                carry_phase(nc, e, layer, W + 2 * H, H, C0 // H, C1 // H)


def kernel(**inputs):
    import concourse.bacc as _bacc
    from concourse.bass_utils import run_bass_kernel_spmd as _run

    a = {k: np.asarray(v) for k, v in inputs.items()}

    def pad(v, rows, fill=0):
        out = np.full((rows,) + v.shape[1:], fill, v.dtype)
        out[:len(v)] = v
        return out

    def cols(v):
        return np.ascontiguousarray(np.swapaxes(v.reshape(T, P, *v.shape[1:]), 0, 1))

    def comp_major(v):
        tail = v[..., C0:].reshape(*v.shape[:-1], C1, 3)
        return np.concatenate([v[..., :C0], np.swapaxes(tail, -1, -2).reshape(*v.shape[:-1], 3 * C1)], -1)

    def with_ones(v):
        return np.concatenate([v, np.ones((1,) + v.shape[1:], v.dtype)], 0)

    dst = pad(a["dst"], EP, N)
    arrays = {
        "x": np.ascontiguousarray(np.swapaxes(pad(comp_major(a["x"]), NP).reshape(NT, P, W), 0, 1)),
        "attr": np.ascontiguousarray(pad(a["node_vec1"][:, 0], NP).reshape(NT, P).T),
        "src_cols": cols(pad(a["src"], EP)),
        "dst_cols": cols(dst),
        "dst_rows": dst.reshape(1, EP),
        "dst_run": np.concatenate([np.array([-1], dst.dtype), dst, np.full(EP // P, -1, dst.dtype)]),
        "ea4_cols": cols(pad(a["edge_attr_4"], EP)),
        "ea3_cols": cols(pad(a["edge_attr_3"], EP, 1)),
        "ea10_rows": np.ascontiguousarray(pad(a["edge_attr_10"], EP).T),
        "ea16_rows": with_ones(pad(a["edge_attr_16"], EP).T),
        "ea64_rows": with_ones(pad(a["edge_attr_64"], EP).T),
    }
    arrays["L2_rad"] = comp_major(np.concatenate([a["L2_gnn_W_rad"].T, a["L2_gnn_b_rad"][None]]))
    for k, v in a.items():
        if "_gnn_" in k:
            arrays[k] = v
    arrays = {k: np.ascontiguousarray(v) for k, v in arrays.items()}
    nc = _bacc.Bacc("TRN2", target_bir_lowering=False, num_devices=1)
    d = {k: nc.dram_tensor(f"in_{k}", v.shape, mybir.dt.from_np(v.dtype), kind="ExternalInput").ap()
         for k, v in arrays.items()}
    d["out"] = nc.dram_tensor("out_nodes", (NP, W), F32, kind="ExternalOutput").ap()
    build(nc, d)
    r = _run(nc, [{f"in_{k}": v for k, v in arrays.items()}], core_ids=[0])
    got = np.asarray(r.results[0]["out_nodes"])[:N]
    tail = np.swapaxes(got[:, C0:].reshape(N, 3, C1), 1, 2).reshape(N, 3 * C1)
    return np.concatenate([got[:, :C0], tail], 1)
```
